# Optimizing a Trainium2 kernel written in Bass

```python
import numpy as np
import jax
import jax.numpy as jnp

def _softmax(x, axis=-1):
    return jax.nn.softmax(x, axis=axis)

def _gelu(x):
    return jax.nn.gelu(x, approximate=True)

def _silu(x):
    return jax.nn.silu(x)

def _sigmoid(x):
    return jax.nn.sigmoid(x)

def _layernorm(x, axis=-1, eps=1e-05):
    m = jnp.mean(x, axis=axis, keepdims=True)
    v = jnp.var(x, axis=axis, keepdims=True)
    return (x - m) / jnp.sqrt(v + eps)

def _scatter_add(tgt, idx, src, axis=0):
    return tgt.at[idx].add(src)

def _segment_sum(src, seg, n):
    return jax.ops.segment_sum(src, seg, n)
kernel_name = 'mk_vit_tower_cls_d1_tok_img1024_r4_cc322e'

def setup_inputs(seed: int=0):
    np.random.seed(seed)
    _w = jnp.asarray

    def _rec_inputs():
        import jax
        import jax.numpy as jnp
        _rk = jax.random.key(seed)
        x = -0.000392918 + 0.999932 * jax.random.normal(jax.random.fold_in(_rk, 1), (8, 256, 256, 1), jnp.float32)
        cls_tok = 0.02 * jax.random.normal(jax.random.fold_in(_rk, 5), (1, 1, 256), jnp.float32)
        return (x, cls_tok)
    x, cls_tok = _rec_inputs()

    def _L0_tok_setup():
        import jax, jax.numpy as jnp
        import numpy as np
        INV_SQRT2 = 0.7071067811865476
        LEVEL = 3

        def _split(x, axis):
            ax = axis % x.ndim
            sl0 = [slice(None)] * x.ndim
            sl0[ax] = slice(0, None, 2)
            sl1 = [slice(None)] * x.ndim
            sl1[ax] = slice(1, None, 2)
            x0, x1 = (x[tuple(sl0)], x[tuple(sl1)])
            return ((x0 + x1) * INV_SQRT2, (x0 - x1) * INV_SQRT2)

        def _merge(lo, hi, axis):
            ax = axis % lo.ndim
            e = (lo + hi) * INV_SQRT2
            o = (lo - hi) * INV_SQRT2
            s = jnp.stack([e, o], axis=ax + 1)
            shape = list(lo.shape)
            shape[ax] *= 2
            return s.reshape(shape)

        def _dwt2(x):
            lo, hi = _split(x, -1)
            a, h = _split(lo, -2)
            v, d = _split(hi, -2)
            return (a, h, v, d)

        def _idwt2(a, h, v, d):
            lo = _merge(a, h, -2)
            hi = _merge(v, d, -2)
            return _merge(lo, hi, -1)
        key = jax.random.key(seed)
        ks = jax.random.split(key, 8)
        B, H, W = (16, 256, 256)
        x = jax.random.normal(ks[0], (B, H, W, 1), dtype=jnp.float32)
        na = H // 8 * (W // 8)
        n2 = H // 4 * (W // 4)
        n1 = H // 2 * (W // 2)
        scale = 0.02
        Wa = jax.random.normal(ks[1], (na, 1), dtype=jnp.float32) * scale
        ba = jnp.zeros((1,), jnp.float32)
        Wd1 = jax.random.normal(ks[2], (3 * na, 3), dtype=jnp.float32) * scale
        bd1 = jnp.zeros((3,), jnp.float32)
        Wd2 = jax.random.normal(ks[3], (3 * n2, 3), dtype=jnp.float32) * scale
        bd2 = jnp.zeros((3,), jnp.float32)
        Wd3 = jax.random.normal(ks[4], (3 * n1, 3), dtype=jnp.float32) * scale
        bd3 = jnp.zeros((3,), jnp.float32)
        return {'x': x, 'Wa': Wa, 'ba': ba, 'Wd1': Wd1, 'bd1': bd1, 'Wd2': Wd2, 'bd2': bd2, 'Wd3': Wd3, 'bd3': bd3}
    _L0_tok_all = _L0_tok_setup()
    _L0_tok_in = {k: v for k, v in _L0_tok_all.items() if k in ('Wa', 'ba', 'Wd1', 'bd1', 'Wd2', 'bd2', 'Wd3', 'bd3')}
    del _L0_tok_all

    def _L0_attn_setup():
        import jax, jax.numpy as jnp
        import numpy as np
        B, N, D = (4, 1024, 256)
        H, F = (16, 64)
        HD = D // H
        EPS_ATTN = 1e-08
        EPS_LN = 1e-05

        def _layernorm(x, gamma, beta):
            mu = jnp.mean(x, axis=-1, keepdims=True)
            var = jnp.var(x, axis=-1, keepdims=True)
            return (x - mu) * jax.lax.rsqrt(var + EPS_LN) * gamma + beta
        key = jax.random.key(seed)
        ks = jax.random.split(key, 10)

        def kaiming(k, shape):
            fan_in = shape[1]
            return jax.random.normal(k, shape, jnp.float32) * jnp.sqrt(2.0 / fan_in)
        pm = jax.random.normal(ks[0], (H, HD, F), jnp.float32)
        return {'x': jax.random.normal(ks[1], (B, N, D), jnp.float32), 'proj': pm, 'w_qkv': kaiming(ks[2], (3 * D, D)), 'w_out': kaiming(ks[3], (D, D)), 'b_out': jnp.zeros((D,), jnp.float32), 'gamma': jnp.ones((D,), jnp.float32), 'beta': jnp.zeros((D,), jnp.float32), 'w1': kaiming(ks[4], (4 * D, D)), 'b1': jnp.zeros((4 * D,), jnp.float32), 'w2': kaiming(ks[5], (D, 4 * D)), 'b2': jnp.zeros((D,), jnp.float32)}
    _L0_attn_all = _L0_attn_setup()
    _L0_attn_in = {k: v for k, v in _L0_attn_all.items() if k in ('proj', 'w_qkv', 'w_out', 'b_out', 'gamma', 'beta', 'w1', 'b1', 'w2', 'b2')}
    del _L0_attn_all

    def _L0_ffn_setup():
        import jax, jax.numpy as jnp
        import numpy as np
        EMB, HID, E, TOPK = (256, 1024, 8, 2)
        key = jax.random.key(seed)
        ks = jax.random.split(key, 10)
        s = 0.02
        return {'x': jax.random.normal(ks[0], (4, 512, EMB), jnp.float32), 'rw1': s * jax.random.normal(ks[1], (EMB, HID), jnp.float32), 'rb1': jnp.zeros((HID,), jnp.float32), 'rw2': s * jax.random.normal(ks[2], (HID, E), jnp.float32), 'rb2': jnp.zeros((E,), jnp.float32), 'w1': s * jax.random.normal(ks[3], (E, EMB, HID), jnp.float32), 'b1': jnp.zeros((E, HID), jnp.float32), 'w2': s * jax.random.normal(ks[4], (E, HID, EMB), jnp.float32), 'b2': jnp.zeros((E, EMB), jnp.float32)}
    _L0_ffn_all = _L0_ffn_setup()
    _L0_ffn_in = {k: v for k, v in _L0_ffn_all.items() if k in ('rw1', 'rb1', 'rw2', 'rb2', 'w1', 'b1', 'w2', 'b2')}
    del _L0_ffn_all
    return {'x': x, 'cls_tok': cls_tok, 'L0_tok_Wa': _L0_tok_in['Wa'], 'L0_tok_ba': _L0_tok_in['ba'], 'L0_tok_Wd1': _L0_tok_in['Wd1'], 'L0_tok_bd1': _L0_tok_in['bd1'], 'L0_tok_Wd2': _L0_tok_in['Wd2'], 'L0_tok_bd2': _L0_tok_in['bd2'], 'L0_tok_Wd3': _L0_tok_in['Wd3'], 'L0_tok_bd3': _L0_tok_in['bd3'], 'L0_attn_proj': _L0_attn_in['proj'], 'L0_attn_w_qkv': _L0_attn_in['w_qkv'], 'L0_attn_w_out': _L0_attn_in['w_out'], 'L0_attn_b_out': _L0_attn_in['b_out'], 'L0_attn_gamma': _L0_attn_in['gamma'], 'L0_attn_beta': _L0_attn_in['beta'], 'L0_attn_w1': _L0_attn_in['w1'], 'L0_attn_b1': _L0_attn_in['b1'], 'L0_attn_w2': _L0_attn_in['w2'], 'L0_attn_b2': _L0_attn_in['b2'], 'L0_ffn_rw1': _L0_ffn_in['rw1'], 'L0_ffn_rb1': _L0_ffn_in['rb1'], 'L0_ffn_rw2': _L0_ffn_in['rw2'], 'L0_ffn_rb2': _L0_ffn_in['rb2'], 'L0_ffn_w1': _L0_ffn_in['w1'], 'L0_ffn_b1': _L0_ffn_in['b1'], 'L0_ffn_w2': _L0_ffn_in['w2'], 'L0_ffn_b2': _L0_ffn_in['b2']}

def reference(x, cls_tok, L0_tok_Wa, L0_tok_ba, L0_tok_Wd1, L0_tok_bd1, L0_tok_Wd2, L0_tok_bd2, L0_tok_Wd3, L0_tok_bd3, L0_attn_proj, L0_attn_w_qkv, L0_attn_w_out, L0_attn_b_out, L0_attn_gamma, L0_attn_beta, L0_attn_w1, L0_attn_b1, L0_attn_w2, L0_attn_b2, L0_ffn_rw1, L0_ffn_rb1, L0_ffn_rw2, L0_ffn_rb2, L0_ffn_w1, L0_ffn_b1, L0_ffn_w2, L0_ffn_b2):
    import jax
    import jax.numpy as jnp

    def _L0_tok_ref(x, Wa, ba, Wd1, bd1, Wd2, bd2, Wd3, bd3):
        import jax, jax.numpy as jnp
        import numpy as np
        INV_SQRT2 = 0.7071067811865476
        LEVEL = 3

        def _split(x, axis):
            ax = axis % x.ndim
            sl0 = [slice(None)] * x.ndim
            sl0[ax] = slice(0, None, 2)
            sl1 = [slice(None)] * x.ndim
            sl1[ax] = slice(1, None, 2)
            x0, x1 = (x[tuple(sl0)], x[tuple(sl1)])
            return ((x0 + x1) * INV_SQRT2, (x0 - x1) * INV_SQRT2)

        def _merge(lo, hi, axis):
            ax = axis % lo.ndim
            e = (lo + hi) * INV_SQRT2
            o = (lo - hi) * INV_SQRT2
            s = jnp.stack([e, o], axis=ax + 1)
            shape = list(lo.shape)
            shape[ax] *= 2
            return s.reshape(shape)

        def _dwt2(x):
            lo, hi = _split(x, -1)
            a, h = _split(lo, -2)
            v, d = _split(hi, -2)
            return (a, h, v, d)

        def _idwt2(a, h, v, d):
            lo = _merge(a, h, -2)
            hi = _merge(v, d, -2)
            return _merge(lo, hi, -1)
        img = x[..., 0]
        B = img.shape[0]
        details = []
        cur = img
        for _ in range(LEVEL):
            cur, h, v, d = _dwt2(cur)
            details.append((h, v, d))
        aw = jax.nn.sigmoid(cur.reshape(B, -1) @ Wa + ba)
        rec = cur * aw[:, :, None]
        det_params = [(Wd1, bd1), (Wd2, bd2), (Wd3, bd3)]
        for (h, v, d), (Wd, bd) in zip(reversed(details), det_params):
            flat = jnp.stack([h, v, d], axis=1).reshape(B, -1)
            w = jax.nn.softmax(flat @ Wd + bd, axis=-1)
            rec = _idwt2(rec, h * w[:, 0, None, None], v * w[:, 1, None, None], d * w[:, 2, None, None])
        return rec

    def _L0_attn_ref(x, proj, w_qkv, w_out, b_out, gamma, beta, w1, b1, w2, b2):
        import jax, jax.numpy as jnp
        import numpy as np
        B, N, D = (4, 1024, 256)
        H, F = (16, 64)
        HD = D // H
        EPS_ATTN = 1e-08
        EPS_LN = 1e-05

        def _layernorm(x, gamma, beta):
            mu = jnp.mean(x, axis=-1, keepdims=True)
            var = jnp.var(x, axis=-1, keepdims=True)
            return (x - mu) * jax.lax.rsqrt(var + EPS_LN) * gamma + beta
        residual = x
        b, n, d = x.shape
        qkv = x @ w_qkv.T
        q, k, v = jnp.split(qkv, 3, axis=-1)

        def to_heads(t):
            return t.reshape(b, n, H, HD).transpose(0, 2, 1, 3)
        q, k, v = (to_heads(q), to_heads(k), to_heads(v))
        q_f = jax.nn.elu(jnp.einsum('bhnd,hdf->bhnf', q, proj)) + 1.0
        k_f = jax.nn.elu(jnp.einsum('bhnd,hdf->bhnf', k, proj)) + 1.0
        kv = jnp.einsum('bhnf,bhnd->bhfd', k_f, v)
        attn = jnp.einsum('bhnf,bhfd->bhnd', q_f, kv)
        k_sum = jnp.sum(k_f, axis=2)
        z = 1.0 / (jnp.einsum('bhnf,bhf->bhn', q_f, k_sum) + EPS_ATTN)
        attn = attn * z[..., None]
        attn = attn.transpose(0, 2, 1, 3).reshape(b, n, d)
        x = residual + attn @ w_out.T + b_out
        x = _layernorm(x, gamma, beta)
        h = jax.nn.gelu(x @ w1.T + b1, approximate=False)
        x = x + h @ w2.T + b2
        x = _layernorm(x, gamma, beta)
        return x

    def _L0_ffn_ref(x, rw1, rb1, rw2, rb2, w1, b1, w2, b2):
        import jax, jax.numpy as jnp
        import numpy as np
        EMB, HID, E, TOPK = (256, 1024, 8, 2)
        B, S, D = x.shape
        logits = jax.nn.silu(jnp.einsum('bsd,dh->bsh', x, rw1) + rb1)
        logits = jnp.einsum('bsh,he->bse', logits, rw2) + rb2
        k_logits, k_index = jax.lax.top_k(logits, TOPK)
        k_prob = jax.nn.softmax(k_logits, axis=-1)
        xf = x.reshape(B * S, D)
        k_index_f = k_index.reshape(B * S, TOPK)
        k_prob_f = k_prob.reshape(B * S, TOPK)
        out = jnp.zeros_like(xf)
        for e in range(E):
            we = jnp.sum(jnp.where(k_index_f == e, k_prob_f, 0.0), axis=-1)
            h = jax.nn.silu(xf @ w1[e] + b1[e]) @ w2[e] + b2[e]
            out = out + we[:, None] * h
        return out.reshape(B, S, D)
    h = _L0_tok_ref(x, L0_tok_Wa, L0_tok_ba, L0_tok_Wd1, L0_tok_bd1, L0_tok_Wd2, L0_tok_bd2, L0_tok_Wd3, L0_tok_bd3)
    h = jnp.concatenate([jnp.broadcast_to(cls_tok, (h.shape[0], 1, h.shape[2])), h], axis=1)
    h = h + _L0_attn_ref(_layernorm(h, axis=-1), L0_attn_proj, L0_attn_w_qkv, L0_attn_w_out, L0_attn_b_out, L0_attn_gamma, L0_attn_beta, L0_attn_w1, L0_attn_b1, L0_attn_w2, L0_attn_b2)
    h = h + _L0_ffn_ref(_layernorm(h, axis=-1), L0_ffn_rw1, L0_ffn_rb1, L0_ffn_rw2, L0_ffn_rb2, L0_ffn_w1, L0_ffn_b1, L0_ffn_w2, L0_ffn_b2)
    return h

_drawn_inputs = setup_inputs


def setup_inputs(seed=0):
    import zlib

    import numpy as np

    out = dict(_drawn_inputs(seed))
    spreads = {'L0_tok_bd1': (0.0, 0.48),
     'L0_tok_bd2': (0.0, 0.58),
     'L0_tok_bd3': (0.0, 0.674),
     'L0_attn_b_out': (0.0, 0.1),
     'L0_attn_gamma': (1.0, 0.2),
     'L0_attn_beta': (0.0, 0.1),
     'L0_attn_b1': (0.0, 0.1),
     'L0_attn_b2': (0.0, 0.1),
     'L0_ffn_rb1': (0.0, 0.1),
     'L0_ffn_rb2': (0.0, 0.1),
     'L0_ffn_b1': (0.0, 0.486),
     'L0_ffn_b2': (0.0, 0.1)}
    factors = {}
    for name, (base, spread) in spreads.items():
        noise = np.random.default_rng([zlib.crc32(name.encode()), seed]).standard_normal(out[name].shape)
        drawn = base * np.exp(spread * noise) if base else spread * noise
        out[name] = jnp.asarray(drawn.astype(out[name].dtype))
    for name, factor in factors.items():
        out[name] = (out[name] * factor).astype(out[name].dtype)
    return out
```

```python
from contextlib import ExitStack

import concourse.bass as bass
from concourse import mybir

F32 = mybir.dt.float32
U32 = mybir.dt.uint32
I32 = mybir.dt.int32
ACT = mybir.ActivationFunctionType
ALU = mybir.AluOpType
AX_X = mybir.AxisListType.X

P = 128
B, IMG = 8, 256
D = IMG
SEQ = IMG + 1
HEADS, HD, FEAT = 16, 16, 64
PAIRS = HEADS // 2
HID = 4 * D
E = 8
KD = D // P
KH = HID // P
T = 2
EPS_LN, EPS_ATTN = 1e-5, 1e-8
TOKENS = B * SEQ
STRIPS = P // B
ROWS = IMG // STRIPS
REGION = 18 * P
MOE_TILES = (2 * TOKENS + E * (P - 1)) // P
PAY = D + 1 + E
VA = HD + 1
PW = 2 * VA
EXPERT = KD * HID + KH * D
ROUTING_LINKS = 17


class Chain:

    def __init__(self, eng, sem):
        self.eng, self.sem, self.n, self.base = eng, sem, 0, 0

    def link(self, ins):
        self.n += 1
        ins.then_inc(self.sem, 1)
        self.eng.wait_ge(self.sem, self.base + self.n)

    def loop(self, count, links, body):
        n = self.n
        with self.eng.Fori(0, count) as it:
            self.base = it * links
            body(it)
        assert self.n - n == links, (self.n - n, links)
        self.n, self.base = n + count * links, 0


def apart(eng, passed):
    eng.sem_inc(passed, 1)


def after(eng, sem, value):
    if not isinstance(value, int) or value > 0:
        eng.wait_ge(sem, value)


def build(nc, t):
    xs_d = nc.dram_tensor("routed_rows", (E * REGION + P, PAY), F32, kind="Internal").ap()
    acc_d = nc.dram_tensor("token_sums", (TOKENS + P, D), F32, kind="Internal").ap()

    with ExitStack() as ctx:
        def sb(name, shape, dt=F32):
            return ctx.enter_context(nc.sbuf_tensor(name, shape, dt))

        def sem(name):
            return ctx.enter_context(nc.semaphore(name))

        arena = sb("arena", [P, E * EXPERT])
        dense = sb("dense", [P, 9280])
        h = sb("h", [P, B * T, D])
        x1 = sb("x1", [P, B * T, D])
        small = sb("small", [P, 2124])

        cut_at = [0]

        def cut(tensor, width):
            a = cut_at[0]
            cut_at[0] += width
            assert cut_at[0] <= tensor.shape[1], (cut_at[0], tensor.shape)
            return tensor[:, a:a + width]

        def at(tensor):
            cut_at[0] = tensor

        at(0)
        wqkvT = cut(dense, KD * 3 * D).rearrange("p (k n) -> p k n", k=KD)
        woT = cut(dense, KD * D).rearrange("p (k n) -> p k n", k=KD)
        w1T = cut(dense, KD * HID).rearrange("p (k n) -> p k n", k=KD)
        w2T = cut(dense, KH * D).rearrange("p (k n) -> p k n", k=KH)
        rw1 = cut(dense, KD * HID).rearrange("p (k n) -> p k n", k=KD)
        projbd = cut(dense, KD * 8 * FEAT).rearrange("p (k n) -> p k n", k=KD)
        rw2 = cut(dense, KH * E).rearrange("p (k n) -> p k n", k=KH)

        at(0)
        xs = [cut(dense, PAY) for _ in range(2)]
        xsT = [cut(dense, D) for _ in range(2)]
        hraw = [cut(dense, HID) for _ in range(2)]
        hT = [cut(dense, HID).rearrange("p (k n) -> p k n", k=KH) for _ in range(2)]
        ybias = [cut(dense, D) for _ in range(2)]
        y = [cut(dense, D) for _ in range(2)]

        at(0)
        img = cut(arena, ROWS * IMG)
        lohi = cut(arena, ROWS * IMG)
        det = {1: cut(arena, 3 * 1024)}
        app = {1: cut(arena, 1024)}
        det[2], app[2] = cut(arena, 3 * 256), cut(arena, 256)
        det[3], app[3] = cut(arena, 3 * 64), cut(arena, 64)
        wd = {2: cut(arena, 9 * 256)}
        at(16384)
        wd[1] = cut(arena, 9 * 1024)
        wd[3] = cut(arena, 9 * 64)
        wa = cut(arena, 64)
        raw_qkv = cut(arena, 6 * D).rearrange("p (m n) -> p m n", m=6)
        raw_o = cut(arena, KD * D).rearrange("p (m n) -> p m n", m=KD)
        raw_w1 = cut(arena, KH * D).rearrange("p (m n) -> p m n", m=KH)
        raw_w2 = cut(arena, KD * HID).rearrange("p (m n) -> p m n", m=KD)
        raw_cols = cut(arena, P)

        at(0)
        xn = [cut(arena, T * D).rearrange("p (t n) -> p t n", t=T) for _ in range(2)]
        xnb = [cut(arena, T * D).rearrange("p (t n) -> p t n", t=T) for _ in range(2)]
        xnT = [cut(arena, KD * IMG).rearrange("p (k n) -> p k n", k=KD) for _ in range(2)]
        qT = [cut(arena, KD * IMG).rearrange("p (k n) -> p k n", k=KD) for _ in range(2)]
        kT = [cut(arena, KD * IMG).rearrange("p (k n) -> p k n", k=KD) for _ in range(2)]
        va = [cut(arena, T * HEADS * VA).rearrange("p (t h d) -> p t h d", t=T, h=HEADS) for _ in range(2)]
        kf = [cut(arena, T * HEADS * FEAT).rearrange("p (t c n) -> p t c n", t=T, c=KD) for _ in range(2)]
        qf = [cut(arena, PAIRS * IMG).rearrange("p (m n) -> p m n", m=PAIRS) for _ in range(2)]
        lin = [cut(arena, 512) for _ in range(4)]
        kvbd = [cut(arena, PAIRS * PW).rearrange("p (m n) -> p m n", m=PAIRS) for _ in range(2)]
        att = [cut(arena, T * D).rearrange("p (t n) -> p t n", t=T) for _ in range(2)]
        attT = [cut(arena, KD * IMG).rearrange("p (k n) -> p k n", k=KD) for _ in range(2)]
        catt = cut(arena, B * D).rearrange("p (b n) -> p b n", b=B)
        c_va = cut(arena, HEADS * VA).rearrange("p (h d) -> p h d", h=HEADS)
        c_kf = cut(arena, HEADS * FEAT)
        c_kl = cut(arena, HEADS * FEAT)

        at(16384)
        xh = [cut(arena, T * D).rearrange("p (t n) -> p t n", t=T) for _ in range(2)]
        x1b = [cut(arena, T * D).rearrange("p (t n) -> p t n", t=T) for _ in range(2)]
        x1T = [cut(arena, KD * IMG).rearrange("p (k n) -> p k n", k=KD) for _ in range(2)]
        gT = [cut(arena, KH * IMG).rearrange("p (k n) -> p k n", k=KH) for _ in range(2)]
        x2 = [cut(arena, T * D).rearrange("p (t n) -> p t n", t=T) for _ in range(2)]
        pay = [cut(arena, T * PAY).rearrange("p (t n) -> p t n", t=T) for _ in range(2)]
        xmT = [cut(arena, KD * IMG).rearrange("p (k n) -> p k n", k=KD) for _ in range(2)]
        rT = [cut(arena, KH * IMG).rearrange("p (k n) -> p k n", k=KH) for _ in range(2)]

        experts = arena[:, :].rearrange("p (e n) -> p e n", e=E)
        b2bc = x1[:, 0:E, :]

        at(0)
        ident = cut(small, P)
        same = cut(small, P)
        before = cut(small, P)
        ones = cut(small, P)
        gamma_bc, beta_bc, beta2_bc, bout_bc = (cut(small, D) for _ in range(4))
        cols = cut(small, E * KH + 2 * KH + 2 * KD)
        eb1T = cols[:, 0:E * KH].rearrange("p (e k) -> p e k", e=E)
        b1T, rb1T = cols[:, 64:72], cols[:, 72:80]
        gammaT, betaT = cols[:, 80:82], cols[:, 82:84]
        gate_now = [cut(small, 1) for _ in range(2)]
        b1now = [cut(small, KH) for _ in range(2)]
        dots = cut(small, 10)
        bd = cut(small, 10)
        gate = cut(small, 10)
        gsc = cut(small, 24)
        stats = cut(small, T * 6).rearrange("p (t n) -> p t n", t=T)
        mv = cut(small, T * 2).rearrange("p (t n) -> p t n", t=T)
        rstd = cut(small, T).rearrange("p (t n) -> p t n", t=T)
        neg_half = cut(small, T).rearrange("p (t n) -> p t n", t=T)
        den = cut(small, (T + 1) * HEADS).rearrange("p (t h) -> p t h", t=T + 1)
        c_xT, c_qT, c_kT = (cut(small, KD) for _ in range(3))
        c_qf, c_ql = cut(small, PAIRS), cut(small, PAIRS)
        rb2_bc = cut(small, E)
        iota8 = cut(small, E)
        lg = cut(small, T * E).rearrange("p (t e) -> p t e", t=T)
        top = cut(small, T * 8).rearrange("p (t e) -> p t e", t=T)
        topf = cut(small, T * 2).rearrange("p (t e) -> p t e", t=T)
        gap = cut(small, T).rearrange("p (t n) -> p t n", t=T)
        half = cut(small, T).rearrange("p (t n) -> p t n", t=T)
        probs = cut(small, 2 * T).rearrange("p (k t n) -> p k t n", k=2, t=T)
        onehot = cut(small, 2 * T * E).rearrange("p (k t e) -> p k t e", k=2, t=T)
        mask = cut(small, T * E).rearrange("p (t e) -> p t e", t=T)
        weighed = cut(small, 2 * T * E).rearrange("p (k t e) -> p k t e", k=2, t=T)
        rank = cut(small, T * E).rearrange("p (t e) -> p t e", t=T)
        placed = cut(small, 2 * T * E).rearrange("p (k t e) -> p k t e", k=2, t=T)
        placef = cut(small, 2 * T).rearrange("p (k t n) -> p k t n", k=2, t=T)
        used = cut(small, E)
        ids = cut(small, T).rearrange("p (t n) -> p t n", t=T)
        topi = sb("topi", [P, T, 8], U32)
        place = [sb(f"place{i}", [P, 2, T], U32) for i in range(2)]
        c_place = sb("c_place", [P, 2], U32)
        slot_ids = [sb(f"slot_ids{i}", [P, 1], U32) for i in range(2)]
        cx = sb("cx", [B, 3, D])
        c_attT = sb("c_attT", [P, KD, B])
        limits = cut(small, 18)
        tnum = cut(small, MOE_TILES)
        region0 = cut(small, E + 1)
        first_src = cut(small, (E + 1) * E).rearrange("p (a e) -> p a e", a=E + 1)
        at(6400)
        over = cut(dense, E * 18).rearrange("p (e j) -> p e j", e=E)
        count = cut(dense, E)
        tiles_e = cut(dense, E)
        lower = cut(dense, (E + 1) * E).rearrange("p (a e) -> p a e", a=E + 1)
        first = cut(dense, E + 1)
        owner = cut(dense, MOE_TILES)
        step = cut(dense, MOE_TILES)
        rowt = cut(dense, MOE_TILES)
        jump = cut(dense, E + 1)
        owner_i, row_i = (cut(dense, MOE_TILES).bitcast(I32) for _ in range(2))
        used_i = cut(dense, E).bitcast(I32)
        padrow = cut(dense, PAY)

        bank = [ctx.enter_context(nc.psum_tensor(f"bank{i}", [P, 512], F32)) for i in range(8)]
        psT, psL, psF, psKV, psAT = bank[0], bank[1:3], bank[3:5], bank[5], bank[6:8]
        psO, psLG, psRK = bank[6:8], bank[1], bank[2]
        psH2 = bank[1:3]

        img_loaded = sem("img_loaded")
        wd1_loaded = sem("wd1_loaded")
        wd2_loaded = sem("wd2_loaded")
        wd3_loaded = sem("wd3_loaded")
        wa_loaded = sem("wa_loaded")
        smalls_loaded = sem("smalls_loaded")
        raw_loaded = sem("raw_loaded")
        direct_loaded = sem("direct_loaded")
        dve_passed = sem("dve_passed")
        pool_passed = sem("pool_passed")
        iota_ready = sem("iota_ready")
        consts_ready = sem("consts_ready")
        pool_step = sem("pool_step")
        dve_step = sem("dve_step")
        act_step = sem("act_step")
        dots_ready = sem("dots_ready")
        totals_ready = sem("totals_ready")
        logits_ready = sem("logits_ready")
        exps_ready = sem("exps_ready")
        image_ready = sem("image_ready")
        relaid = sem("relaid")
        wT_ps = sem("wT_ps")
        wT_sb = sem("wT_sb")
        c_norm = sem("c_norm")
        c_ps = sem("c_ps")
        c_done = sem("c_done")
        catt_moved = sem("catt_moved")
        cattT_ps = sem("cattT_ps")
        cattT_sb = sem("cattT_sb")
        c_out_ps = sem("c_out_ps")
        c_x1 = sem("c_x1")
        c_var = sem("c_var")
        c_root = sem("c_root")
        t_var = sem("t_var")
        t_root = sem("t_root")
        x_var = sem("x_var")
        x_root = sem("x_root")
        m_var = sem("m_var")
        m_root = sem("m_root")
        ln_ready = sem("ln_ready")
        xnb_ready = sem("xnb_ready")
        xT_ps = sem("xT_ps")
        xT_sb = sem("xT_sb")
        q_ps = sem("q_ps")
        q_sb = sem("q_sb")
        k_ps = sem("k_ps")
        k_sb = sem("k_sb")
        v_ps = sem("v_ps")
        v_sb = sem("v_sb")
        f_ps = sem("f_ps")
        f_neg = sem("f_neg")
        f_read = sem("f_read")
        f_exp = sem("f_exp")
        f_sum = sem("f_sum")
        kv_ps = sem("kv_ps")
        kvbd_ready = sem("kvbd_ready")
        attn_ps = sem("attn_ps")
        att_ready = sem("att_ready")
        attT_ps = sem("attT_ps")
        attT_sb = sem("attT_sb")
        out_ps = sem("out_ps")
        x1_ready = sem("x1_ready")
        xh_ready = sem("xh_ready")
        x1b_ready = sem("x1b_ready")
        x1T_ps = sem("x1T_ps")
        x1T_sb = sem("x1T_sb")
        m_ps = sem("m_ps")
        m_sb = sem("m_sb")
        mlp_ps = sem("mlp_ps")
        xm_ready = sem("xm_ready")
        h1_ready = sem("h1_ready")
        xmT_ps = sem("xmT_ps")
        xmT_sb = sem("xmT_sb")
        lg_ps = sem("lg_ps")
        lg_gap = sem("lg_gap")
        lg_half = sem("lg_half")
        mask_ready = sem("mask_ready")
        rk_ps = sem("rk_ps")
        place_ready = sem("place_ready")
        scat0 = sem("scat0")
        scat1 = sem("scat1")
        h1_stored0 = sem("h1_stored0")
        h1_stored1 = sem("h1_stored1")
        used_ready = sem("used_ready")
        pad_ready = sem("pad_ready")
        tables_ready = sem("tables_ready")
        pads_stored = sem("pads_stored")
        dump_zeroed = sem("dump_zeroed")
        low_loaded = sem("low_loaded")
        high_loaded = sem("high_loaded")
        b2_loaded = sem("b2_loaded")
        xs_loaded0 = sem("xs_loaded0")
        xs_loaded1 = sem("xs_loaded1")
        xsT_ps = sem("xsT_ps")
        xsT_sb = sem("xsT_sb")
        h_ps = sem("h_ps")
        hraw_ready = sem("hraw_ready")
        hT_ps = sem("hT_ps")
        hT_sb = sem("hT_sb")
        y_ps = sem("y_ps")
        y_ready = sem("y_ready")
        b1_ready = sem("b1_ready")
        slot_ready = sem("slot_ready")
        rows_added = sem("rows_added")
        out_stored = sem("out_stored")

        def vector(name):
            return t[name].rearrange("(o n) -> o n", o=1)

        smalls = [(gamma_bc, vector("L0_attn_gamma").to_broadcast([P, D])),
                  (beta_bc, vector("L0_attn_beta").to_broadcast([P, D])),
                  (beta2_bc, vector("L0_attn_b2").to_broadcast([P, D])),
                  (bout_bc, vector("L0_attn_b_out").to_broadcast([P, D])),
                  (bd[:, 0:1], vector("L0_tok_ba").to_broadcast([P, 1])),
                  (bd[:, 1:4], vector("L0_tok_bd1").to_broadcast([P, 3])),
                  (bd[:, 4:7], vector("L0_tok_bd2").to_broadcast([P, 3])),
                  (bd[:, 7:10], vector("L0_tok_bd3").to_broadcast([P, 3])),
                  (rb2_bc, vector("L0_ffn_rb2").to_broadcast([P, E])),
                  (cx[0:B, 0, :], t["cls_tok"].rearrange("o q n -> (o q) n").to_broadcast([B, D]))]
        raws = [(raw_qkv, t["L0_attn_w_qkv"].rearrange("(m p) n -> p m n", p=P)),
                (raw_o, t["L0_attn_w_out"].rearrange("(m p) n -> p m n", p=P)),
                (raw_w1, t["L0_attn_w1"].rearrange("(m p) n -> p m n", p=P)),
                (raw_w2, t["L0_attn_w2"].rearrange("(m p) n -> p m n", p=P)),
                (raw_cols[0:64, :], t["L0_ffn_b1"].rearrange("e (k p) -> (e k) p", p=P)),
                (raw_cols[64:72, :], t["L0_attn_b1"].rearrange("(k p) -> k p", p=P)),
                (raw_cols[72:80, :], t["L0_ffn_rb1"].rearrange("(k p) -> k p", p=P)),
                (raw_cols[80:82, :], t["L0_attn_gamma"].rearrange("(k p) -> k p", p=P)),
                (raw_cols[82:84, :], t["L0_attn_beta"].rearrange("(k p) -> k p", p=P))]

        def feature_rows(par, i):
            if i < 4:
                return kf[par][:, i // 2, i % 2, :]
            return qf[par][:, 2 * (i - 4):2 * (i - 4) + 2, :].rearrange("p m n -> p (m n)")

        def block_of(raw, m, k):
            return raw[:, m, k * P:(k + 1) * P]

        turned = [(wqkvT[:, k, 0:4 * P], [block_of(raw_qkv, m, k) for m in range(4)]) for k in range(KD)]
        turned += [(wqkvT[:, :, 4 * P:6 * P], [block_of(raw_qkv, m, k) for k in range(KD) for m in (4, 5)])]
        turned += [(woT[:, :, :], [block_of(raw_o, m, k) for k in range(KD) for m in range(KD)])]
        turned += [(w1T[:, k, 4 * P * q:4 * P * (q + 1)], [block_of(raw_w1, m, k) for m in range(4 * q, 4 * q + 4)])
                   for k in range(KD) for q in range(2)]
        turned += [(w2T[:, 2 * i:2 * i + 2, :], [block_of(raw_w2, m, k) for k in (2 * i, 2 * i + 1) for m in range(KD)])
                   for i in range(KH // 2)]

        def normalize(dve, link, src, dst, n, tiles, asked, answered, count):
            apart(dve, dve_passed)
            for j in range(tiles):
                ins = dve.bn_stats(stats[0:n, j, :], src(j))
            link(ins)
            apart(dve, dve_passed)
            for j in range(tiles):
                ins = dve.bn_aggr(mv[0:n, j, :], stats[0:n, j, :])
            ins.then_inc(asked, 1)
            dve.wait_ge(answered, count)
            for j in range(tiles):
                ins = dve.tensor_scalar(dst(j), src(j), mv[0:n, j, 0:1], rstd[0:n, j, :], ALU.subtract, ALU.mult)
            return ins

        def root(pool, link, n, tiles, asked, answered, count):
            pool.wait_ge(asked, count)
            apart(pool, pool_passed)
            link(pool.tensor_scalar(rstd[0:n, 0:tiles, :], mv[0:n, 0:tiles, 1:2], EPS_LN, None, ALU.add))
            pool.tensor_tensor(rstd[0:n, 0:tiles, :], rstd[0:n, 0:tiles, :], neg_half[0:n, 0:tiles, :], ALU.pow
                               ).then_inc(answered, 1)

        block = ctx.enter_context(nc.Block())

        @block.sync
        def _(sp):
            sp.dma_start(img, t["x"].rearrange("b (s r) w c -> (b s) (r w c)", s=STRIPS)).then_inc(img_loaded, 16)
            for lvl, loaded, w in ((3, wd3_loaded, t["L0_tok_Wd1"]), (2, wd2_loaded, t["L0_tok_Wd2"]),
                                   (1, wd1_loaded, t["L0_tok_Wd3"])):
                n = wd[lvl].shape[1] // 3
                src = w.rearrange("(c s n) k -> s c (n k)", c=3, s=STRIPS)
                for b in range(B):
                    dst = wd[lvl][STRIPS * b:STRIPS * (b + 1), :].rearrange("p (c m) -> p c m", c=3)
                    assert dst.shape[2] == n
                    sp.dma_start(dst, src).then_inc(loaded, 16)
            for b in range(B):
                sp.dma_start(wa[STRIPS * b:STRIPS * (b + 1), :],
                             t["L0_tok_Wa"].rearrange("(s n) k -> s (n k)", s=STRIPS)).then_inc(wa_loaded, 16)
            sp.wait_ge(image_ready, 1)
            for b in range(B):
                for j in range(T):
                    p0 = STRIPS * b + STRIPS // T * j
                    sp.dma_start(h[:, T * b + j, :],
                                 img[p0:p0 + STRIPS // T, :].rearrange("p (r n) -> p r n", r=ROWS)
                                 ).then_inc(relaid, 16)
            sp.wait_ge(att_ready, 3 * B)
            sp.dma_start(cx[0:B, 2, :], catt[0:1, :, :]).then_inc(catt_moved, 16)
            sp.wait_ge(c_x1, 1)
            sp.wait_ge(x1_ready, B)
            sp.wait_ge(catt_moved, 16)
            def load_expert(e, loaded):
                sp.dma_start(experts[:, e, 0:KD * HID].rearrange("p (k n) -> p k n", k=KD),
                             t["L0_ffn_w1"][e].rearrange("(k p) n -> p k n", p=P)).then_inc(loaded, 16)
                sp.dma_start(experts[:, e, KD * HID:EXPERT].rearrange("p (k n) -> p k n", k=KH),
                             t["L0_ffn_w2"][e].rearrange("(k p) n -> p k n", p=P)).then_inc(loaded, 16)

            for e in range(E // 2):
                load_expert(e, low_loaded)
            stored = [h1_stored0, h1_stored1]

            def store_h1(g, par):
                sp.wait_ge(h1_ready, g + 1)
                sp.dma_start(acc_d[bass.ds(g * SEQ + 1, IMG), :].rearrange("(t p) n -> p t n", p=P),
                             h[:, bass.ds(T * g, T), :]).then_inc(stored[par], 16)
            with sp.Fori(0, B // 2) as it:
                store_h1(2 * it, 0)
                store_h1(2 * it + 1, 1)
            sp.wait_ge(h1_ready, B + 1)
            sp.dma_start(acc_d[0:TOKENS, :].rearrange("(b q) n -> b q n", b=B)[:, 0, :],
                         cx[0:B, 0, :]).then_inc(h1_stored0, 16)
            sp.wait_ge(rk_ps, B + 1)
            sp.wait_ge(scat0, 16 * 2 * (T * B // 2 + 1))
            sp.wait_ge(scat1, 16 * 2 * (T * B // 2))
            for e in range(E // 2, E):
                load_expert(e, high_loaded)
            sp.dma_start(b2bc, t["L0_ffn_b2"].rearrange("(o e) n -> o e n", o=1).to_broadcast([P, E, D])
                         ).then_inc(b2_loaded, 16)
            sp.wait_ge(pad_ready, 1)
            sp.dma_start(acc_d[TOKENS:TOKENS + P, :], padrow[:, 0:D]).then_inc(dump_zeroed, 16)
            with sp.Fori(0, E) as e:
                row = sp.value_load(used_i[0:1, bass.ds(e, 1)], min_val=0, max_val=E * REGION - P)
                sp.dma_start(xs_d[bass.ds(row, P), :], padrow[:, :]).then_inc(pads_stored, 16)
            sp.dma_start(xs_d[E * REGION:E * REGION + P, :], padrow[:, :]).then_inc(pads_stored, 16)
            sp.wait_ge(pads_stored, 16 * (E + 1))
            sp.wait_ge(tables_ready, 1)
            loaded = [xs_loaded0, xs_loaded1]

            def load_rows(i, par, ahead):
                if ahead:
                    sp.wait_ge(xsT_ps, i - 1)
                    sp.wait_ge(slot_ready, i - 1)
                row = sp.value_load(row_i[0:1, bass.ds(i, 1)], min_val=0, max_val=E * REGION)
                sp.dma_start(xs[par], xs_d[bass.ds(row, P), :]).then_inc(loaded[par], 16)
            load_rows(0, 0, False)
            load_rows(1, 1, False)
            with sp.Fori(0, MOE_TILES // 2 - 1) as it:
                load_rows(2 * it + 2, 0, True)
                load_rows(2 * it + 3, 1, True)
            sp.wait_ge(rows_added, 16 * MOE_TILES)
            sp.dma_start(t["out"].rearrange("b q n -> (b q) n"), acc_d[0:TOKENS, :]).then_inc(out_stored, 16)
            sp.wait_ge(out_stored, 16)

        @block.gpsimd
        def _(pool):
            chain = Chain(pool, pool_step)
            link = chain.link

            def triangle(out, op, base, fill, mult, pattern):
                return pool.affine_select(out=out, in_=out, compare_op=op, fill=fill, base=base,
                                          pattern=pattern, channel_multiplier=mult)

            pool.memset(ident, 0.0)
            pool.memset(same, 1.0)
            pool.memset(before, 1.0)
            pool.memset(ones, 1.0)
            pool.memset(neg_half, -0.5)
            pool.memset(first_src[:, :, :], 1.0)
            pool.memset(projbd[:, :, :], 0.0).then_inc(iota_ready, 1)
            link(pool.memset(cols, 0.0))
            triangle(ident, ALU.not_equal, 0, 1.0, 1, [[-1, P]])
            link(triangle(same.rearrange("p (b s) -> p b s", b=B), ALU.is_ge, 0, 0.0, 1, [[-STRIPS, B], [0, STRIPS]]))
            triangle(same.rearrange("p (b s) -> p b s", b=B), ALU.is_ge, STRIPS - 1, 0.0, -1,
                     [[STRIPS, B], [0, STRIPS]])
            triangle(before, ALU.is_ge, -1, 0.0, -1, [[1, P]])
            triangle(first_src, ALU.is_ge, -1, 0.0, 0, [[1, E + 1], [-1, E]])
            pool.iota(iota8, [[1, E]], base=0, channel_multiplier=0, allow_small_or_imprecise_dtypes=True)
            pool.iota(used, [[REGION, E]], base=0, channel_multiplier=0, allow_small_or_imprecise_dtypes=True)
            pool.iota(region0, [[REGION, E + 1]], base=0, channel_multiplier=0, allow_small_or_imprecise_dtypes=True)
            pool.iota(limits, [[P, 18]], base=0, channel_multiplier=0, allow_small_or_imprecise_dtypes=True)
            pool.iota(tnum, [[1, MOE_TILES]], base=0, channel_multiplier=0, allow_small_or_imprecise_dtypes=True)
            pool.iota(ids[:, :, 0], [[P, T]], base=1, channel_multiplier=1,
                      allow_small_or_imprecise_dtypes=True).then_inc(consts_ready, 1)
            pool.wait_ge(smalls_loaded, 16 * len(smalls))
            link(pool.tensor_tensor(beta2_bc, beta2_bc, beta_bc, ALU.add))

            def residual(g, par):
                pool.wait_ge(ln_ready, g + 1)
                after(pool, x1_ready, g - 1)
                for j in range(T):
                    ins = pool.tensor_tensor(xnb[par][:, j, :], xn[par][:, j, :], bout_bc, ALU.add)
                ins.then_inc(xnb_ready, 1)
            root(pool, link, B, 1, c_var, c_root, 1)
            root(pool, link, P, T, t_var, t_root, 1)
            root(pool, link, P, T, t_var, t_root, 2)
            residual(0, 0)

            def attention_step(g, par):
                for i in range(8):
                    u = 8 * g + i
                    pool.wait_ge(f_exp, u + 1)
                    dst = feature_rows(par, i)
                    pool.tensor_tensor(dst, dst, lin[i % 4], ALU.add).then_inc(f_sum, 1)
                if not isinstance(g, int) or g + 1 < B:
                    residual(g + 1, 1 - par)
                if not isinstance(g, int) or g + 2 < B:
                    root(pool, link, P, T, t_var, t_root, g + 3)

            attention_step(0, 0)

            def turn(it):
                attention_step(2 * it + 1, 1)
                attention_step(2 * it + 2, 0)
            chain.loop((B - 4) // 2, 2, turn)
            for g in range(B - 3, B):
                attention_step(g, g % 2)

            def affine(g, par):
                pool.wait_ge(xh_ready, g + 1)
                tiles, n, hx = (T, P, None) if not (isinstance(g, int) and g == B) else (1, B, cx)
                after(pool, xm_ready, g - 1)
                for j in range(tiles):
                    ins = pool.tensor_tensor(x1b[par][0:n, j, :], xh[par][0:n, j, :], gamma_bc[0:n, :], ALU.mult)
                for j in range(tiles):
                    hj = h[:, bass.ds(T * g + j, 1), :].rearrange("p o n -> p (o n)") if hx is None else cx[0:B, 0, :]
                    ins = pool.tensor_tensor(hj, hj, beta_bc[0:n, :], ALU.add)
                link(ins)
                for j in range(tiles):
                    ins = pool.tensor_tensor(x1b[par][0:n, j, :], x1b[par][0:n, j, :], beta2_bc[0:n, :], ALU.add)
                ins.then_inc(x1b_ready, 1)

            def scatter(g, par):
                pool.wait_ge(place_ready, g + 1)
                apart(pool, pool_passed)
                tail = isinstance(g, int) and g == B
                done = scat0 if par == 0 else scat1
                for j in range(1 if tail else T):
                    for k in range(2):
                        n = B if tail else P
                        idx = c_place[0:B, k:k + 1] if tail else place[par][:, k, j:j + 1]
                        pool.indirect_dma_start(
                            out=xs_d[:, :], out_offset=bass.IndirectOffsetOnAxis(ap=idx, axis=0),
                            in_=pay[par][0:n, j, :], in_offset=None).then_inc(done, 16)

            root(pool, link, P, T, x_var, x_root, 1)
            root(pool, link, P, T, x_var, x_root, 2)
            affine(0, 0)
            affine(1, 1)

            def routing_step(g, par):
                if not isinstance(g, int) or g <= B:
                    n, tiles = (B, 1) if isinstance(g, int) and g == B else (P, T)
                    root(pool, link, n, tiles, m_var, m_root, 2 * g + 1)
                    root(pool, link, n, tiles, m_var, m_root, 2 * g + 2)
                if not isinstance(g, int) or g + 2 <= B:
                    n, tiles = (B, 1) if isinstance(g, int) and g + 2 == B else (P, T)
                    root(pool, link, n, tiles, x_var, x_root, g + 3)
                if not isinstance(g, int) or g >= 1:
                    scatter(g - 1, 1 - par)
                if not isinstance(g, int) or g + 2 <= B:
                    affine(g + 2, par)
            routing_step(0, 0)

            def turn(it):
                routing_step(2 * it + 1, 1)
                routing_step(2 * it + 2, 0)
            chain.loop(2, 8, turn)
            for g in range(5, B + 2):
                routing_step(g, g % 2)

            pool.wait_ge(used_ready, 1)
            link(pool.memset(padrow, 0.0))
            pool.iota(padrow[:, D:D + 1], [[0, 1]], base=TOKENS, channel_multiplier=1,
                      allow_small_or_imprecise_dtypes=True).then_inc(pad_ready, 1)

            pool.wait_ge(h1_stored0, 16 * (B // 2 + 1))
            pool.wait_ge(h1_stored1, 16 * (B // 2))
            pool.wait_ge(dump_zeroed, 16)

            def add_rows(i, par, later):
                if later:
                    pool.wait_ge(rows_added, i * 16)
                pool.wait_ge(y_ready, i + 1)
                apart(pool, pool_passed)
                pool.indirect_dma_start(
                    out=acc_d[:, :], out_offset=bass.IndirectOffsetOnAxis(ap=slot_ids[par][:, 0:1], axis=0),
                    in_=y[par], in_offset=None, compute_op=ALU.add).then_inc(rows_added, 16)
            add_rows(0, 0, False)
            add_rows(1, 1, True)
            with pool.Fori(0, MOE_TILES // 2 - 1) as it:
                add_rows(2 * it + 2, 0, True)
                add_rows(2 * it + 3, 1, True)

        @block.vector
        def _(dve):
            chain = Chain(dve, dve_step)
            link = chain.link

            dve.wait_ge(img_loaded, 16)
            cur, side, rows = img, IMG, ROWS
            for lvl in (1, 2, 3):
                c2 = cur[:, 0:rows * side].rearrange("p (m two) -> p m two", two=2)
                n = rows * side // 2
                lo, hi = lohi[:, 0:n], lohi[:, n:2 * n]
                dve.tensor_tensor(lo, c2[:, :, 0], c2[:, :, 1], ALU.add)
                link(dve.tensor_tensor(hi, c2[:, :, 0], c2[:, :, 1], ALU.subtract))
                q = n // 2
                lo4 = lo.rearrange("p (r two c) -> p r two c", two=2, c=side // 2)
                hi4 = hi.rearrange("p (r two c) -> p r two c", two=2, c=side // 2)

                def band(ap):
                    return ap.rearrange("p (r c) -> p r c", c=side // 2)
                dd = det[lvl]
                dve.tensor_tensor(band(app[lvl][:, 0:q]), lo4[:, :, 0, :], lo4[:, :, 1, :], ALU.add)
                dve.tensor_tensor(band(dd[:, 0:q]), lo4[:, :, 0, :], lo4[:, :, 1, :], ALU.subtract)
                dve.tensor_tensor(band(dd[:, q:2 * q]), hi4[:, :, 0, :], hi4[:, :, 1, :], ALU.add)
                link(dve.tensor_tensor(band(dd[:, 2 * q:3 * q]), hi4[:, :, 0, :], hi4[:, :, 1, :], ALU.subtract))
                cur, side, rows = app[lvl], side // 2, rows // 2

            junk = img
            dve.wait_ge(wa_loaded, 16 * B)
            link(dve.tensor_tensor_reduce(junk[:, 0:64], app[3], wa, 1.0, 0.0, ALU.mult, ALU.add, dots[:, 0:1]))
            for lvl, loaded, c0 in ((3, wd3_loaded, 1), (2, wd2_loaded, 4), (1, wd1_loaded, 7)):
                dve.wait_ge(loaded, 16 * B)
                n = det[lvl].shape[1]
                w3 = wd[lvl].rearrange("p (n k) -> p n k", k=3)
                for k in range(3):
                    ins = dve.tensor_tensor_reduce(junk[:, 0:n], det[lvl][:, :], w3[:, :, k], 1.0, 0.0, ALU.mult,
                                                   ALU.add, dots[:, c0 + k:c0 + k + 1])
                    if lvl == 1 and k == 2:
                        ins.then_inc(dots_ready, 1)
                    else:
                        link(ins)
            dve.wait_ge(smalls_loaded, 16 * len(smalls))
            dve.wait_ge(totals_ready, 1)
            for c0, c1, scale in ((0, 4, 0.125), (4, 7, 0.25), (7, 10, 0.5)):
                ins = dve.scalar_tensor_tensor(out=gate[:, c0:c1], in0=psT[:, c0:c1], scalar=scale,
                                               in1=bd[:, c0:c1], op0=ALU.mult, op1=ALU.add)
            link(ins)
            g3 = gate[:, 1:10].rearrange("p (l k) -> p l k", k=3)
            m3 = gsc[:, 0:3].rearrange("p (l o) -> p l o", o=1)
            link(dve.tensor_reduce(gsc[:, 0:3], g3, AX_X, ALU.max))
            dve.tensor_tensor(g3, g3, m3.to_broadcast([P, 3, 3]), ALU.subtract).then_inc(logits_ready, 1)
            dve.wait_ge(exps_ready, 1)
            dve.tensor_scalar(gsc[:, 3:4], gate[:, 0:1], 1.0, None, ALU.add)
            link(dve.tensor_reduce(gsc[:, 4:7], g3, AX_X, ALU.add))
            link(dve.reciprocal(gsc[:, 7:11], gsc[:, 3:7]))
            dve.tensor_scalar(gate[:, 0:1], gsc[:, 7:8], 1.0 / 64, None, ALU.mult)
            for l, f in ((0, 1.0 / 64), (1, 1.0 / 16), (2, 1.0 / 4)):
                ins = dve.tensor_scalar(gate[:, 1 + 3 * l:4 + 3 * l], gate[:, 1 + 3 * l:4 + 3 * l],
                                        gsc[:, 8 + l:9 + l], f, ALU.mult, ALU.mult)
            link(ins)
            link(dve.tensor_scalar(gsc[:, 12:21], gate[:, 1:10], -1.0, None, ALU.mult))

            link(dve.tensor_scalar(app[3][:, :], app[3][:, :], gate[:, 0:1], None, ALU.mult))
            for l, lvl in ((0, 3), (1, 2), (2, 1)):
                q = app[lvl].shape[1]
                side = IMG >> lvl
                dd = det[lvl]
                lo4 = lohi[:, 0:2 * q].rearrange("p (r two c) -> p r two c", two=2, c=side)
                hi4 = lohi[:, 2 * q:4 * q].rearrange("p (r two c) -> p r two c", two=2, c=side)

                def band(ap):
                    return ap.rearrange("p (r c) -> p r c", c=side)
                gh, gv, gd = (gate[:, 1 + 3 * l + k:2 + 3 * l + k] for k in range(3))
                ngh = gsc[:, 12 + 3 * l:13 + 3 * l]
                link(dve.tensor_scalar(dd[:, 2 * q:3 * q], dd[:, 2 * q:3 * q], gd, None, ALU.mult))
                for r, g, op in ((0, gh, ALU.add), (1, ngh, ALU.add)):
                    dve.scalar_tensor_tensor(out=lo4[:, :, r, :], in0=band(dd[:, 0:q]), scalar=g,
                                             in1=band(app[lvl]), op0=ALU.mult, op1=op)
                for r, op in ((0, ALU.add), (1, ALU.subtract)):
                    ins = dve.scalar_tensor_tensor(out=hi4[:, :, r, :], in0=band(dd[:, q:2 * q]), scalar=gv,
                                                   in1=band(dd[:, 2 * q:3 * q]), op0=ALU.mult, op1=op)
                link(ins)
                to = img if lvl == 1 else app[lvl - 1]
                o2 = to[:, 0:4 * q].rearrange("p (m two) -> p m two", two=2)
                dve.tensor_tensor(o2[:, :, 0], lohi[:, 0:2 * q], lohi[:, 2 * q:4 * q], ALU.add)
                ins = dve.tensor_tensor(o2[:, :, 1], lohi[:, 0:2 * q], lohi[:, 2 * q:4 * q], ALU.subtract)
                if lvl == 1:
                    ins.then_inc(image_ready, 1)
                else:
                    link(ins)

            normalize(dve, link, lambda j: cx[0:B, 0, :], lambda j: cx[0:B, 1, :], B, 1, c_var, c_root, 1
                      ).then_inc(c_norm, 1)
            dve.wait_ge(c_norm, 1)
            dve.wait_ge(c_ps, 1)
            dve.tensor_copy(c_xT, psT[:, 0:KD]).then_inc(c_done, 1)
            dve.wait_ge(c_ps, 2)
            dve.tensor_copy(c_qT, psT[:, 4:4 + KD])
            dve.tensor_copy(c_kT, psT[:, 6:6 + KD]).then_inc(c_done, 1)
            link(dve.memset(c_va[0:1, :, :], 1.0))
            dve.tensor_copy(c_va[0:1, :, 0:HD], psL[0][0:1, 0:D].rearrange("p (h d) -> p h d", h=HEADS))
            dve.wait_ge(c_ps, 3)
            for i in range(2):
                dve.tensor_scalar(c_kl[0:1, 512 * i:512 * i + 512], psF[i][0:1, :], 0.0, None, ALU.max)
                dve.tensor_scalar(c_kf[0:1, 512 * i:512 * i + 512], psF[i][0:1, :], 0.0, None, ALU.min)
            dve.tensor_scalar(c_ql, psL[1][:, 0:PAIRS], 0.0, None, ALU.max)
            dve.tensor_scalar(c_qf, psL[1][:, 0:PAIRS], 0.0, None, ALU.min).then_inc(c_done, 1)
            dve.wait_ge(c_done, 3)
            dve.wait_ge(act_step, 1)
            dve.tensor_tensor(c_qf, c_qf, c_ql, ALU.add)
            dve.tensor_tensor(c_kf[0:1, :], c_kf[0:1, :], c_kl[0:1, :], ALU.add).then_inc(c_done, 1)
            dve.tensor_tensor(cx[0:B, 1, :], cx[0:B, 1, :], bout_bc[0:B, :], ALU.add)
            for i in range(2):
                dve.memset(va[i][:, :, :, HD:VA], 1.0)
                ins = dve.memset(kvbd[i][:, :, :], 0.0)
            link(ins)

            dve.wait_ge(relaid, 16 * B * T)

            def norm_tokens(g, par):
                after(dve, xT_ps, g - 1)
                after(dve, xnb_ready, g - 1)
                normalize(dve, link, lambda j: h[:, bass.ds(T * g + j, 1), :].rearrange("p o n -> p (o n)"),
                          lambda j: xn[par][:, j, :], P, T, t_var, t_root, g + 1).then_inc(ln_ready, 1)

            def v_rows(g, par):
                dve.wait_ge(v_ps, g + 1)
                after(dve, kv_ps, g - 1)
                dve.tensor_copy(va[par][:, :, :, 0:HD],
                                psL[1][:, :].rearrange("p (t h d) -> p t h d", t=T, h=HEADS)).then_inc(v_sb, 1)

            def x1_rows(g, par):
                dve.wait_ge(out_ps, g + 1)
                dve.wait_ge(xnb_ready, g + 1)
                dve.tensor_tensor(x1[:, bass.ds(T * g, T), :], psL[0][:, :].rearrange("p (t n) -> p t n", t=T),
                                  xnb[par][:, :, :], ALU.add).then_inc(x1_ready, 1)

            norm_tokens(0, 0)
            norm_tokens(1, 1)
            v_rows(0, 0)

            def attention_step(g, par):
                peeled = isinstance(g, int)
                after(dve, kv_ps, g - 1)
                after(dve, attn_ps, (T + 1) * (g - 1))
                for i in range(8):
                    dve.wait_ge(f_ps, 8 * g + i + 1)
                    dve.tensor_scalar(feature_rows(par, i), psF[i % 2][:, :], 0.0, None, ALU.min
                                      ).then_inc(f_neg, 1)
                if not peeled or g >= 1:
                    x1_rows(g - 1, 1 - par)
                dve.wait_ge(kv_ps, g + 1)
                kvv = psKV[:, 0:PAIRS * PW].rearrange("p (m n) -> p m n", m=PAIRS)
                dve.tensor_copy(kvbd[par][0:64, :, 0:VA], kvv[0:64, :, 0:VA])
                dve.tensor_copy(kvbd[par][64:P, :, VA:PW], kvv[64:P, :, VA:PW]).then_inc(kvbd_ready, 1)
                if not peeled or g + 1 < B:
                    v_rows(g + 1, 1 - par)
                after(dve, attT_ps, g - 1)
                for j in range(T + 1):
                    dve.wait_ge(attn_ps, (T + 1) * g + j + 1)
                    n = P if j < T else 1
                    src = (psAT[j] if j < T else psKV)[0:n, 0:PAIRS * PW].rearrange("p (h d) -> p h d", h=HEADS)
                    d3 = den[0:n, j, :].rearrange("p (h o) -> p h o", o=1)
                    link(dve.tensor_scalar(d3, src[:, :, HD:VA], EPS_ATTN, None, ALU.add))
                    link(dve.reciprocal(den[0:n, j, :], den[0:n, j, :]))
                    dst = (att[par][:, j, :] if j < T else
                           catt[0:1, bass.ds(g, 1), :].rearrange("p o n -> p (o n)"))
                    dve.tensor_tensor(dst.rearrange("p (h d) -> p h d", h=HEADS), src[:, :, 0:HD],
                                      d3.to_broadcast([n, HEADS, HD]), ALU.mult).then_inc(att_ready, 1)
                if not peeled or g + 2 < B:
                    norm_tokens(g + 2, par)

            attention_step(0, 0)

            def turn(it):
                attention_step(2 * it + 1, 1)
                attention_step(2 * it + 2, 0)
            chain.loop((B - 4) // 2, 14, turn)
            for g in range(B - 3, B):
                attention_step(g, g % 2)
            x1_rows(B - 1, 1)
            dve.wait_ge(c_out_ps, 1)
            dve.tensor_tensor(cx[0:B, 1, :], psL[1][0:B, 0:D], cx[0:B, 1, :], ALU.add).then_inc(c_x1, 1)
            dve.wait_ge(c_x1, 1)
            dve.wait_ge(x1_ready, B)

            def norm_x1(g, par):
                tail = isinstance(g, int) and g == B
                after(dve, x1T_ps, g - 1)
                after(dve, x1b_ready, g - 1)
                src = ((lambda j: cx[0:B, 1, :]) if tail else
                       (lambda j: x1[:, bass.ds(T * g + j, 1), :].rearrange("p o n -> p (o n)")))
                n, tiles = (B, 1) if tail else (P, T)
                normalize(dve, link, src, lambda j: xh[par][0:n, j, :], n, tiles, x_var, x_root, g + 1
                          ).then_inc(xh_ready, 1)

            def choose(g, par):
                tail = isinstance(g, int) and g == B
                n, tiles = (B, 1) if tail else (P, T)
                dve.wait_ge(lg_ps, g + 1)
                link(dve.tensor_tensor(lg[0:n, 0:tiles, :], psLG[0:n, 0:tiles * E].rearrange("p (t e) -> p t e", e=E),
                                       rb2_bc[0:n, :].rearrange("p (o e) -> p o e", o=1).to_broadcast([n, tiles, E]),
                                       ALU.add))
                apart(dve, dve_passed)
                for j in range(tiles):
                    ins = dve.max(top[0:n, j, :], lg[0:n, j, :])
                link(ins)
                dve.tensor_tensor(gap[0:n, 0:tiles, :], top[0:n, 0:tiles, 0:1], top[0:n, 0:tiles, 1:2],
                                  ALU.subtract).then_inc(lg_gap, 1)
                for j in range(tiles):
                    ins = dve.max_index(topi[0:n, j, :], top[0:n, j, :], lg[0:n, j, :])
                link(ins)
                link(dve.tensor_copy(topf[0:n, 0:tiles, :], topi[0:n, 0:tiles, 0:2]))
                after(dve, rk_ps, g)
                if tail:
                    dve.memset(mask[:, :, :], 0.0)
                for k in range(2):
                    for j in range(tiles):
                        ins = dve.tensor_scalar(onehot[0:n, k, j, :], iota8[0:n, :], topf[0:n, j, k:k + 1], None,
                                                ALU.is_equal)
                link(ins)
                dve.tensor_tensor(mask[0:n, 0:tiles, :], onehot[0:n, 0, 0:tiles, :], onehot[0:n, 1, 0:tiles, :],
                                  ALU.add).then_inc(mask_ready, 1)
                dve.wait_ge(lg_half, g + 1)
                dve.tensor_scalar(probs[0:n, 0, 0:tiles, :], half[0:n, 0:tiles, :], 0.5, 0.5, ALU.mult, ALU.add)
                link(dve.tensor_scalar(probs[0:n, 1, 0:tiles, :], half[0:n, 0:tiles, :], -0.5, 0.5, ALU.mult, ALU.add))
                for k in range(2):
                    ins = dve.tensor_tensor(weighed[0:n, k, 0:tiles, :], onehot[0:n, k, 0:tiles, :],
                                            probs[0:n, k, 0:tiles, :].to_broadcast([n, tiles, E]), ALU.mult)
                link(ins)
                dve.tensor_tensor(pay[par][0:n, 0:tiles, D + 1:PAY], weighed[0:n, 0, 0:tiles, :],
                                  weighed[0:n, 1, 0:tiles, :], ALU.add)
                if tail:
                    dve.tensor_scalar(pay[par][0:n, 0, D:D + 1], ids[0:n, 0, :], float(-B * SEQ - 1), float(SEQ),
                                      ALU.add, ALU.mult)
                else:
                    dve.tensor_copy(pay[par][:, :, D:D + 1], ids[:, :, :])
                    link(dve.tensor_scalar(ids[:, :, :], ids[:, :, :], float(SEQ), None, ALU.add))

            def settle(g, par):
                tail = isinstance(g, int) and g == B
                n, tiles = (B, 1) if tail else (P, T)
                dve.wait_ge(rk_ps, g + 1)
                rk = psRK[:, 0:(T + 1) * E].rearrange("p (t e) -> p t e", e=E)
                link(dve.tensor_tensor(rank[0:n, 0:tiles, :], rk[0:n, 0:tiles, :],
                                       used[0:n, :].rearrange("p (o e) -> p o e", o=1).to_broadcast([n, tiles, E]),
                                       ALU.add))
                dve.tensor_tensor(used, used, rk[:, T, :], ALU.add)
                for k in range(2):
                    ins = dve.tensor_tensor(placed[0:n, k, 0:tiles, :], onehot[0:n, k, 0:tiles, :],
                                            rank[0:n, 0:tiles, :], ALU.mult)
                link(ins)
                for k in range(2):
                    ins = dve.tensor_reduce(placef[0:n, k, 0:tiles, :], placed[0:n, k, 0:tiles, :], AX_X, ALU.add)
                link(ins)
                dst = c_place[0:n, :].rearrange("p (k o) -> p k o", o=1) if tail else place[par][:, :, :]
                dve.tensor_copy(dst, placef[0:n, :, 0:tiles, 0]).then_inc(place_ready, 1)

            def finish_rows(g, par):
                tail = isinstance(g, int) and g == B
                n, tiles = (B, 1) if tail else (P, T)

                def hrow(j):
                    return cx[0:B, 0, :] if tail else h[:, bass.ds(T * g + j, 1), :].rearrange("p o n -> p (o n)")
                dve.wait_ge(x1b_ready, g + 1)
                for j in range(tiles):
                    dve.wait_ge(mlp_ps, T * g + j + 1)
                    ins = dve.tensor_tensor(x2[par][0:n, j, :], psO[j][0:n, 0:D], x1b[par][0:n, j, :], ALU.add)
                link(ins)
                link(normalize(dve, link, lambda j: x2[par][0:n, j, :], lambda j: x2[par][0:n, j, :], n, tiles,
                               m_var, m_root, 2 * g + 1))
                for j in range(tiles):
                    ins = dve.tensor_tensor(x2[par][0:n, j, :], x2[par][0:n, j, :], gamma_bc[0:n, :], ALU.mult)
                link(ins)
                for j in range(tiles):
                    ins = dve.tensor_tensor(hrow(j), hrow(j), x2[par][0:n, j, :], ALU.add)
                ins.then_inc(h1_ready, 1)
                dve.wait_ge(h1_ready, g + 1)
                done = scat0 if par == 0 else scat1
                if isinstance(g, int):
                    after(dve, done, 32 * T * (g // 2))
                else:
                    dve.wait_ge(done, (g - par) * (16 * T))
                after(dve, xmT_ps, g - 1)
                normalize(dve, link, hrow, lambda j: pay[par][0:n, j, 0:D], n, tiles, m_var, m_root, 2 * g + 2
                          ).then_inc(xm_ready, 1)

            norm_x1(0, 0)
            norm_x1(1, 1)

            def routing_step(g, par):
                peeled = isinstance(g, int)
                if not peeled or g >= 1:
                    choose(g - 1, 1 - par)
                    settle(g - 1, 1 - par)
                if not peeled or g <= B:
                    finish_rows(g, par)
                if not peeled or g + 2 <= B:
                    norm_x1(g + 2, par)
            routing_step(0, 0)

            def turn(it):
                routing_step(2 * it + 1, 1)
                routing_step(2 * it + 2, 0)
            chain.loop(2, 2 * ROUTING_LINKS, turn)
            for g in range(5, B + 2):
                routing_step(g, g % 2)

            dve.tensor_copy(used_i[:, :], used)
            dve.tensor_tensor(count, used, region0[:, 0:E], ALU.subtract).then_inc(used_ready, 1)
            dve.wait_ge(used_ready, 1)
            link(dve.tensor_tensor(over[:, :, :], count.rearrange("p (e o) -> p e o", o=1).to_broadcast([P, E, 18]),
                                   limits.rearrange("p (o j) -> p o j", o=1).to_broadcast([P, E, 18]), ALU.is_gt))
            link(dve.tensor_reduce(tiles_e, over[:, :, :], AX_X, ALU.add))
            link(dve.tensor_tensor(lower[:, :, :], first_src[:, :, :],
                                   tiles_e.rearrange("p (o e) -> p o e", o=1).to_broadcast([P, E + 1, E]), ALU.mult))
            link(dve.tensor_reduce(first, lower[:, :, :], AX_X, ALU.add))
            link(dve.scalar_tensor_tensor(out=jump, in0=first, scalar=float(-P), in1=region0, op0=ALU.mult,
                                          op1=ALU.add))
            dve.memset(owner, 0.0)
            link(dve.tensor_scalar(rowt, tnum, float(P), None, ALU.mult))
            for e in range(1, E + 1):
                link(dve.tensor_scalar(step, tnum, first[:, e:e + 1], None, ALU.is_ge))
                if e < E:
                    dve.tensor_tensor(owner, owner, step, ALU.add)
                link(dve.tensor_tensor(lower[:, 0, 0:1], jump[:, e:e + 1], jump[:, e - 1:e], ALU.subtract))
                link(dve.scalar_tensor_tensor(out=rowt, in0=step, scalar=lower[:, 0, 0:1], in1=rowt, op0=ALU.mult,
                                              op1=ALU.add))
            link(dve.tensor_scalar(rowt, rowt, float(E * REGION), None, ALU.min))
            dve.tensor_copy(owner_i[:, :], owner)
            dve.tensor_copy(row_i[:, :], rowt).then_inc(tables_ready, 1)
            dve.wait_ge(tables_ready, 1)

            dve.wait_ge(b2_loaded, 16)
            loaded = [xs_loaded0, xs_loaded1]

            def tile_in(i, par, turns):
                e = dve.value_load(owner_i[0:1, bass.ds(i, 1)], min_val=0, max_val=E - 1)
                after(dve, hT_sb, KH * (i - 1))
                dve.tensor_copy(b1now[par].rearrange("p (o k) -> p o k", o=1),
                                eb1T[:, bass.ds(e, 1), :]).then_inc(b1_ready, 1)
                dve.wait_ge(loaded[par], 16 * turns)
                after(dve, rows_added, 16 * (i - 1))
                dve.tensor_copy(gate_now[par], xs[par][:, bass.ds(e + (D + 1), 1)])
                dve.tensor_copy(slot_ids[par][:, :], xs[par][:, D:D + 1]).then_inc(slot_ready, 1)
                after(dve, hT_ps, i - 1)
                for c in range(2):
                    dve.wait_ge(h_ps, 2 * i + c + 1)
                    dve.tensor_copy(hraw[par][:, 512 * c:512 * c + 512], psF[c][:, :]).then_inc(hraw_ready, 1)

            def tile_out(i, par):
                e = dve.value_load(owner_i[0:1, bass.ds(i, 1)], min_val=0, max_val=E - 1)
                dve.wait_ge(y_ps, i + 1)
                link(dve.tensor_tensor(ybias[par].rearrange("p (o n) -> p o n", o=1),
                                       psAT[par][:, 0:D].rearrange("p (o n) -> p o n", o=1),
                                       b2bc[:, bass.ds(e, 1), :], ALU.add))
                dve.tensor_scalar(y[par], ybias[par], gate_now[par], None, ALU.mult).then_inc(y_ready, 1)

            tile_in(0, 0, 1)

            def turn(it):
                tile_in(2 * it + 1, 1, it + 1)
                tile_out(2 * it, 0)
                tile_in(2 * it + 2, 0, it + 2)
                tile_out(2 * it + 1, 1)
            chain.loop(MOE_TILES // 2 - 1, 2, turn)
            tile_in(MOE_TILES - 1, 1, MOE_TILES // 2)
            tile_out(MOE_TILES - 2, 0)
            tile_out(MOE_TILES - 1, 1)

        @block.scalar
        def _(act):
            for dst, src in smalls:
                act.dma_start(dst, src).then_inc(smalls_loaded, 16)
            for dst, src in raws:
                act.dma_start(dst, src).then_inc(raw_loaded, 16)
            act.dma_start(rw1, t["L0_ffn_rw1"].rearrange("(k p) n -> p k n", p=P)).then_inc(direct_loaded, 16)
            act.dma_start(rw2, t["L0_ffn_rw2"].rearrange("(k p) n -> p k n", p=P)).then_inc(direct_loaded, 16)
            act.wait_ge(iota_ready, 1)
            for hh in range(HEADS):
                p0, c0 = HD * (hh % 8), FEAT * (hh % 8)
                act.dma_start(projbd[p0:p0 + HD, hh // 8, c0:c0 + FEAT],
                              t["L0_attn_proj"][hh]).then_inc(direct_loaded, 16)

            for u, (dst, blocks) in enumerate(turned):
                act.wait_ge(wT_ps, u + 1)
                src = psF[u % 2][:, :]
                if len(dst.shape) == 3:
                    src = src.rearrange("p (a n) -> p a n", a=dst.shape[1])
                act.copy(dst, src).then_inc(wT_sb, 1)
            act.wait_ge(wT_ps, len(turned) + 1)
            act.copy(cols, psF[len(turned) % 2][:, 0:84]).then_inc(wT_sb, 1)

            act.wait_ge(logits_ready, 1)
            act.activation(gate[:, 0:1], gate[:, 0:1], ACT.Exp, scale=-1.0)
            act.activation(gate[:, 1:10], gate[:, 1:10], ACT.Exp).then_inc(exps_ready, 1)

            act.wait_ge(c_done, 3)
            act.activation(c_kf[0:1, :], c_kf[0:1, :], ACT.Exp)
            act.activation(c_qf, c_qf, ACT.Exp).then_inc(act_step, 1)

            def tokens_T(g, par):
                act.wait_ge(xT_ps, g + 1)
                after(act, v_ps, g - 1)
                act.copy(xnT[par][:, :, :], psT[:, :].rearrange("p (k n) -> p k n", k=KD)).then_inc(xT_sb, 1)

            def qk_T(g, par):
                act.wait_ge(q_ps, g + 1)
                after(act, f_ps, 8 * (g - 1))
                act.copy(qT[par][:, :, :], psL[1][:, :].rearrange("p (k n) -> p k n", k=KD)).then_inc(q_sb, 1)
                act.wait_ge(k_ps, g + 1)
                act.copy(kT[par][:, :, :], psL[0][:, :].rearrange("p (k n) -> p k n", k=KD)).then_inc(k_sb, 1)

            def att_T(g, par):
                act.wait_ge(attT_ps, g + 1)
                act.copy(attT[par][:, :, :], psT[:, :].rearrange("p (k n) -> p k n", k=KD)).then_inc(attT_sb, 1)

            tokens_T(0, 0)
            qk_T(0, 0)

            def attention_step(g, par):
                peeled = isinstance(g, int)

                def bank_out(i):
                    u = 8 * g + i
                    act.wait_ge(f_neg, u + 1)
                    after(act, f_sum, u - 3)
                    act.activation(lin[i % 4], psF[i % 2][:, :], ACT.Relu).then_inc(f_read, 1)
                    act.activation(feature_rows(par, i), feature_rows(par, i), ACT.Exp).then_inc(f_exp, 1)
                for i in range(4):
                    bank_out(i)
                if not peeled or g >= 1:
                    att_T(g - 1, 1 - par)
                if not peeled or g + 1 < B:
                    tokens_T(g + 1, 1 - par)
                for i in range(4, 8):
                    bank_out(i)
                if not peeled or g + 1 < B:
                    qk_T(g + 1, 1 - par)

            attention_step(0, 0)
            with act.Fori(0, (B - 2) // 2) as it:
                attention_step(2 * it + 1, 1)
                attention_step(2 * it + 2, 0)
            attention_step(B - 1, 1)
            att_T(B - 1, 1)
            act.wait_ge(cattT_ps, 1)
            act.copy(c_attT[:, :, :], psT[:, 0:KD * B].rearrange("p (k n) -> p k n", k=KD)).then_inc(cattT_sb, 1)
            act.wait_ge(c_x1, 1)
            act.wait_ge(x1_ready, B)

            def x1_T(g, par):
                tail = isinstance(g, int) and g == B
                n = B if tail else IMG
                act.wait_ge(x1T_ps, g + 1)
                for k in range(KD):
                    ins = act.activation(x1T[par][:, k, 0:n], psT[:, k * IMG:k * IMG + n], ACT.Identity,
                                         bias=betaT[:, k:k + 1], scale=gammaT[:, k:k + 1])
                ins.then_inc(x1T_sb, 1)

            def xm_T(g, par):
                tail = isinstance(g, int) and g == B
                n = B if tail else IMG
                act.wait_ge(xmT_ps, g + 1)
                act.copy(xmT[par][:, :, 0:n], psT[:, :].rearrange("p (k n) -> p k n", k=KD)[:, :, 0:n]
                         ).then_inc(xmT_sb, 1)

            def hidden(g, first_use, func, bias, dst, n):
                for i in range(4):
                    act.wait_ge(m_ps, first_use + i + 1)
                    for m in range(2):
                        ins = act.activation(dst[:, 2 * i + m, 0:n], psF[i % 2][:, m * IMG:m * IMG + n], func,
                                             bias=bias[:, 2 * i + m:2 * i + m + 1])
                    ins.then_inc(m_sb, 1)

            x1_T(0, 0)

            def routing_step(g, par):
                peeled = isinstance(g, int)
                if not peeled or g <= B:
                    n = B if peeled and g == B else IMG
                    after(act, mlp_ps, T * (g - 1))
                    hidden(g, 8 * g - 4 if not peeled or g else 0, ACT.Gelu, b1T, gT[par], n)
                if not peeled or g >= 1:
                    xm_T(g - 1, 1 - par)
                if not peeled or g + 1 <= B:
                    x1_T(g + 1, 1 - par)
                if not peeled or g >= 1:
                    n = B if peeled and g - 1 == B else IMG
                    after(act, lg_ps, g - 2 if peeled else g - 2)
                    hidden(g - 1, 8 * g if not peeled or g <= B else 8 * g - 4, ACT.Silu, rb1T, rT[1 - par], n)
                    tiles, rows = (1, B) if peeled and g - 1 == B else (T, P)
                    act.wait_ge(lg_gap, g)
                    act.activation(half[0:rows, 0:tiles, :], gap[0:rows, 0:tiles, :], ACT.Tanh, scale=0.5
                                   ).then_inc(lg_half, 1)
            routing_step(0, 0)
            routing_step(1, 1)
            routing_step(2, 0)
            with act.Fori(0, 2) as it:
                routing_step(2 * it + 3, 1)
                routing_step(2 * it + 4, 0)
            for g in range(7, B + 2):
                routing_step(g, g % 2)

            def rows_T(i, par):
                act.wait_ge(xsT_ps, i + 1)
                after(act, h_ps, 2 * (i - 1))
                act.copy(xsT[par], psT[:, 0:D]).then_inc(xsT_sb, 1)

            def tile_step(i, par):
                act.wait_ge(b1_ready, i + 1)
                act.wait_ge(hT_ps, i + 1)
                after(act, y_ps, i - 1)
                for k in range(KH):
                    act.activation(hT[par][:, k, :], psH2[k // 4][:, P * (k % 4):P * (k % 4) + P], ACT.Silu,
                                   bias=b1now[par][:, k:k + 1]).then_inc(hT_sb, 1)
            rows_T(0, 0)

            def full(i, par):
                rows_T(i + 1, 1 - par)
                tile_step(i, par)
            full(0, 0)
            with act.Fori(0, MOE_TILES // 2 - 1) as it:
                full(2 * it + 1, 1)
                full(2 * it + 2, 0)
            tile_step(MOE_TILES - 1, 1)

        @block.tensor
        def _(pe):
            def mm(out, lhsT, rhs, start=True, stop=True, **kw):
                return pe.matmul(out, lhsT, rhs, start=start, stop=stop, **kw)

            pe.wait_ge(consts_ready, 1)
            pe.wait_ge(raw_loaded, 16 * len(raws))
            for u, (_, blocks) in enumerate(turned):
                after(pe, wT_sb, u - 1)
                for i, src in enumerate(blocks):
                    ins = pe.transpose(psF[u % 2][:, P * i:P * i + P], src, ident)
                ins.then_inc(wT_ps, 1)
            pe.wait_ge(wT_sb, len(turned) - 1)
            pe.transpose(psF[len(turned) % 2][:, 0:84], raw_cols[0:84, :], ident[0:84, 0:84]).then_inc(wT_ps, 1)

            pe.wait_ge(dots_ready, 1)
            mm(psT[:, 0:10], same, dots).then_inc(totals_ready, 1)

            pe.wait_ge(c_norm, 1)
            for k in range(KD):
                ins = pe.transpose(psT[:, k:k + 1], cx[0:1, 1, k * P:k * P + P], ident[0:1, 0:1])
            ins.then_inc(c_ps, 1)
            pe.wait_ge(c_done, 1)
            pe.wait_ge(wT_sb, len(turned) + 1)
            for i in range(4):
                for k in range(KD):
                    mm(psT[:, 4 + i:5 + i], wqkvT[:, k, P * i:P * i + P], c_xT[:, k:k + 1], k == 0, k == KD - 1)
            for k in range(KD):
                ins = mm(psL[0][0:1, 0:D], c_xT[:, k:k + 1], wqkvT[:, k, 2 * D:3 * D], k == 0, k == KD - 1)
            ins.then_inc(c_ps, 1)
            pe.wait_ge(c_done, 2)
            pe.wait_ge(direct_loaded, 16 * (2 + HEADS))
            for c in range(2):
                mm(psF[c][0:1, :], c_kT[:, c:c + 1], projbd[:, c, :])
            for m in range(PAIRS):
                ins = mm(psL[1][:, m:m + 1], projbd[:, m // 4, P * (m % 4):P * (m % 4) + P], c_qT[:, m // 4:m // 4 + 1])
            ins.then_inc(c_ps, 1)

            def tokens_T(g, par):
                pe.wait_ge(ln_ready, g + 1)
                after(pe, attT_sb, g - 1)
                for j in range(T):
                    for k in range(KD):
                        ins = pe.transpose(psT[:, k * IMG + j * P:k * IMG + j * P + P],
                                           xn[par][:, j, k * P:k * P + P], ident)
                ins.then_inc(xT_ps, 1)

            def qkv(g, par):
                pe.wait_ge(xT_sb, g + 1)
                after(pe, v_sb, g)
                for half_, dst, done in ((0, psL[1], q_ps), (1, psL[0], k_ps)):
                    if half_:
                        after(pe, x1_ready, g - 1)
                    for m in range(KD):
                        c0 = D * half_ + P * m
                        for k in range(KD):
                            ins = mm(dst[:, m * IMG:(m + 1) * IMG], wqkvT[:, k, c0:c0 + P], xnT[par][:, k, :],
                                     k == 0, k == KD - 1)
                    ins.then_inc(done, 1)
                pe.wait_ge(q_sb, g + 1)
                for j in range(T):
                    for k in range(KD):
                        ins = mm(psL[1][:, j * D:(j + 1) * D], xnT[par][:, k, j * P:j * P + P],
                                 wqkvT[:, k, 2 * D:3 * D], k == 0, k == KD - 1)
                ins.then_inc(v_ps, 1)

            def features(g, par, i):
                u = 8 * g + i
                after(pe, f_read, u - 1)
                if i < 4:
                    ins = mm(psF[i % 2][:, :], kT[par][:, i % 2, (i // 2) * P:(i // 2) * P + P], projbd[:, i % 2, :])
                else:
                    for m in range(2):
                        pair = 2 * (i - 4) + m
                        c0 = P * (pair % 4)
                        ins = mm(psF[i % 2][:, m * IMG:(m + 1) * IMG], projbd[:, pair // 4, c0:c0 + P],
                                 qT[par][:, pair // 4, :])
                ins.then_inc(f_ps, 1)

            def att_T(g, par):
                pe.wait_ge(att_ready, (T + 1) * g + T)
                pe.wait_ge(xT_sb, g + 2 if not isinstance(g, int) or g + 2 <= B else B)
                for j in range(T):
                    for k in range(KD):
                        ins = pe.transpose(psT[:, k * IMG + j * P:k * IMG + j * P + P],
                                           att[par][:, j, k * P:k * P + P], ident)
                ins.then_inc(attT_ps, 1)

            def out_rows(g, par):
                pe.wait_ge(attT_sb, g + 1)
                pe.wait_ge(k_sb, g + 2 if not isinstance(g, int) or g + 2 <= B else B)
                for j in range(T):
                    for k in range(KD):
                        ins = mm(psL[0][:, j * D:(j + 1) * D], attT[par][:, k, j * P:j * P + P], woT[:, k, :],
                                 k == 0, k == KD - 1)
                ins.then_inc(out_ps, 1)

            def key_values(g, par):
                pe.wait_ge(f_sum, 8 * g + 4)
                pe.wait_ge(v_sb, g + 1)
                after(pe, att_ready, (T + 1) * g)
                for m in range(PAIRS):
                    c0 = P * (m % 4)
                    o = psKV[:, m * PW:(m + 1) * PW]
                    for j in range(T):
                        mm(o, kf[par][:, j, m // 4, c0:c0 + P],
                           va[par][:, j, 2 * m:2 * m + 2, :].rearrange("p h d -> p (h d)"),
                           m == 0 and j == 0, False, skip_group_check=True)
                    ins = mm(o, c_kf[0:1, m * P:m * P + P],
                             c_va[0:1, 2 * m:2 * m + 2, :].rearrange("p h d -> p (h d)"), False, m == PAIRS - 1,
                             skip_group_check=True)
                ins.then_inc(kv_ps, 1)

            def attend(g, par):
                pe.wait_ge(f_sum, 8 * g + 8)
                pe.wait_ge(kvbd_ready, g + 1)
                for j in range(T + 1):
                    for m in range(PAIRS):
                        if j < T:
                            o, lhsT = psAT[j][:, m * PW:(m + 1) * PW], qf[par][:, m, j * P:j * P + P]
                        else:
                            o, lhsT = psKV[0:1, m * PW:(m + 1) * PW], c_qf[:, m:m + 1]
                        ins = mm(o, lhsT, kvbd[par][:, m, :])
                    ins.then_inc(attn_ps, 1)

            tokens_T(0, 0)
            pe.wait_ge(c_done, 4)
            qkv(0, 0)

            def attention_step(g, par):
                peeled = isinstance(g, int)
                for i in range(4):
                    if i == 0:
                        pe.wait_ge(k_sb, g + 1)
                    features(g, par, i)
                if not peeled or g >= 1:
                    att_T(g - 1, 1 - par)
                if not peeled or g + 1 < B:
                    tokens_T(g + 1, 1 - par)
                for i in range(4, 8):
                    features(g, par, i)
                if not peeled or g >= 1:
                    out_rows(g - 1, 1 - par)
                key_values(g, par)
                if not peeled or g + 1 < B:
                    qkv(g + 1, 1 - par)
                attend(g, par)

            attention_step(0, 0)
            with pe.Fori(0, (B - 2) // 2) as it:
                attention_step(2 * it + 1, 1)
                attention_step(2 * it + 2, 0)
            attention_step(B - 1, 1)
            att_T(B - 1, 1)
            out_rows(B - 1, 1)
            pe.wait_ge(catt_moved, 16)
            for k in range(KD):
                ins = pe.transpose(psT[:, k * B:(k + 1) * B], cx[0:B, 2, k * P:k * P + P], ident[0:B, 0:B])
            ins.then_inc(cattT_ps, 1)
            pe.wait_ge(cattT_sb, 1)
            for k in range(KD):
                ins = mm(psL[1][0:B, 0:D], c_attT[:, k, :], woT[:, k, :], k == 0, k == KD - 1)
            ins.then_inc(c_out_ps, 1)

            def x1_T(g, par):
                tail = isinstance(g, int) and g == B
                n, tiles = (B, 1) if tail else (P, T)
                pe.wait_ge(xh_ready, g + 1)
                after(pe, xmT_sb, g - 1)
                after(pe, x1T_sb, g)
                for j in range(tiles):
                    for k in range(KD):
                        ins = pe.transpose(psT[:, k * IMG + j * P:k * IMG + j * P + n],
                                           xh[par][0:n, j, k * P:k * P + P], ident[0:n, 0:n])
                ins.then_inc(x1T_ps, 1)

            def xm_T(g, par):
                tail = isinstance(g, int) and g == B
                n, tiles = (B, 1) if tail else (P, T)
                pe.wait_ge(xm_ready, g + 1)
                after(pe, x1T_sb, g + 2 if not isinstance(g, int) or g + 2 <= B else B + 1)
                for j in range(tiles):
                    for k in range(KD):
                        ins = pe.transpose(psT[:, k * IMG + j * P:k * IMG + j * P + n],
                                           pay[par][0:n, j, k * P:k * P + P], ident[0:n, 0:n])
                ins.then_inc(xmT_ps, 1)

            def hidden(first_use, w, src, n):
                for i in range(4):
                    after(pe, m_sb, first_use + i - 1)
                    for m in range(2):
                        c0 = P * (2 * i + m)
                        for k in range(KD):
                            ins = mm(psF[i % 2][:, m * IMG:m * IMG + n], w[:, k, c0:c0 + P], src[:, k, 0:n],
                                     k == 0, k == KD - 1)
                    ins.then_inc(m_ps, 1)

            def mlp_out(g, par, j, first_use):
                tail = isinstance(g, int) and g == B
                n = B if tail else P
                if j == 0:
                    pe.wait_ge(m_sb, first_use + 4)
                    after(pe, h1_ready, g)
                for k in range(KH):
                    ins = mm(psO[j][0:n, 0:D], gT[par][:, k, j * P:j * P + n], w2T[:, k, :], k == 0, k == KH - 1)
                ins.then_inc(mlp_ps, 1)

            def router_out(g, par, first_use):
                tail = isinstance(g, int) and g == B
                n, tiles = (B, 1) if tail else (P, T)
                pe.wait_ge(m_sb, first_use + 4)
                after(pe, lg_gap, g)
                for j in range(tiles):
                    for k in range(KH):
                        ins = mm(psLG[0:n, j * E:(j + 1) * E], rT[par][:, k, j * P:j * P + n], rw2[:, k, :],
                                 k == 0, k == KH - 1)
                ins.then_inc(lg_ps, 1)

            def ranks(g):
                pe.wait_ge(mask_ready, g + 1)
                after(pe, place_ready, g)
                mm(psRK[:, 0:E], before, mask[:, 0, :])
                mm(psRK[:, E:2 * E], before, mask[:, 1, :], True, False)
                mm(psRK[:, E:2 * E], ones, mask[:, 0, :], False, True)
                mm(psRK[:, 2 * E:3 * E], ones, mask[:, 0, :], True, False)
                mm(psRK[:, 2 * E:3 * E], ones, mask[:, 1, :], False, True).then_inc(rk_ps, 1)

            pe.wait_ge(c_x1, 1)
            x1_T(0, 0)

            def routing_step(g, par):
                peeled = isinstance(g, int)
                mlp, router = not peeled or g <= B, not peeled or g >= 1
                mlp_use = 8 * g - 4 if not peeled or g else 0
                router_use = 8 * g if not peeled or g <= B else 8 * g - 4
                if mlp:
                    pe.wait_ge(x1T_sb, g + 1)
                    hidden(mlp_use, w1T, x1T[par], B if peeled and g == B else IMG)
                if router:
                    xm_T(g - 1, 1 - par)
                if not peeled or g + 1 <= B:
                    x1_T(g + 1, 1 - par)
                if router:
                    pe.wait_ge(xmT_sb, g)
                    hidden(router_use, rw1, xmT[1 - par], B if peeled and g - 1 == B else IMG)
                if mlp:
                    mlp_out(g, par, 0, mlp_use)
                if router:
                    router_out(g - 1, 1 - par, router_use)
                if mlp and not (peeled and g == B):
                    mlp_out(g, par, 1, mlp_use)
                if router:
                    ranks(g - 1)
            routing_step(0, 0)
            with pe.Fori(0, 3) as it:
                routing_step(2 * it + 1, 1)
                routing_step(2 * it + 2, 0)
            for g in range(7, B + 2):
                routing_step(g, g % 2)

            loaded = [xs_loaded0, xs_loaded1]
            pe.wait_ge(tables_ready, 1)

            def weights(e, c0, n):
                return experts[:, bass.ds(e, 1), c0:c0 + n].rearrange("p o n -> p (o n)")

            def rows_T(i, par, turns):
                pe.wait_ge(loaded[par], 16 * turns)
                after(pe, xsT_sb, i)
                for k in range(KD):
                    ins = pe.transpose(psT[:, k * P:(k + 1) * P], xs[par][:, k * P:k * P + P], ident)
                ins.then_inc(xsT_ps, 1)

            def up(i, par):
                e = pe.value_load(owner_i[0:1, bass.ds(i, 1)], min_val=0, max_val=E - 1)
                pe.wait_ge(xsT_sb, i + 1)
                after(pe, hraw_ready, 2 * i)
                for c in range(2):
                    for k in range(KD):
                        ins = mm(psF[c][:, :], xsT[par][:, k * P:k * P + P], weights(e, k * HID + 512 * c, 512),
                                 k == 0, k == KD - 1)
                    ins.then_inc(h_ps, 1)

            def hidden_T(i, par):
                pe.wait_ge(hraw_ready, 2 * i + 2)
                after(pe, hT_sb, KH * i)
                for k in range(KH):
                    ins = pe.transpose(psH2[k // 4][:, P * (k % 4):P * (k % 4) + P],
                                       hraw[par][:, k * P:k * P + P], ident)
                ins.then_inc(hT_ps, 1)

            def down(i, par):
                e = pe.value_load(owner_i[0:1, bass.ds(i, 1)], min_val=0, max_val=E - 1)
                pe.wait_ge(hT_sb, KH * (i + 1))
                for k in range(KH):
                    ins = mm(psAT[par][:, 0:D], hT[par][:, k, :], weights(e, KD * HID + k * D, D), k == 0, k == KH - 1)
                ins.then_inc(y_ps, 1)

            rows_T(0, 0, 1)
            pe.wait_ge(low_loaded, 16 * E)
            pe.wait_ge(high_loaded, 16 * E)
            up(0, 0)
            rows_T(1, 1, 1)
            hidden_T(0, 0)
            with pe.Fori(0, MOE_TILES // 2 - 1) as it:
                up(2 * it + 1, 1)
                rows_T(2 * it + 2, 0, it + 2)
                down(2 * it, 0)
                hidden_T(2 * it + 1, 1)
                up(2 * it + 2, 0)
                rows_T(2 * it + 3, 1, it + 2)
                down(2 * it + 1, 1)
                hidden_T(2 * it + 2, 0)
            up(MOE_TILES - 1, 1)
            down(MOE_TILES - 2, 0)
            hidden_T(MOE_TILES - 1, 1)
            down(MOE_TILES - 1, 1)


_INS = ["x", "cls_tok", "L0_tok_Wa", "L0_tok_ba", "L0_tok_Wd1", "L0_tok_bd1", "L0_tok_Wd2", "L0_tok_bd2",
        "L0_tok_Wd3", "L0_tok_bd3", "L0_attn_proj", "L0_attn_w_qkv", "L0_attn_w_out", "L0_attn_b_out",
        "L0_attn_gamma", "L0_attn_beta", "L0_attn_w1", "L0_attn_b1", "L0_attn_w2", "L0_attn_b2",
        "L0_ffn_rw1", "L0_ffn_rb1", "L0_ffn_rw2", "L0_ffn_rb2", "L0_ffn_w1", "L0_ffn_b1", "L0_ffn_w2", "L0_ffn_b2"]


def kernel(**inputs):
    import numpy as _np
    import concourse.bacc as _bacc
    from concourse import mybir as _mybir
    from concourse.bass_utils import run_bass_kernel_spmd as _run

    nc = _bacc.Bacc("TRN2", target_bir_lowering=False, num_devices=1)
    arrays, tensors = {}, {}
    for name in _INS:
        a = _np.ascontiguousarray(inputs[name])
        arrays[f"in_{name}"] = a
        tensors[name] = nc.dram_tensor(f"in_{name}", a.shape, _mybir.dt.from_np(a.dtype), kind="ExternalInput").ap()
    tensors["out"] = nc.dram_tensor("out_tokens", (B, SEQ, D), F32, kind="ExternalOutput").ap()
    build(nc, tensors)
    r = _run(nc, [arrays], core_ids=[0])
    return r.results[0]["out_tokens"]
```

```python
from contextlib import ExitStack

import concourse.bass as bass
from concourse import mybir

F32 = mybir.dt.float32
U32 = mybir.dt.uint32
I32 = mybir.dt.int32
ACT = mybir.ActivationFunctionType
ALU = mybir.AluOpType
AX_X = mybir.AxisListType.X

P = 128
B, IMG = 8, 256
D = IMG
SEQ = IMG + 1
HEADS, HD, FEAT = 16, 16, 64
PAIRS = HEADS // 2
HID = 4 * D
E = 8
KD = D // P
KH = HID // P
T = 2
EPS_LN, EPS_ATTN = 1e-5, 1e-8
TOKENS = B * SEQ
STRIPS = P // B
ROWS = IMG // STRIPS
REGION = 18 * P
MOE_TILES = (2 * TOKENS + E * (P - 1)) // P
PAY = D + 1 + E
VA = HD + 1
PW = 2 * VA
EXPERT = KD * HID + KH * D
ROUTING_LINKS = 17


class Chain:

    def __init__(self, eng, sem):
        self.eng, self.sem, self.n, self.base = eng, sem, 0, 0

    def link(self, ins):
        self.n += 1
        ins.then_inc(self.sem, 1)
        self.eng.wait_ge(self.sem, self.base + self.n)

    def loop(self, count, links, body):
        n = self.n
        with self.eng.Fori(0, count) as it:
            self.base = it * links
            body(it)
        assert self.n - n == links, (self.n - n, links)
        self.n, self.base = n + count * links, 0


def apart(eng, passed):
    eng.sem_inc(passed, 1)


def after(eng, sem, value):
    if not isinstance(value, int) or value > 0:
        eng.wait_ge(sem, value)


def build(nc, t):
    xs_d = nc.dram_tensor("routed_rows", (E * REGION + P, PAY), F32, kind="Internal").ap()
    acc_d = nc.dram_tensor("token_sums", (TOKENS + P, D), F32, kind="Internal").ap()

    with ExitStack() as ctx:
        def sb(name, shape, dt=F32):
            return ctx.enter_context(nc.sbuf_tensor(name, shape, dt))

        def sem(name):
            return ctx.enter_context(nc.semaphore(name))

        arena = sb("arena", [P, E * EXPERT])
        dense = sb("dense", [P, 9280])
        h = sb("h", [P, B * T, D])
        x1 = sb("x1", [P, B * T, D])
        small = sb("small", [P, 2124])

        cut_at = [0]

        def cut(tensor, width):
            a = cut_at[0]
            cut_at[0] += width
            assert cut_at[0] <= tensor.shape[1], (cut_at[0], tensor.shape)
            return tensor[:, a:a + width]

        def at(tensor):
            cut_at[0] = tensor

        at(0)
        wqkvT = cut(dense, KD * 3 * D).rearrange("p (k n) -> p k n", k=KD)
        woT = cut(dense, KD * D).rearrange("p (k n) -> p k n", k=KD)
        w1T = cut(dense, KD * HID).rearrange("p (k n) -> p k n", k=KD)
        w2T = cut(dense, KH * D).rearrange("p (k n) -> p k n", k=KH)
        rw1 = cut(dense, KD * HID).rearrange("p (k n) -> p k n", k=KD)
        projbd = cut(dense, KD * 8 * FEAT).rearrange("p (k n) -> p k n", k=KD)
        rw2 = cut(dense, KH * E).rearrange("p (k n) -> p k n", k=KH)

        at(0)
        xs = [cut(dense, PAY) for _ in range(2)]
        xsT = [cut(dense, D) for _ in range(2)]
        w1now = [cut(dense, KD * HID).rearrange("p (k n) -> p k n", k=KD) for _ in range(2)]
        hT = [cut(dense, HID).rearrange("p (k n) -> p k n", k=KH) for _ in range(2)]
        ybias = [cut(dense, D) for _ in range(2)]
        y = [cut(dense, D) for _ in range(2)]

        at(0)
        img = cut(arena, ROWS * IMG)
        lohi = cut(arena, ROWS * IMG)
        det = {1: cut(arena, 3 * 1024)}
        app = {1: cut(arena, 1024)}
        det[2], app[2] = cut(arena, 3 * 256), cut(arena, 256)
        det[3], app[3] = cut(arena, 3 * 64), cut(arena, 64)
        wd = {2: cut(arena, 9 * 256)}
        at(16384)
        wd[1] = cut(arena, 9 * 1024)
        wd[3] = cut(arena, 9 * 64)
        wa = cut(arena, 64)
        raw_qkv = cut(arena, 6 * D).rearrange("p (m n) -> p m n", m=6)
        raw_o = cut(arena, KD * D).rearrange("p (m n) -> p m n", m=KD)
        raw_w1 = cut(arena, KH * D).rearrange("p (m n) -> p m n", m=KH)
        raw_w2 = cut(arena, KD * HID).rearrange("p (m n) -> p m n", m=KD)
        raw_cols = cut(arena, P)

        at(0)
        xn = [cut(arena, T * D).rearrange("p (t n) -> p t n", t=T) for _ in range(2)]
        xnb = [cut(arena, T * D).rearrange("p (t n) -> p t n", t=T) for _ in range(2)]
        xnT = [cut(arena, KD * IMG).rearrange("p (k n) -> p k n", k=KD) for _ in range(2)]
        qT = [cut(arena, KD * IMG).rearrange("p (k n) -> p k n", k=KD) for _ in range(2)]
        kT = [cut(arena, KD * IMG).rearrange("p (k n) -> p k n", k=KD) for _ in range(2)]
        va = [cut(arena, T * HEADS * VA).rearrange("p (t h d) -> p t h d", t=T, h=HEADS) for _ in range(2)]
        kf = [cut(arena, T * HEADS * FEAT).rearrange("p (t c n) -> p t c n", t=T, c=KD) for _ in range(2)]
        qf = [cut(arena, PAIRS * IMG).rearrange("p (m n) -> p m n", m=PAIRS) for _ in range(2)]
        lin = [cut(arena, 512) for _ in range(4)]
        kvbd = [cut(arena, PAIRS * PW).rearrange("p (m n) -> p m n", m=PAIRS) for _ in range(2)]
        att = [cut(arena, T * D).rearrange("p (t n) -> p t n", t=T) for _ in range(2)]
        attT = [cut(arena, KD * IMG).rearrange("p (k n) -> p k n", k=KD) for _ in range(2)]
        catt = cut(arena, B * D).rearrange("p (b n) -> p b n", b=B)
        c_va = cut(arena, HEADS * VA).rearrange("p (h d) -> p h d", h=HEADS)
        c_kf = cut(arena, HEADS * FEAT)
        c_kl = cut(arena, HEADS * FEAT)
        t_mv = [cut(arena, T * 2).rearrange("p (t n) -> p t n", t=T) for _ in range(2)]
        t_rstd = [cut(arena, T).rearrange("p (t n) -> p t n", t=T) for _ in range(2)]

        at(0)
        xh = [cut(dense, T * D).rearrange("p (t n) -> p t n", t=T) for _ in range(2)]
        x2 = cut(dense, T * D).rearrange("p (t n) -> p t n", t=T)
        at(KD * (3 * D + D + HID + D * KH // KD + HID))
        x1b = [cut(dense, T * D).rearrange("p (t n) -> p t n", t=T) for _ in range(2)]
        at((E - 2) * EXPERT)
        x1T = [cut(arena, KD * IMG).rearrange("p (k n) -> p k n", k=KD) for _ in range(2)]
        gT = cut(arena, KH * IMG).rearrange("p (k n) -> p k n", k=KH)
        pay = [None, cut(arena, T * PAY).rearrange("p (t n) -> p t n", t=T)]
        at((E - 1) * EXPERT)
        pay[0] = cut(arena, T * PAY).rearrange("p (t n) -> p t n", t=T)
        xmT = [cut(arena, KD * IMG).rearrange("p (k n) -> p k n", k=KD) for _ in range(2)]
        rT = cut(arena, KH * IMG).rearrange("p (k n) -> p k n", k=KH)

        experts = arena[:, :].rearrange("p (e n) -> p e n", e=E)
        b2bc = x1[:, 0:E, :]

        at(0)
        ident = cut(small, P)
        same = cut(small, P)
        before = cut(small, P)
        ones = cut(small, P)
        gamma_bc, beta_bc, beta2_bc, bout_bc = (cut(small, D) for _ in range(4))
        cols = cut(small, E * KH + 2 * KH + 2 * KD)
        eb1T = cols[:, 0:E * KH].rearrange("p (e k) -> p e k", e=E)
        b1T, rb1T = cols[:, 64:72], cols[:, 72:80]
        gammaT, betaT = cols[:, 80:82], cols[:, 82:84]
        gate_now = [cut(small, 1) for _ in range(2)]
        b1now = [cut(small, KH) for _ in range(2)]
        dots = cut(small, 10)
        bd = cut(small, 10)
        gate = cut(small, 10)
        gsc = cut(small, 24)
        stats = cut(small, T * 6).rearrange("p (t n) -> p t n", t=T)
        mv = cut(small, T * 2).rearrange("p (t n) -> p t n", t=T)
        rstd = cut(small, T).rearrange("p (t n) -> p t n", t=T)
        neg_half = cut(small, T).rearrange("p (t n) -> p t n", t=T)
        den = cut(small, (T + 1) * HEADS).rearrange("p (t h) -> p t h", t=T + 1)
        c_xT, c_qT, c_kT = (cut(small, KD) for _ in range(3))
        c_qf, c_ql = cut(small, PAIRS), cut(small, PAIRS)
        rb2_bc = cut(small, E)
        iota8 = cut(small, E)
        lg = cut(small, T * E).rearrange("p (t e) -> p t e", t=T)
        top = cut(small, T * 8).rearrange("p (t e) -> p t e", t=T)
        topf = cut(small, T * 2).rearrange("p (t e) -> p t e", t=T)
        gap = cut(small, T).rearrange("p (t n) -> p t n", t=T)
        half = cut(small, T).rearrange("p (t n) -> p t n", t=T)
        probs = cut(small, 2 * T).rearrange("p (k t n) -> p k t n", k=2, t=T)
        onehot = cut(small, 2 * T * E).rearrange("p (k t e) -> p k t e", k=2, t=T)
        mask = cut(small, T * E).rearrange("p (t e) -> p t e", t=T)
        weighed = cut(small, 2 * T * E).rearrange("p (k t e) -> p k t e", k=2, t=T)
        rank = cut(small, T * E).rearrange("p (t e) -> p t e", t=T)
        placed = cut(small, 2 * T * E).rearrange("p (k t e) -> p k t e", k=2, t=T)
        placef = cut(small, 2 * T).rearrange("p (k t n) -> p k t n", k=2, t=T)
        used = cut(small, E)
        ids = cut(small, T).rearrange("p (t n) -> p t n", t=T)
        topi = sb("topi", [P, T, 8], U32)
        place = [sb(f"place{i}", [P, 2, T], U32) for i in range(2)]
        c_place = sb("c_place", [P, 2], U32)
        slot_ids = [sb(f"slot_ids{i}", [P, 1], U32) for i in range(2)]
        cx = sb("cx", [B, 3, D])
        c_attT = sb("c_attT", [P, KD, B])
        limits = cut(small, 18)
        tnum = cut(small, MOE_TILES)
        region0 = cut(small, E + 1)
        first_src = cut(small, (E + 1) * E).rearrange("p (a e) -> p a e", a=E + 1)
        at(2 * (PAY + D + KD * HID + HID + D + D))
        over = cut(dense, E * 18).rearrange("p (e j) -> p e j", e=E)
        count = cut(dense, E)
        tiles_e = cut(dense, E)
        lower = cut(dense, (E + 1) * E).rearrange("p (a e) -> p a e", a=E + 1)
        first = cut(dense, E + 1)
        owner = cut(dense, MOE_TILES)
        step = cut(dense, MOE_TILES)
        rowt = cut(dense, MOE_TILES)
        jump = cut(dense, E + 1)
        owner_i, row_i = (cut(dense, MOE_TILES).bitcast(I32) for _ in range(2))
        used_i = cut(dense, E).bitcast(I32)
        padrow = cut(dense, PAY)

        bank = [ctx.enter_context(nc.psum_tensor(f"bank{i}", [P, 512], F32)) for i in range(8)]
        psT, psL, psF, psKV, psAT = bank[0], bank[1:3], bank[3:5], bank[5], bank[6:8]
        psO, psLG, psRK = bank[6:8], bank[1], bank[2]
        psUP = [bank[3:5], bank[1:3]]

        img_loaded = sem("img_loaded")
        wd1_loaded = sem("wd1_loaded")
        wd2_loaded = sem("wd2_loaded")
        wd3_loaded = sem("wd3_loaded")
        wa_loaded = sem("wa_loaded")
        smalls_loaded = sem("smalls_loaded")
        raw_loaded = sem("raw_loaded")
        direct_loaded = sem("direct_loaded")
        dve_passed = sem("dve_passed")
        pool_passed = sem("pool_passed")
        iota_ready = sem("iota_ready")
        consts_ready = sem("consts_ready")
        pool_step = sem("pool_step")
        dve_step = sem("dve_step")
        act_step = sem("act_step")
        dots_ready = sem("dots_ready")
        totals_ready = sem("totals_ready")
        logits_ready = sem("logits_ready")
        exps_ready = sem("exps_ready")
        image_ready = sem("image_ready")
        relaid = sem("relaid")
        wT_ps = sem("wT_ps")
        wT_sb = sem("wT_sb")
        c_norm = sem("c_norm")
        c_ps = sem("c_ps")
        c_done = sem("c_done")
        catt_moved = sem("catt_moved")
        cattT_ps = sem("cattT_ps")
        cattT_sb = sem("cattT_sb")
        c_out_ps = sem("c_out_ps")
        c_x1 = sem("c_x1")
        c_var = sem("c_var")
        c_root = sem("c_root")
        t_var = sem("t_var")
        t_root = sem("t_root")
        x_var = sem("x_var")
        x_root = sem("x_root")
        m_var = sem("m_var")
        m_root = sem("m_root")
        ln_ready = sem("ln_ready")
        xnb_ready = sem("xnb_ready")
        xT_ps = sem("xT_ps")
        xT_sb = sem("xT_sb")
        q_ps = sem("q_ps")
        q_sb = sem("q_sb")
        k_ps = sem("k_ps")
        k_sb = sem("k_sb")
        v_ps = sem("v_ps")
        v_sb = sem("v_sb")
        f_ps = sem("f_ps")
        f_neg = sem("f_neg")
        f_read = sem("f_read")
        f_exp = sem("f_exp")
        f_sum = sem("f_sum")
        kv_ps = sem("kv_ps")
        kvbd_ready = sem("kvbd_ready")
        attn_ps = sem("attn_ps")
        att_ready = sem("att_ready")
        attT_ps = sem("attT_ps")
        attT_sb = sem("attT_sb")
        out_ps = sem("out_ps")
        x1_ready = sem("x1_ready")
        xh_ready = sem("xh_ready")
        x1b_ready = sem("x1b_ready")
        x1T_ps = sem("x1T_ps")
        x1T_sb = sem("x1T_sb")
        m_ps = sem("m_ps")
        m_sb = sem("m_sb")
        mlp_ps = sem("mlp_ps")
        xm_ready = sem("xm_ready")
        h1_ready = sem("h1_ready")
        xmT_ps = sem("xmT_ps")
        xmT_sb = sem("xmT_sb")
        lg_ps = sem("lg_ps")
        lg_gap = sem("lg_gap")
        lg_half = sem("lg_half")
        mask_ready = sem("mask_ready")
        rk_ps = sem("rk_ps")
        place_ready = sem("place_ready")
        scat0 = sem("scat0")
        scat1 = sem("scat1")
        h1_stored0 = sem("h1_stored0")
        h1_stored1 = sem("h1_stored1")
        used_ready = sem("used_ready")
        pad_ready = sem("pad_ready")
        tables_ready = sem("tables_ready")
        pads_stored = sem("pads_stored")
        dump_zeroed = sem("dump_zeroed")
        low_loaded = sem("low_loaded")
        high_loaded = sem("high_loaded")
        b2_loaded = sem("b2_loaded")
        xs_loaded0 = sem("xs_loaded0")
        xs_loaded1 = sem("xs_loaded1")
        xsT_ps = sem("xsT_ps")
        xsT_sb = sem("xsT_sb")
        h_ps = sem("h_ps")
        w1_ready = sem("w1_ready")
        hT_sb = sem("hT_sb")
        y_ps = sem("y_ps")
        y_ready = sem("y_ready")
        b1_ready = sem("b1_ready")
        slot_ready = sem("slot_ready")
        rows_added = sem("rows_added")
        out_stored = sem("out_stored")

        def vector(name):
            return t[name].rearrange("(o n) -> o n", o=1)

        smalls = [(gamma_bc, vector("L0_attn_gamma").to_broadcast([P, D])),
                  (beta_bc, vector("L0_attn_beta").to_broadcast([P, D])),
                  (beta2_bc, vector("L0_attn_b2").to_broadcast([P, D])),
                  (bout_bc, vector("L0_attn_b_out").to_broadcast([P, D])),
                  (bd[:, 0:1], vector("L0_tok_ba").to_broadcast([P, 1])),
                  (bd[:, 1:4], vector("L0_tok_bd1").to_broadcast([P, 3])),
                  (bd[:, 4:7], vector("L0_tok_bd2").to_broadcast([P, 3])),
                  (bd[:, 7:10], vector("L0_tok_bd3").to_broadcast([P, 3])),
                  (rb2_bc, vector("L0_ffn_rb2").to_broadcast([P, E])),
                  (cx[0:B, 0, :], t["cls_tok"].rearrange("o q n -> (o q) n").to_broadcast([B, D]))]
        raws = [(raw_qkv, t["L0_attn_w_qkv"].rearrange("(m p) n -> p m n", p=P)),
                (raw_o, t["L0_attn_w_out"].rearrange("(m p) n -> p m n", p=P)),
                (raw_w1, t["L0_attn_w1"].rearrange("(m p) n -> p m n", p=P)),
                (raw_w2, t["L0_attn_w2"].rearrange("(m p) n -> p m n", p=P)),
                (raw_cols[0:64, :], t["L0_ffn_b1"].rearrange("e (k p) -> (e k) p", p=P)),
                (raw_cols[64:72, :], t["L0_attn_b1"].rearrange("(k p) -> k p", p=P)),
                (raw_cols[72:80, :], t["L0_ffn_rb1"].rearrange("(k p) -> k p", p=P)),
                (raw_cols[80:82, :], t["L0_attn_gamma"].rearrange("(k p) -> k p", p=P)),
                (raw_cols[82:84, :], t["L0_attn_beta"].rearrange("(k p) -> k p", p=P))]

        def feature_rows(par, i):
            if i < 4:
                return kf[par][:, i // 2, i % 2, :]
            return qf[par][:, 2 * (i - 4):2 * (i - 4) + 2, :].rearrange("p m n -> p (m n)")

        def block_of(raw, m, k):
            return raw[:, m, k * P:(k + 1) * P]

        turned = [(wqkvT[:, k, 0:4 * P], [block_of(raw_qkv, m, k) for m in range(4)]) for k in range(KD)]
        turned += [(wqkvT[:, :, 4 * P:6 * P], [block_of(raw_qkv, m, k) for k in range(KD) for m in (4, 5)])]
        turned += [(woT[:, :, :], [block_of(raw_o, m, k) for k in range(KD) for m in range(KD)])]
        turned += [(w1T[:, k, 4 * P * q:4 * P * (q + 1)], [block_of(raw_w1, m, k) for m in range(4 * q, 4 * q + 4)])
                   for k in range(KD) for q in range(2)]
        turned += [(w2T[:, 2 * i:2 * i + 2, :], [block_of(raw_w2, m, k) for k in (2 * i, 2 * i + 1) for m in range(KD)])
                   for i in range(KH // 2)]

        def normalize(dve, link, src, dst, n, tiles, asked, answered, count):
            apart(dve, dve_passed)
            for j in range(tiles):
                ins = dve.bn_stats(stats[0:n, j, :], src(j))
            link(ins)
            apart(dve, dve_passed)
            for j in range(tiles):
                ins = dve.bn_aggr(mv[0:n, j, :], stats[0:n, j, :])
            ins.then_inc(asked, 1)
            dve.wait_ge(answered, count)
            for j in range(tiles):
                ins = dve.tensor_scalar(dst(j), src(j), mv[0:n, j, 0:1], rstd[0:n, j, :], ALU.subtract, ALU.mult)
            return ins

        def root(pool, link, n, tiles, asked, answered, count, mv=mv, rstd=rstd):
            pool.wait_ge(asked, count)
            apart(pool, pool_passed)
            link(pool.tensor_scalar(rstd[0:n, 0:tiles, :], mv[0:n, 0:tiles, 1:2], EPS_LN, None, ALU.add))
            pool.tensor_tensor(rstd[0:n, 0:tiles, :], rstd[0:n, 0:tiles, :], neg_half[0:n, 0:tiles, :], ALU.pow
                               ).then_inc(answered, 1)

        block = ctx.enter_context(nc.Block())

        @block.sync
        def _(sp):
            sp.dma_start(img, t["x"].rearrange("b (s r) w c -> (b s) (r w c)", s=STRIPS)).then_inc(img_loaded, 16)
            for lvl, loaded, w in ((3, wd3_loaded, t["L0_tok_Wd1"]), (2, wd2_loaded, t["L0_tok_Wd2"]),
                                   (1, wd1_loaded, t["L0_tok_Wd3"])):
                n = wd[lvl].shape[1] // 3
                src = w.rearrange("(c s n) k -> s c (n k)", c=3, s=STRIPS)
                for b in range(B):
                    dst = wd[lvl][STRIPS * b:STRIPS * (b + 1), :].rearrange("p (c m) -> p c m", c=3)
                    assert dst.shape[2] == n
                    sp.dma_start(dst, src).then_inc(loaded, 16)
            for b in range(B):
                sp.dma_start(wa[STRIPS * b:STRIPS * (b + 1), :],
                             t["L0_tok_Wa"].rearrange("(s n) k -> s (n k)", s=STRIPS)).then_inc(wa_loaded, 16)
            sp.wait_ge(image_ready, 1)
            for b in range(B):
                for j in range(T):
                    p0 = STRIPS * b + STRIPS // T * j
                    sp.dma_start(h[:, T * b + j, :],
                                 img[p0:p0 + STRIPS // T, :].rearrange("p (r n) -> p r n", r=ROWS)
                                 ).then_inc(relaid, 16)
            sp.wait_ge(att_ready, 3 * B)
            sp.dma_start(cx[0:B, 2, :], catt[0:1, :, :]).then_inc(catt_moved, 16)
            sp.wait_ge(c_x1, 1)
            sp.wait_ge(x1_ready, B)
            sp.wait_ge(catt_moved, 16)
            def load_expert(e, loaded):
                sp.dma_start(experts[:, e, 0:KD * HID].rearrange("p (k n) -> p k n", k=KD),
                             t["L0_ffn_w1"][e].rearrange("(k p) n -> p k n", p=P)).then_inc(loaded, 16)
                sp.dma_start(experts[:, e, KD * HID:EXPERT].rearrange("p (k n) -> p k n", k=KH),
                             t["L0_ffn_w2"][e].rearrange("(k p) n -> p k n", p=P)).then_inc(loaded, 16)

            for e in range(E - 2):
                load_expert(e, low_loaded)
            stored = [h1_stored0, h1_stored1]

            def store_h1(g, par):
                sp.wait_ge(h1_ready, g + 1)
                sp.dma_start(acc_d[bass.ds(g * SEQ + 1, IMG), :].rearrange("(t p) n -> p t n", p=P),
                             h[:, bass.ds(T * g, T), :]).then_inc(stored[par], 16)
            with sp.Fori(0, B // 2) as it:
                store_h1(2 * it, 0)
                store_h1(2 * it + 1, 1)
            sp.wait_ge(h1_ready, B + 1)
            sp.dma_start(acc_d[0:TOKENS, :].rearrange("(b q) n -> b q n", b=B)[:, 0, :],
                         cx[0:B, 0, :]).then_inc(h1_stored0, 16)
            sp.wait_ge(xh_ready, B)
            sp.dma_start(b2bc, t["L0_ffn_b2"].rearrange("(o e) n -> o e n", o=1).to_broadcast([P, E, D])
                         ).then_inc(b2_loaded, 16)
            sp.wait_ge(mlp_ps, T * B + 1)
            sp.wait_ge(scat1, 16 * 2 * (T * B // 2))
            load_expert(E - 2, high_loaded)
            sp.wait_ge(pad_ready, 1)
            with sp.Fori(0, E) as e:
                row = sp.value_load(used_i[0:1, bass.ds(e, 1)], min_val=0, max_val=E * REGION - P)
                sp.dma_start(xs_d[bass.ds(row, P), :], padrow[:, :]).then_inc(pads_stored, 16)
            sp.dma_start(xs_d[E * REGION:E * REGION + P, :], padrow[:, :]).then_inc(pads_stored, 16)
            sp.dma_start(acc_d[TOKENS:TOKENS + P, :], padrow[:, 0:D]).then_inc(dump_zeroed, 16)
            sp.wait_ge(scat0, 16 * 2 * (T * B // 2 + 1))
            load_expert(E - 1, high_loaded)
            sp.wait_ge(pads_stored, 16 * (E + 1))
            sp.wait_ge(tables_ready, 1)
            loaded = [xs_loaded0, xs_loaded1]

            def load_rows(i, par, ahead):
                if ahead:
                    sp.wait_ge(xsT_ps, i - 1)
                    sp.wait_ge(slot_ready, i - 1)
                row = sp.value_load(row_i[0:1, bass.ds(i, 1)], min_val=0, max_val=E * REGION)
                sp.dma_start(xs[par], xs_d[bass.ds(row, P), :]).then_inc(loaded[par], 16)
            load_rows(0, 0, False)
            load_rows(1, 1, False)
            with sp.Fori(0, MOE_TILES // 2 - 1) as it:
                load_rows(2 * it + 2, 0, True)
                load_rows(2 * it + 3, 1, True)
            sp.wait_ge(rows_added, 16 * MOE_TILES)
            sp.dma_start(t["out"].rearrange("b q n -> (b q) n"), acc_d[0:TOKENS, :]).then_inc(out_stored, 16)
            sp.wait_ge(out_stored, 16)

        @block.gpsimd
        def _(pool):
            chain = Chain(pool, pool_step)
            link = chain.link

            def triangle(out, op, base, fill, mult, pattern):
                return pool.affine_select(out=out, in_=out, compare_op=op, fill=fill, base=base,
                                          pattern=pattern, channel_multiplier=mult)

            pool.memset(ident, 0.0)
            pool.memset(same, 1.0)
            pool.memset(before, 1.0)
            pool.memset(ones, 1.0)
            pool.memset(neg_half, -0.5)
            pool.memset(first_src[:, :, :], 1.0)
            pool.memset(projbd[:, :, :], 0.0).then_inc(iota_ready, 1)
            link(pool.memset(cols, 0.0))
            triangle(ident, ALU.not_equal, 0, 1.0, 1, [[-1, P]])
            link(triangle(same.rearrange("p (b s) -> p b s", b=B), ALU.is_ge, 0, 0.0, 1, [[-STRIPS, B], [0, STRIPS]]))
            triangle(same.rearrange("p (b s) -> p b s", b=B), ALU.is_ge, STRIPS - 1, 0.0, -1,
                     [[STRIPS, B], [0, STRIPS]])
            triangle(before, ALU.is_ge, -1, 0.0, -1, [[1, P]])
            triangle(first_src, ALU.is_ge, -1, 0.0, 0, [[1, E + 1], [-1, E]])
            pool.iota(iota8, [[1, E]], base=0, channel_multiplier=0, allow_small_or_imprecise_dtypes=True)
            pool.iota(used, [[REGION, E]], base=0, channel_multiplier=0, allow_small_or_imprecise_dtypes=True)
            pool.iota(region0, [[REGION, E + 1]], base=0, channel_multiplier=0, allow_small_or_imprecise_dtypes=True)
            pool.iota(limits, [[P, 18]], base=0, channel_multiplier=0, allow_small_or_imprecise_dtypes=True)
            pool.iota(tnum, [[1, MOE_TILES]], base=0, channel_multiplier=0, allow_small_or_imprecise_dtypes=True)
            pool.iota(ids[:, :, 0], [[P, T]], base=1, channel_multiplier=1,
                      allow_small_or_imprecise_dtypes=True).then_inc(consts_ready, 1)
            pool.wait_ge(smalls_loaded, 16 * len(smalls))
            link(pool.tensor_tensor(beta2_bc, beta2_bc, beta_bc, ALU.add))

            def residual(g, par):
                pool.wait_ge(ln_ready, g + 1)
                after(pool, x1_ready, g - 1)
                for j in range(T):
                    ins = pool.tensor_tensor(xnb[par][:, j, :], xn[par][:, j, :], bout_bc, ALU.add)
                ins.then_inc(xnb_ready, 1)
            root(pool, link, B, 1, c_var, c_root, 1)
            for g in range(3):
                root(pool, link, P, T, t_var, t_root, g + 1, t_mv[g % 2], t_rstd[g % 2])
            residual(0, 0)

            def attention_step(g, par):
                for i in range(8):
                    u = 8 * g + i
                    pool.wait_ge(f_exp, u + 1)
                    dst = feature_rows(par, i)
                    pool.tensor_tensor(dst, dst, lin[i % 4], ALU.add).then_inc(f_sum, 1)
                    if i == 4 and (not isinstance(g, int) or g + 3 < B):
                        root(pool, link, P, T, t_var, t_root, g + 4, t_mv[1 - par], t_rstd[1 - par])
                if not isinstance(g, int) or g + 1 < B:
                    residual(g + 1, 1 - par)

            attention_step(0, 0)

            def turn(it):
                attention_step(2 * it + 1, 1)
                attention_step(2 * it + 2, 0)
            chain.loop((B - 4) // 2, 2, turn)
            for g in range(B - 3, B):
                attention_step(g, g % 2)

            def affine(g, par):
                pool.wait_ge(xh_ready, g + 1)
                tiles, n, hx = (T, P, None) if not (isinstance(g, int) and g == B) else (1, B, cx)
                after(pool, xm_ready, g - 1)
                for j in range(tiles):
                    ins = pool.tensor_tensor(x1b[par][0:n, j, :], xh[par][0:n, j, :], gamma_bc[0:n, :], ALU.mult)
                for j in range(tiles):
                    hj = h[:, bass.ds(T * g + j, 1), :].rearrange("p o n -> p (o n)") if hx is None else cx[0:B, 0, :]
                    ins = pool.tensor_tensor(hj, hj, beta_bc[0:n, :], ALU.add)
                link(ins)
                for j in range(tiles):
                    ins = pool.tensor_tensor(x1b[par][0:n, j, :], x1b[par][0:n, j, :], beta2_bc[0:n, :], ALU.add)
                ins.then_inc(x1b_ready, 1)

            def scatter(g, par):
                pool.wait_ge(place_ready, g + 1)
                apart(pool, pool_passed)
                tail = isinstance(g, int) and g == B
                done = scat0 if par == 0 else scat1
                for j in range(1 if tail else T):
                    for k in range(2):
                        n = B if tail else P
                        idx = c_place[0:B, k:k + 1] if tail else place[par][:, k, j:j + 1]
                        pool.indirect_dma_start(
                            out=xs_d[:, :], out_offset=bass.IndirectOffsetOnAxis(ap=idx, axis=0),
                            in_=pay[par][0:n, j, :], in_offset=None).then_inc(done, 16)

            root(pool, link, P, T, x_var, x_root, 1)
            affine(0, 0)

            def routing_step(g, par):
                peeled = isinstance(g, int)
                if not peeled or 1 <= g <= B + 1:
                    n, tiles = (B, 1) if peeled and g - 1 == B else (P, T)
                    root(pool, link, n, tiles, m_var, m_root, 2 * g - 1)
                    root(pool, link, n, tiles, m_var, m_root, 2 * g)
                if not peeled or g + 1 <= B:
                    n, tiles = (B, 1) if peeled and g + 1 == B else (P, T)
                    root(pool, link, n, tiles, x_var, x_root, g + 2)
                    affine(g + 1, 1 - par)
                if not peeled or g >= 2:
                    scatter(g - 2, par)
            for g in range(3):
                routing_step(g, g % 2)

            def turn(it):
                routing_step(2 * it + 3, 1)
                routing_step(2 * it + 4, 0)
            chain.loop(2, 8, turn)
            for g in range(7, B + 3):
                routing_step(g, g % 2)

            pool.wait_ge(used_ready, 1)
            link(pool.memset(padrow, 0.0))
            pool.iota(padrow[:, D:D + 1], [[0, 1]], base=TOKENS, channel_multiplier=1,
                      allow_small_or_imprecise_dtypes=True).then_inc(pad_ready, 1)

            pool.wait_ge(h1_stored0, 16 * (B // 2 + 1))
            pool.wait_ge(h1_stored1, 16 * (B // 2))
            pool.wait_ge(dump_zeroed, 16)

            def add_rows(i, par, later):
                if later:
                    pool.wait_ge(rows_added, i * 16)
                pool.wait_ge(y_ready, i + 1)
                apart(pool, pool_passed)
                pool.indirect_dma_start(
                    out=acc_d[:, :], out_offset=bass.IndirectOffsetOnAxis(ap=slot_ids[par][:, 0:1], axis=0),
                    in_=y[par], in_offset=None, compute_op=ALU.add).then_inc(rows_added, 16)
            add_rows(0, 0, False)
            add_rows(1, 1, True)
            with pool.Fori(0, MOE_TILES // 2 - 1) as it:
                add_rows(2 * it + 2, 0, True)
                add_rows(2 * it + 3, 1, True)

        @block.vector
        def _(dve):
            chain = Chain(dve, dve_step)
            link = chain.link

            dve.wait_ge(img_loaded, 16)
            cur, side, rows = img, IMG, ROWS
            for lvl in (1, 2, 3):
                c2 = cur[:, 0:rows * side].rearrange("p (m two) -> p m two", two=2)
                n = rows * side // 2
                lo, hi = lohi[:, 0:n], lohi[:, n:2 * n]
                dve.tensor_tensor(lo, c2[:, :, 0], c2[:, :, 1], ALU.add)
                link(dve.tensor_tensor(hi, c2[:, :, 0], c2[:, :, 1], ALU.subtract))
                q = n // 2
                lo4 = lo.rearrange("p (r two c) -> p r two c", two=2, c=side // 2)
                hi4 = hi.rearrange("p (r two c) -> p r two c", two=2, c=side // 2)

                def band(ap):
                    return ap.rearrange("p (r c) -> p r c", c=side // 2)
                dd = det[lvl]
                dve.tensor_tensor(band(app[lvl][:, 0:q]), lo4[:, :, 0, :], lo4[:, :, 1, :], ALU.add)
                dve.tensor_tensor(band(dd[:, 0:q]), lo4[:, :, 0, :], lo4[:, :, 1, :], ALU.subtract)
                dve.tensor_tensor(band(dd[:, q:2 * q]), hi4[:, :, 0, :], hi4[:, :, 1, :], ALU.add)
                link(dve.tensor_tensor(band(dd[:, 2 * q:3 * q]), hi4[:, :, 0, :], hi4[:, :, 1, :], ALU.subtract))
                cur, side, rows = app[lvl], side // 2, rows // 2

            junk = img
            dve.wait_ge(wa_loaded, 16 * B)
            link(dve.tensor_tensor_reduce(junk[:, 0:64], app[3], wa, 1.0, 0.0, ALU.mult, ALU.add, dots[:, 0:1]))
            for lvl, loaded, c0 in ((3, wd3_loaded, 1), (2, wd2_loaded, 4), (1, wd1_loaded, 7)):
                dve.wait_ge(loaded, 16 * B)
                n = det[lvl].shape[1]
                w3 = wd[lvl].rearrange("p (n k) -> p n k", k=3)
                for k in range(3):
                    ins = dve.tensor_tensor_reduce(junk[:, 0:n], det[lvl][:, :], w3[:, :, k], 1.0, 0.0, ALU.mult,
                                                   ALU.add, dots[:, c0 + k:c0 + k + 1])
                    if lvl == 1 and k == 2:
                        ins.then_inc(dots_ready, 1)
                    else:
                        link(ins)
            dve.wait_ge(smalls_loaded, 16 * len(smalls))
            dve.wait_ge(totals_ready, 1)
            for c0, c1, scale in ((0, 4, 0.125), (4, 7, 0.25), (7, 10, 0.5)):
                ins = dve.scalar_tensor_tensor(out=gate[:, c0:c1], in0=psT[:, c0:c1], scalar=scale,
                                               in1=bd[:, c0:c1], op0=ALU.mult, op1=ALU.add)
            link(ins)
            g3 = gate[:, 1:10].rearrange("p (l k) -> p l k", k=3)
            m3 = gsc[:, 0:3].rearrange("p (l o) -> p l o", o=1)
            link(dve.tensor_reduce(gsc[:, 0:3], g3, AX_X, ALU.max))
            dve.tensor_tensor(g3, g3, m3.to_broadcast([P, 3, 3]), ALU.subtract).then_inc(logits_ready, 1)
            dve.wait_ge(exps_ready, 1)
            dve.tensor_scalar(gsc[:, 3:4], gate[:, 0:1], 1.0, None, ALU.add)
            link(dve.tensor_reduce(gsc[:, 4:7], g3, AX_X, ALU.add))
            link(dve.reciprocal(gsc[:, 7:11], gsc[:, 3:7]))
            dve.tensor_scalar(gate[:, 0:1], gsc[:, 7:8], 1.0 / 64, None, ALU.mult)
            for l, f in ((0, 1.0 / 64), (1, 1.0 / 16), (2, 1.0 / 4)):
                ins = dve.tensor_scalar(gate[:, 1 + 3 * l:4 + 3 * l], gate[:, 1 + 3 * l:4 + 3 * l],
                                        gsc[:, 8 + l:9 + l], f, ALU.mult, ALU.mult)
            link(ins)
            link(dve.tensor_scalar(gsc[:, 12:21], gate[:, 1:10], -1.0, None, ALU.mult))

            link(dve.tensor_scalar(app[3][:, :], app[3][:, :], gate[:, 0:1], None, ALU.mult))
            for l, lvl in ((0, 3), (1, 2), (2, 1)):
                q = app[lvl].shape[1]
                side = IMG >> lvl
                dd = det[lvl]
                lo4 = lohi[:, 0:2 * q].rearrange("p (r two c) -> p r two c", two=2, c=side)
                hi4 = lohi[:, 2 * q:4 * q].rearrange("p (r two c) -> p r two c", two=2, c=side)

                def band(ap):
                    return ap.rearrange("p (r c) -> p r c", c=side)
                gh, gv, gd = (gate[:, 1 + 3 * l + k:2 + 3 * l + k] for k in range(3))
                ngh = gsc[:, 12 + 3 * l:13 + 3 * l]
                link(dve.tensor_scalar(dd[:, 2 * q:3 * q], dd[:, 2 * q:3 * q], gd, None, ALU.mult))
                for r, g, op in ((0, gh, ALU.add), (1, ngh, ALU.add)):
                    dve.scalar_tensor_tensor(out=lo4[:, :, r, :], in0=band(dd[:, 0:q]), scalar=g,
                                             in1=band(app[lvl]), op0=ALU.mult, op1=op)
                for r, op in ((0, ALU.add), (1, ALU.subtract)):
                    ins = dve.scalar_tensor_tensor(out=hi4[:, :, r, :], in0=band(dd[:, q:2 * q]), scalar=gv,
                                                   in1=band(dd[:, 2 * q:3 * q]), op0=ALU.mult, op1=op)
                link(ins)
                to = img if lvl == 1 else app[lvl - 1]
                o2 = to[:, 0:4 * q].rearrange("p (m two) -> p m two", two=2)
                dve.tensor_tensor(o2[:, :, 0], lohi[:, 0:2 * q], lohi[:, 2 * q:4 * q], ALU.add)
                ins = dve.tensor_tensor(o2[:, :, 1], lohi[:, 0:2 * q], lohi[:, 2 * q:4 * q], ALU.subtract)
                if lvl == 1:
                    ins.then_inc(image_ready, 1)
                else:
                    link(ins)

            normalize(dve, link, lambda j: cx[0:B, 0, :], lambda j: cx[0:B, 1, :], B, 1, c_var, c_root, 1
                      ).then_inc(c_norm, 1)
            dve.wait_ge(c_norm, 1)
            dve.wait_ge(c_ps, 1)
            dve.tensor_copy(c_xT, psT[:, 0:KD]).then_inc(c_done, 1)
            dve.wait_ge(c_ps, 2)
            dve.tensor_copy(c_qT, psT[:, 4:4 + KD])
            dve.tensor_copy(c_kT, psT[:, 6:6 + KD]).then_inc(c_done, 1)
            link(dve.memset(c_va[0:1, :, :], 1.0))
            dve.tensor_copy(c_va[0:1, :, 0:HD], psL[0][0:1, 0:D].rearrange("p (h d) -> p h d", h=HEADS))
            dve.wait_ge(c_ps, 3)
            for i in range(2):
                dve.tensor_scalar(c_kl[0:1, 512 * i:512 * i + 512], psF[i][0:1, :], 0.0, None, ALU.max)
                dve.tensor_scalar(c_kf[0:1, 512 * i:512 * i + 512], psF[i][0:1, :], 0.0, None, ALU.min)
            dve.tensor_scalar(c_ql, psL[1][:, 0:PAIRS], 0.0, None, ALU.max)
            dve.tensor_scalar(c_qf, psL[1][:, 0:PAIRS], 0.0, None, ALU.min).then_inc(c_done, 1)
            dve.wait_ge(c_done, 3)
            dve.wait_ge(act_step, 1)
            dve.tensor_tensor(c_qf, c_qf, c_ql, ALU.add)
            dve.tensor_tensor(c_kf[0:1, :], c_kf[0:1, :], c_kl[0:1, :], ALU.add).then_inc(c_done, 1)
            dve.tensor_tensor(cx[0:B, 1, :], cx[0:B, 1, :], bout_bc[0:B, :], ALU.add)
            for i in range(2):
                dve.memset(va[i][:, :, :, HD:VA], 1.0)
                ins = dve.memset(kvbd[i][:, :, :], 0.0)
            link(ins)

            dve.wait_ge(relaid, 16 * B * T)

            def token(g, j):
                return h[:, bass.ds(T * g + j, 1), :].rearrange("p o n -> p (o n)")

            def token_stats(g, par):
                after(dve, t_var, g)
                apart(dve, dve_passed)
                for j in range(T):
                    ins = dve.bn_stats(stats[:, j, :], token(g, j))
                link(ins)
                apart(dve, dve_passed)
                for j in range(T):
                    ins = dve.bn_aggr(t_mv[par][:, j, :], stats[:, j, :])
                ins.then_inc(t_var, 1)

            def norm_tokens(g, par):
                dve.wait_ge(t_root, g + 1)
                after(dve, xT_ps, g - 1)
                after(dve, xnb_ready, g - 1)
                for j in range(T):
                    ins = dve.tensor_scalar(xn[par][:, j, :], token(g, j), t_mv[par][:, j, 0:1], t_rstd[par][:, j, :],
                                            ALU.subtract, ALU.mult)
                ins.then_inc(ln_ready, 1)

            def v_rows(g, par):
                dve.wait_ge(v_ps, g + 1)
                after(dve, kv_ps, g - 1)
                dve.tensor_copy(va[par][:, :, :, 0:HD],
                                psL[1][:, :].rearrange("p (t h d) -> p t h d", t=T, h=HEADS)).then_inc(v_sb, 1)

            def x1_rows(g, par):
                dve.wait_ge(out_ps, g + 1)
                dve.wait_ge(xnb_ready, g + 1)
                dve.tensor_tensor(x1[:, bass.ds(T * g, T), :], psL[0][:, :].rearrange("p (t n) -> p t n", t=T),
                                  xnb[par][:, :, :], ALU.add).then_inc(x1_ready, 1)

            token_stats(0, 0)
            token_stats(1, 1)
            norm_tokens(0, 0)
            dve.wait_ge(ln_ready, 1)
            token_stats(2, 0)
            norm_tokens(1, 1)
            v_rows(0, 0)

            def attention_step(g, par):
                peeled = isinstance(g, int)
                def negatives(i):
                    dve.wait_ge(f_ps, 8 * g + i + 1)
                    dve.tensor_scalar(feature_rows(par, i), psF[i % 2][:, :], 0.0, None, ALU.min
                                      ).then_inc(f_neg, 1)
                negatives(0)
                negatives(1)
                if not peeled or g + 2 < B:
                    norm_tokens(g + 2, par)
                negatives(2)
                negatives(3)
                if not peeled or g + 3 < B:
                    token_stats(g + 3, 1 - par)
                for i in range(4, 8):
                    negatives(i)
                if not peeled or g >= 1:
                    x1_rows(g - 1, 1 - par)
                dve.wait_ge(kv_ps, g + 1)
                kvv = psKV[:, 0:PAIRS * PW].rearrange("p (m n) -> p m n", m=PAIRS)
                dve.tensor_copy(kvbd[par][0:64, :, 0:VA], kvv[0:64, :, 0:VA])
                dve.tensor_copy(kvbd[par][64:P, :, VA:PW], kvv[64:P, :, VA:PW]).then_inc(kvbd_ready, 1)
                if not peeled or g + 1 < B:
                    v_rows(g + 1, 1 - par)
                for j in range(T + 1):
                    dve.wait_ge(attn_ps, (T + 1) * g + j + 1)
                    n = P if j < T else 1
                    src = (psAT[j] if j < T else psKV)[0:n, 0:PAIRS * PW].rearrange("p (h d) -> p h d", h=HEADS)
                    d3 = den[0:n, j, :].rearrange("p (h o) -> p h o", o=1)
                    link(dve.tensor_scalar(d3, src[:, :, HD:VA], EPS_ATTN, None, ALU.add))
                    link(dve.reciprocal(den[0:n, j, :], den[0:n, j, :]))
                    dst = (att[par][:, j, :] if j < T else
                           catt[0:1, bass.ds(g, 1), :].rearrange("p o n -> p (o n)"))
                    dve.tensor_tensor(dst.rearrange("p (h d) -> p h d", h=HEADS), src[:, :, 0:HD],
                                      d3.to_broadcast([n, HEADS, HD]), ALU.mult).then_inc(att_ready, 1)

            attention_step(0, 0)

            def turn(it):
                attention_step(2 * it + 1, 1)
                attention_step(2 * it + 2, 0)
            chain.loop((B - 4) // 2, 14, turn)
            for g in range(B - 3, B):
                attention_step(g, g % 2)
            x1_rows(B - 1, 1)
            dve.wait_ge(c_out_ps, 1)
            dve.tensor_tensor(cx[0:B, 1, :], psL[1][0:B, 0:D], cx[0:B, 1, :], ALU.add).then_inc(c_x1, 1)
            dve.wait_ge(c_x1, 1)
            dve.wait_ge(x1_ready, B)

            def norm_x1(g, par):
                tail = isinstance(g, int) and g == B
                after(dve, x1T_ps, g - 1)
                after(dve, x1b_ready, g - 1)
                src = ((lambda j: cx[0:B, 1, :]) if tail else
                       (lambda j: x1[:, bass.ds(T * g + j, 1), :].rearrange("p o n -> p (o n)")))
                n, tiles = (B, 1) if tail else (P, T)
                normalize(dve, link, src, lambda j: xh[par][0:n, j, :], n, tiles, x_var, x_root, g + 1
                          ).then_inc(xh_ready, 1)

            def choose(g, par):
                tail = isinstance(g, int) and g == B
                n, tiles = (B, 1) if tail else (P, T)
                dve.wait_ge(lg_ps, g + 1)
                link(dve.tensor_tensor(lg[0:n, 0:tiles, :], psLG[0:n, 0:tiles * E].rearrange("p (t e) -> p t e", e=E),
                                       rb2_bc[0:n, :].rearrange("p (o e) -> p o e", o=1).to_broadcast([n, tiles, E]),
                                       ALU.add))
                apart(dve, dve_passed)
                for j in range(tiles):
                    ins = dve.max(top[0:n, j, :], lg[0:n, j, :])
                link(ins)
                dve.tensor_tensor(gap[0:n, 0:tiles, :], top[0:n, 0:tiles, 0:1], top[0:n, 0:tiles, 1:2],
                                  ALU.subtract).then_inc(lg_gap, 1)
                for j in range(tiles):
                    ins = dve.max_index(topi[0:n, j, :], top[0:n, j, :], lg[0:n, j, :])
                link(ins)
                link(dve.tensor_copy(topf[0:n, 0:tiles, :], topi[0:n, 0:tiles, 0:2]))
                if tail:
                    dve.memset(mask[:, :, :], 0.0)
                for k in range(2):
                    for j in range(tiles):
                        ins = dve.tensor_scalar(onehot[0:n, k, j, :], iota8[0:n, :], topf[0:n, j, k:k + 1], None,
                                                ALU.is_equal)
                link(ins)
                dve.tensor_tensor(mask[0:n, 0:tiles, :], onehot[0:n, 0, 0:tiles, :], onehot[0:n, 1, 0:tiles, :],
                                  ALU.add).then_inc(mask_ready, 1)

            def gates(g, par):
                tail = isinstance(g, int) and g == B
                n, tiles = (B, 1) if tail else (P, T)
                dve.wait_ge(lg_half, g + 1)
                dve.tensor_scalar(probs[0:n, 0, 0:tiles, :], half[0:n, 0:tiles, :], 0.5, 0.5, ALU.mult, ALU.add)
                link(dve.tensor_scalar(probs[0:n, 1, 0:tiles, :], half[0:n, 0:tiles, :], -0.5, 0.5, ALU.mult, ALU.add))
                for k in range(2):
                    ins = dve.tensor_tensor(weighed[0:n, k, 0:tiles, :], onehot[0:n, k, 0:tiles, :],
                                            probs[0:n, k, 0:tiles, :].to_broadcast([n, tiles, E]), ALU.mult)
                link(ins)
                dve.tensor_tensor(pay[par][0:n, 0:tiles, D + 1:PAY], weighed[0:n, 0, 0:tiles, :],
                                  weighed[0:n, 1, 0:tiles, :], ALU.add)
                if tail:
                    dve.tensor_scalar(pay[par][0:n, 0, D:D + 1], ids[0:n, 0, :], float(-B * SEQ - 1), float(SEQ),
                                      ALU.add, ALU.mult)
                else:
                    dve.tensor_copy(pay[par][:, :, D:D + 1], ids[:, :, :])
                    link(dve.tensor_scalar(ids[:, :, :], ids[:, :, :], float(SEQ), None, ALU.add))

            def settle(g, par):
                tail = isinstance(g, int) and g == B
                n, tiles = (B, 1) if tail else (P, T)
                dve.wait_ge(rk_ps, g + 1)
                rk = psRK[:, 0:(T + 1) * E].rearrange("p (t e) -> p t e", e=E)
                link(dve.tensor_tensor(rank[0:n, 0:tiles, :], rk[0:n, 0:tiles, :],
                                       used[0:n, :].rearrange("p (o e) -> p o e", o=1).to_broadcast([n, tiles, E]),
                                       ALU.add))
                dve.tensor_tensor(used, used, rk[:, T, :], ALU.add)
                for k in range(2):
                    ins = dve.tensor_tensor(placed[0:n, k, 0:tiles, :], onehot[0:n, k, 0:tiles, :],
                                            rank[0:n, 0:tiles, :], ALU.mult)
                link(ins)
                for k in range(2):
                    ins = dve.tensor_reduce(placef[0:n, k, 0:tiles, :], placed[0:n, k, 0:tiles, :], AX_X, ALU.add)
                link(ins)
                gates(g, par)
                dst = c_place[0:n, :].rearrange("p (k o) -> p k o", o=1) if tail else place[par][:, :, :]
                dve.tensor_copy(dst, placef[0:n, :, 0:tiles, 0]).then_inc(place_ready, 1)

            def finish_rows(g, par):
                tail = isinstance(g, int) and g == B
                n, tiles = (B, 1) if tail else (P, T)

                def hrow(j):
                    return cx[0:B, 0, :] if tail else h[:, bass.ds(T * g + j, 1), :].rearrange("p o n -> p (o n)")
                dve.wait_ge(x1b_ready, g + 1)
                for j in range(tiles):
                    dve.wait_ge(mlp_ps, T * g + j + 1)
                    ins = dve.tensor_tensor(x2[0:n, j, :], psO[j][0:n, 0:D], x1b[par][0:n, j, :], ALU.add)
                link(ins)
                link(normalize(dve, link, lambda j: x2[0:n, j, :], lambda j: x2[0:n, j, :], n, tiles,
                               m_var, m_root, 2 * g + 1))
                for j in range(tiles):
                    ins = dve.tensor_tensor(x2[0:n, j, :], x2[0:n, j, :], gamma_bc[0:n, :], ALU.mult)
                link(ins)
                for j in range(tiles):
                    ins = dve.tensor_tensor(hrow(j), hrow(j), x2[0:n, j, :], ALU.add)
                ins.then_inc(h1_ready, 1)
                dve.wait_ge(h1_ready, g + 1)
                done = scat0 if par == 0 else scat1
                if isinstance(g, int):
                    after(dve, done, 32 * T * (g // 2))
                else:
                    dve.wait_ge(done, (g - par) * (16 * T))
                after(dve, xmT_ps, g - 1)
                normalize(dve, link, hrow, lambda j: pay[par][0:n, j, 0:D], n, tiles, m_var, m_root, 2 * g + 2
                          ).then_inc(xm_ready, 1)

            norm_x1(0, 0)

            def routing_step(g, par):
                peeled = isinstance(g, int)
                if not peeled or 1 <= g <= B + 1:
                    finish_rows(g - 1, 1 - par)
                if not peeled or g >= 2:
                    choose(g - 2, par)
                if not peeled or g + 1 <= B:
                    norm_x1(g + 1, 1 - par)
                if not peeled or g >= 2:
                    settle(g - 2, par)
            for g in range(3):
                routing_step(g, g % 2)

            def turn(it):
                routing_step(2 * it + 3, 1)
                routing_step(2 * it + 4, 0)
            chain.loop(2, 2 * ROUTING_LINKS, turn)
            for g in range(7, B + 3):
                routing_step(g, g % 2)

            dve.tensor_copy(used_i[:, :], used)
            dve.tensor_tensor(count, used, region0[:, 0:E], ALU.subtract).then_inc(used_ready, 1)
            dve.wait_ge(used_ready, 1)
            link(dve.tensor_tensor(over[:, :, :], count.rearrange("p (e o) -> p e o", o=1).to_broadcast([P, E, 18]),
                                   limits.rearrange("p (o j) -> p o j", o=1).to_broadcast([P, E, 18]), ALU.is_gt))
            link(dve.tensor_reduce(tiles_e, over[:, :, :], AX_X, ALU.add))
            link(dve.tensor_tensor(lower[:, :, :], first_src[:, :, :],
                                   tiles_e.rearrange("p (o e) -> p o e", o=1).to_broadcast([P, E + 1, E]), ALU.mult))
            link(dve.tensor_reduce(first, lower[:, :, :], AX_X, ALU.add))
            link(dve.scalar_tensor_tensor(out=jump, in0=first, scalar=float(-P), in1=region0, op0=ALU.mult,
                                          op1=ALU.add))
            dve.memset(owner, 0.0)
            link(dve.tensor_scalar(rowt, tnum, float(P), None, ALU.mult))
            for e in range(1, E + 1):
                link(dve.tensor_scalar(step, tnum, first[:, e:e + 1], None, ALU.is_ge))
                if e < E:
                    dve.tensor_tensor(owner, owner, step, ALU.add)
                link(dve.tensor_tensor(lower[:, 0, 0:1], jump[:, e:e + 1], jump[:, e - 1:e], ALU.subtract))
                link(dve.scalar_tensor_tensor(out=rowt, in0=step, scalar=lower[:, 0, 0:1], in1=rowt, op0=ALU.mult,
                                              op1=ALU.add))
            link(dve.tensor_scalar(rowt, rowt, float(E * REGION), None, ALU.min))
            dve.tensor_copy(owner_i[:, :], owner)
            dve.tensor_copy(row_i[:, :], rowt).then_inc(tables_ready, 1)
            dve.wait_ge(tables_ready, 1)

            dve.wait_ge(b2_loaded, 16)
            dve.wait_ge(low_loaded, 16 * 2 * (E - 2))
            dve.wait_ge(high_loaded, 16 * 2 * 2)
            loaded = [xs_loaded0, xs_loaded1]

            def weights_in(i, par):
                e = dve.value_load(owner_i[0:1, bass.ds(i, 1)], min_val=0, max_val=E - 1)
                after(dve, h_ps, 2 * (i - 1))
                dve.tensor_copy(w1now[par].rearrange("p k n -> p (k n)").rearrange("p (o n) -> p o n", o=1),
                                experts[:, bass.ds(e, 1), 0:KD * HID]).then_inc(w1_ready, 1)
                after(dve, hT_sb, KH * (i - 1))
                dve.tensor_copy(b1now[par].rearrange("p (o k) -> p o k", o=1),
                                eb1T[:, bass.ds(e, 1), :]).then_inc(b1_ready, 1)

            def rows_in(i, par, turns):
                e = dve.value_load(owner_i[0:1, bass.ds(i, 1)], min_val=0, max_val=E - 1)
                dve.wait_ge(loaded[par], 16 * turns)
                after(dve, rows_added, 16 * (i - 1))
                dve.tensor_copy(gate_now[par], xs[par][:, bass.ds(e + (D + 1), 1)])
                dve.tensor_copy(slot_ids[par][:, :], xs[par][:, D:D + 1]).then_inc(slot_ready, 1)

            def tile_out(i, par):
                e = dve.value_load(owner_i[0:1, bass.ds(i, 1)], min_val=0, max_val=E - 1)
                dve.wait_ge(y_ps, i + 1)
                link(dve.tensor_tensor(ybias[par].rearrange("p (o n) -> p o n", o=1),
                                       psAT[par][:, 0:D].rearrange("p (o n) -> p o n", o=1),
                                       b2bc[:, bass.ds(e, 1), :], ALU.add))
                dve.tensor_scalar(y[par], ybias[par], gate_now[par], None, ALU.mult).then_inc(y_ready, 1)

            weights_in(0, 0)
            weights_in(1, 1)
            rows_in(0, 0, 1)

            def expert_step(i, par, turns):
                if not isinstance(i, int) or i + 2 < MOE_TILES:
                    weights_in(i + 2, par)
                if not isinstance(i, int) or i + 1 < MOE_TILES:
                    rows_in(i + 1, 1 - par, turns + par)
                tile_out(i, par)
            expert_step(0, 0, 1)
            expert_step(1, 1, 1)

            def turn(it):
                expert_step(2 * it + 2, 0, it + 2)
                expert_step(2 * it + 3, 1, it + 2)
            chain.loop(MOE_TILES // 2 - 2, 2, turn)
            expert_step(MOE_TILES - 2, 0, MOE_TILES // 2)
            expert_step(MOE_TILES - 1, 1, MOE_TILES // 2)

        @block.scalar
        def _(act):
            for dst, src in smalls:
                act.dma_start(dst, src).then_inc(smalls_loaded, 16)
            for dst, src in raws:
                act.dma_start(dst, src).then_inc(raw_loaded, 16)
            act.dma_start(rw1, t["L0_ffn_rw1"].rearrange("(k p) n -> p k n", p=P)).then_inc(direct_loaded, 16)
            act.dma_start(rw2, t["L0_ffn_rw2"].rearrange("(k p) n -> p k n", p=P)).then_inc(direct_loaded, 16)
            act.wait_ge(iota_ready, 1)
            for hh in range(HEADS):
                p0, c0 = HD * (hh % 8), FEAT * (hh % 8)
                act.dma_start(projbd[p0:p0 + HD, hh // 8, c0:c0 + FEAT],
                              t["L0_attn_proj"][hh]).then_inc(direct_loaded, 16)

            for u, (dst, blocks) in enumerate(turned):
                act.wait_ge(wT_ps, u + 1)
                src = psF[u % 2][:, :]
                if len(dst.shape) == 3:
                    src = src.rearrange("p (a n) -> p a n", a=dst.shape[1])
                act.copy(dst, src).then_inc(wT_sb, 1)
            act.wait_ge(wT_ps, len(turned) + 1)
            act.copy(cols, psF[len(turned) % 2][:, 0:84]).then_inc(wT_sb, 1)

            act.wait_ge(logits_ready, 1)
            act.activation(gate[:, 0:1], gate[:, 0:1], ACT.Exp, scale=-1.0)
            act.activation(gate[:, 1:10], gate[:, 1:10], ACT.Exp).then_inc(exps_ready, 1)

            act.wait_ge(c_done, 3)
            act.activation(c_kf[0:1, :], c_kf[0:1, :], ACT.Exp)
            act.activation(c_qf, c_qf, ACT.Exp).then_inc(act_step, 1)

            def tokens_T(g, par):
                act.wait_ge(xT_ps, g + 1)
                after(act, v_ps, g - 1)
                act.copy(xnT[par][:, :, :], psT[:, :].rearrange("p (k n) -> p k n", k=KD)).then_inc(xT_sb, 1)

            def q_T(g, par):
                act.wait_ge(q_ps, g + 1)
                after(act, f_ps, 8 * (g - 1))
                act.copy(qT[par][:, :, :], psL[1][:, :].rearrange("p (k n) -> p k n", k=KD)).then_inc(q_sb, 1)

            def k_T(g, par):
                act.wait_ge(k_ps, g + 1)
                act.copy(kT[par][:, :, :], psL[0][:, :].rearrange("p (k n) -> p k n", k=KD)).then_inc(k_sb, 1)

            def att_T(g, par):
                act.wait_ge(attT_ps, g + 1)
                act.copy(attT[par][:, :, :], psT[:, :].rearrange("p (k n) -> p k n", k=KD)).then_inc(attT_sb, 1)

            tokens_T(0, 0)
            q_T(0, 0)
            k_T(0, 0)
            tokens_T(1, 1)

            def attention_step(g, par):
                peeled = isinstance(g, int)

                def bank_out(i):
                    u = 8 * g + i
                    act.wait_ge(f_neg, u + 1)
                    after(act, f_sum, u - 3)
                    act.activation(lin[i % 4], psF[i % 2][:, :], ACT.Relu).then_inc(f_read, 1)
                    act.activation(feature_rows(par, i), feature_rows(par, i), ACT.Exp).then_inc(f_exp, 1)
                bank_out(0)
                bank_out(1)
                if not peeled or g + 1 < B:
                    q_T(g + 1, 1 - par)
                bank_out(2)
                bank_out(3)
                if not peeled or g >= 1:
                    att_T(g - 1, 1 - par)
                if not peeled or g + 1 < B:
                    k_T(g + 1, 1 - par)
                bank_out(4)
                bank_out(5)
                if not peeled or g + 2 < B:
                    tokens_T(g + 2, par)
                bank_out(6)
                bank_out(7)

            attention_step(0, 0)
            with act.Fori(0, (B - 4) // 2) as it:
                attention_step(2 * it + 1, 1)
                attention_step(2 * it + 2, 0)
            for g in range(B - 3, B):
                attention_step(g, g % 2)
            att_T(B - 1, 1)
            act.wait_ge(cattT_ps, 1)
            act.copy(c_attT[:, :, :], psT[:, 0:KD * B].rearrange("p (k n) -> p k n", k=KD)).then_inc(cattT_sb, 1)
            act.wait_ge(c_x1, 1)
            act.wait_ge(x1_ready, B)

            def x1_T(g, par):
                tail = isinstance(g, int) and g == B
                n = B if tail else IMG
                act.wait_ge(x1T_ps, g + 1)
                for k in range(KD):
                    ins = act.activation(x1T[par][:, k, 0:n], psT[:, k * IMG:k * IMG + n], ACT.Identity,
                                         bias=betaT[:, k:k + 1], scale=gammaT[:, k:k + 1])
                ins.then_inc(x1T_sb, 1)

            def xm_T(g, par):
                tail = isinstance(g, int) and g == B
                n = B if tail else IMG
                act.wait_ge(xmT_ps, g + 1)
                act.copy(xmT[par][:, :, 0:n], psT[:, :].rearrange("p (k n) -> p k n", k=KD)[:, :, 0:n]
                         ).then_inc(xmT_sb, 1)

            def hidden(g, first_use, func, bias, dst, n):
                for i in range(4):
                    act.wait_ge(m_ps, first_use + i + 1)
                    for m in range(2):
                        ins = act.activation(dst[:, 2 * i + m, 0:n], psF[i % 2][:, m * IMG:m * IMG + n], func,
                                             bias=bias[:, 2 * i + m:2 * i + m + 1])
                    ins.then_inc(m_sb, 1)

            x1_T(0, 0)

            def routing_step(g, par):
                peeled = isinstance(g, int)
                if not peeled or g <= B:
                    n = B if peeled and g == B else IMG
                    hidden(g, 8 * g - 4 if not peeled or g else 0, ACT.Gelu, b1T, gT, n)
                if not peeled or 1 <= g <= B + 1:
                    n = B if peeled and g - 1 == B else IMG
                    xm_T(g - 1, 1 - par)
                    hidden(g - 1, 8 * g if not peeled or g <= B else 8 * g - 4, ACT.Silu, rb1T, rT, n)
                if not peeled or g + 1 <= B:
                    x1_T(g + 1, 1 - par)
                if not peeled or g >= 2:
                    tiles, rows = (1, B) if peeled and g - 2 == B else (T, P)
                    act.wait_ge(lg_gap, g - 1)
                    act.activation(half[0:rows, 0:tiles, :], gap[0:rows, 0:tiles, :], ACT.Tanh, scale=0.5
                                   ).then_inc(lg_half, 1)
            for g in range(3):
                routing_step(g, g % 2)
            with act.Fori(0, 2) as it:
                routing_step(2 * it + 3, 1)
                routing_step(2 * it + 4, 0)
            for g in range(7, B + 3):
                routing_step(g, g % 2)

            def rows_T(i, par):
                act.wait_ge(xsT_ps, i + 1)
                act.copy(xsT[par], psT[:, 0:D]).then_inc(xsT_sb, 1)

            def hidden_rows(i, par):
                act.wait_ge(b1_ready, i + 1)
                for c in range(2):
                    act.wait_ge(h_ps, 2 * i + c + 1)
                    for m in range(4):
                        k = 4 * c + m
                        act.activation(hT[par][:, k, :], psUP[par][c][:, P * m:P * m + P], ACT.Silu,
                                       bias=b1now[par][:, k:k + 1]).then_inc(hT_sb, 1)

            rows_T(0, 0)
            rows_T(1, 1)
            hidden_rows(0, 0)

            def expert_step(i, par):
                if not isinstance(i, int) or i + 1 < MOE_TILES:
                    hidden_rows(i + 1, 1 - par)
                if not isinstance(i, int) or i + 2 < MOE_TILES:
                    rows_T(i + 2, par)
            expert_step(0, 0)
            expert_step(1, 1)
            with act.Fori(0, MOE_TILES // 2 - 2) as it:
                expert_step(2 * it + 2, 0)
                expert_step(2 * it + 3, 1)
            expert_step(MOE_TILES - 2, 0)
            expert_step(MOE_TILES - 1, 1)

        @block.tensor
        def _(pe):
            def mm(out, lhsT, rhs, start=True, stop=True, **kw):
                return pe.matmul(out, lhsT, rhs, start=start, stop=stop, **kw)

            pe.wait_ge(consts_ready, 1)
            pe.wait_ge(raw_loaded, 16 * len(raws))
            for u, (_, blocks) in enumerate(turned):
                after(pe, wT_sb, u - 1)
                for i, src in enumerate(blocks):
                    ins = pe.transpose(psF[u % 2][:, P * i:P * i + P], src, ident)
                ins.then_inc(wT_ps, 1)
            pe.wait_ge(wT_sb, len(turned) - 1)
            pe.transpose(psF[len(turned) % 2][:, 0:84], raw_cols[0:84, :], ident[0:84, 0:84]).then_inc(wT_ps, 1)

            pe.wait_ge(dots_ready, 1)
            mm(psT[:, 0:10], same, dots).then_inc(totals_ready, 1)

            pe.wait_ge(c_norm, 1)
            for k in range(KD):
                ins = pe.transpose(psT[:, k:k + 1], cx[0:1, 1, k * P:k * P + P], ident[0:1, 0:1])
            ins.then_inc(c_ps, 1)
            pe.wait_ge(c_done, 1)
            pe.wait_ge(wT_sb, len(turned) + 1)
            for i in range(4):
                for k in range(KD):
                    mm(psT[:, 4 + i:5 + i], wqkvT[:, k, P * i:P * i + P], c_xT[:, k:k + 1], k == 0, k == KD - 1)
            for k in range(KD):
                ins = mm(psL[0][0:1, 0:D], c_xT[:, k:k + 1], wqkvT[:, k, 2 * D:3 * D], k == 0, k == KD - 1)
            ins.then_inc(c_ps, 1)
            pe.wait_ge(c_done, 2)
            pe.wait_ge(direct_loaded, 16 * (2 + HEADS))
            for c in range(2):
                mm(psF[c][0:1, :], c_kT[:, c:c + 1], projbd[:, c, :])
            for m in range(PAIRS):
                ins = mm(psL[1][:, m:m + 1], projbd[:, m // 4, P * (m % 4):P * (m % 4) + P], c_qT[:, m // 4:m // 4 + 1])
            ins.then_inc(c_ps, 1)

            def tokens_T(g, par):
                pe.wait_ge(ln_ready, g + 1)
                after(pe, xT_sb, g)
                after(pe, attT_sb, g - 2)
                for j in range(T):
                    for k in range(KD):
                        ins = pe.transpose(psT[:, k * IMG + j * P:k * IMG + j * P + P],
                                           xn[par][:, j, k * P:k * P + P], ident)
                ins.then_inc(xT_ps, 1)

            def qk(g, par, half_):
                if half_:
                    dst, done = psL[0], k_ps
                else:
                    dst, done = psL[1], q_ps
                    pe.wait_ge(xT_sb, g + 1)
                    after(pe, v_sb, g)
                for m in range(KD):
                    c0 = D * half_ + P * m
                    for k in range(KD):
                        ins = mm(dst[:, m * IMG:(m + 1) * IMG], wqkvT[:, k, c0:c0 + P], xnT[par][:, k, :],
                                 k == 0, k == KD - 1)
                ins.then_inc(done, 1)

            def values(g, par):
                pe.wait_ge(q_sb, g + 1)
                for j in range(T):
                    for k in range(KD):
                        ins = mm(psL[1][:, j * D:(j + 1) * D], xnT[par][:, k, j * P:j * P + P],
                                 wqkvT[:, k, 2 * D:3 * D], k == 0, k == KD - 1)
                ins.then_inc(v_ps, 1)

            def features(g, par, i):
                u = 8 * g + i
                after(pe, f_read, u - 1)
                if i < 4:
                    ins = mm(psF[i % 2][:, :], kT[par][:, i % 2, (i // 2) * P:(i // 2) * P + P], projbd[:, i % 2, :])
                else:
                    for m in range(2):
                        pair = 2 * (i - 4) + m
                        c0 = P * (pair % 4)
                        ins = mm(psF[i % 2][:, m * IMG:(m + 1) * IMG], projbd[:, pair // 4, c0:c0 + P],
                                 qT[par][:, pair // 4, :])
                ins.then_inc(f_ps, 1)

            def att_T(g, par):
                pe.wait_ge(att_ready, (T + 1) * g + T)
                pe.wait_ge(xT_sb, g + 3 if not isinstance(g, int) or g + 3 <= B else B)
                for j in range(T):
                    for k in range(KD):
                        ins = pe.transpose(psT[:, k * IMG + j * P:k * IMG + j * P + P],
                                           att[par][:, j, k * P:k * P + P], ident)
                ins.then_inc(attT_ps, 1)

            def out_rows(g, par):
                pe.wait_ge(attT_sb, g + 1)
                pe.wait_ge(k_sb, g + 3 if not isinstance(g, int) or g + 3 <= B else B)
                for j in range(T):
                    for k in range(KD):
                        ins = mm(psL[0][:, j * D:(j + 1) * D], attT[par][:, k, j * P:j * P + P], woT[:, k, :],
                                 k == 0, k == KD - 1)
                ins.then_inc(out_ps, 1)

            def key_values(g, par):
                pe.wait_ge(f_sum, 8 * g + 4)
                pe.wait_ge(v_sb, g + 1)
                after(pe, att_ready, (T + 1) * g)
                for m in range(PAIRS):
                    c0 = P * (m % 4)
                    o = psKV[:, m * PW:(m + 1) * PW]
                    for j in range(T):
                        mm(o, kf[par][:, j, m // 4, c0:c0 + P],
                           va[par][:, j, 2 * m:2 * m + 2, :].rearrange("p h d -> p (h d)"),
                           m == 0 and j == 0, False, skip_group_check=True)
                    ins = mm(o, c_kf[0:1, m * P:m * P + P],
                             c_va[0:1, 2 * m:2 * m + 2, :].rearrange("p h d -> p (h d)"), False, m == PAIRS - 1,
                             skip_group_check=True)
                ins.then_inc(kv_ps, 1)

            def attend(g, par):
                pe.wait_ge(f_sum, 8 * g + 8)
                pe.wait_ge(kvbd_ready, g + 1)
                for j in range(T + 1):
                    for m in range(PAIRS):
                        if j < T:
                            o, lhsT = psAT[j][:, m * PW:(m + 1) * PW], qf[par][:, m, j * P:j * P + P]
                        else:
                            o, lhsT = psKV[0:1, m * PW:(m + 1) * PW], c_qf[:, m:m + 1]
                        ins = mm(o, lhsT, kvbd[par][:, m, :])
                    ins.then_inc(attn_ps, 1)

            tokens_T(0, 0)
            pe.wait_ge(c_done, 4)
            qk(0, 0, 0)
            qk(0, 0, 1)
            tokens_T(1, 1)
            values(0, 0)

            def attention_step(g, par):
                peeled = isinstance(g, int)
                pe.wait_ge(k_sb, g + 1)
                features(g, par, 0)
                features(g, par, 1)
                if not peeled or g + 1 < B:
                    qk(g + 1, 1 - par, 0)
                features(g, par, 2)
                features(g, par, 3)
                if not peeled or g >= 1:
                    att_T(g - 1, 1 - par)
                if not peeled or g + 1 < B:
                    qk(g + 1, 1 - par, 1)
                features(g, par, 4)
                features(g, par, 5)
                if not peeled or g + 2 < B:
                    tokens_T(g + 2, par)
                if not peeled or g >= 1:
                    out_rows(g - 1, 1 - par)
                features(g, par, 6)
                features(g, par, 7)
                key_values(g, par)
                if not peeled or g + 1 < B:
                    values(g + 1, 1 - par)
                attend(g, par)

            attention_step(0, 0)
            with pe.Fori(0, (B - 4) // 2) as it:
                attention_step(2 * it + 1, 1)
                attention_step(2 * it + 2, 0)
            for g in range(B - 3, B):
                attention_step(g, g % 2)
            att_T(B - 1, 1)
            out_rows(B - 1, 1)
            pe.wait_ge(catt_moved, 16)
            for k in range(KD):
                ins = pe.transpose(psT[:, k * B:(k + 1) * B], cx[0:B, 2, k * P:k * P + P], ident[0:B, 0:B])
            ins.then_inc(cattT_ps, 1)
            pe.wait_ge(cattT_sb, 1)
            for k in range(KD):
                ins = mm(psL[1][0:B, 0:D], c_attT[:, k, :], woT[:, k, :], k == 0, k == KD - 1)
            ins.then_inc(c_out_ps, 1)

            def x1_T(g, par):
                tail = isinstance(g, int) and g == B
                n, tiles = (B, 1) if tail else (P, T)
                pe.wait_ge(xh_ready, g + 1)
                after(pe, xmT_sb, g - 1)
                after(pe, x1T_sb, g)
                for j in range(tiles):
                    for k in range(KD):
                        ins = pe.transpose(psT[:, k * IMG + j * P:k * IMG + j * P + n],
                                           xh[par][0:n, j, k * P:k * P + P], ident[0:n, 0:n])
                ins.then_inc(x1T_ps, 1)

            def xm_T(g, par):
                tail = isinstance(g, int) and g == B
                n, tiles = (B, 1) if tail else (P, T)
                pe.wait_ge(xm_ready, g + 1)
                after(pe, x1T_sb, g + 2 if not isinstance(g, int) or g + 2 <= B else B + 1)
                for j in range(tiles):
                    for k in range(KD):
                        ins = pe.transpose(psT[:, k * IMG + j * P:k * IMG + j * P + n],
                                           pay[par][0:n, j, k * P:k * P + P], ident[0:n, 0:n])
                ins.then_inc(xmT_ps, 1)

            def hidden(first_use, w, src, n):
                for i in range(4):
                    after(pe, m_sb, first_use + i - 1)
                    for m in range(2):
                        c0 = P * (2 * i + m)
                        for k in range(KD):
                            ins = mm(psF[i % 2][:, m * IMG:m * IMG + n], w[:, k, c0:c0 + P], src[:, k, 0:n],
                                     k == 0, k == KD - 1)
                    ins.then_inc(m_ps, 1)

            def mlp_out(g, par, j, first_use):
                tail = isinstance(g, int) and g == B
                n = B if tail else P
                if j == 0:
                    pe.wait_ge(m_sb, first_use + 4)
                    after(pe, h1_ready, g)
                for k in range(KH):
                    ins = mm(psO[j][0:n, 0:D], gT[:, k, j * P:j * P + n], w2T[:, k, :], k == 0, k == KH - 1)
                ins.then_inc(mlp_ps, 1)

            def router_out(g, par, first_use):
                tail = isinstance(g, int) and g == B
                n, tiles = (B, 1) if tail else (P, T)
                pe.wait_ge(m_sb, first_use + 4)
                for j in range(tiles):
                    for k in range(KH):
                        ins = mm(psLG[0:n, j * E:(j + 1) * E], rT[:, k, j * P:j * P + n], rw2[:, k, :],
                                 k == 0, k == KH - 1)
                ins.then_inc(lg_ps, 1)

            def ranks(g):
                pe.wait_ge(mask_ready, g + 1)
                mm(psRK[:, 0:E], before, mask[:, 0, :])
                mm(psRK[:, E:2 * E], before, mask[:, 1, :], True, False)
                mm(psRK[:, E:2 * E], ones, mask[:, 0, :], False, True)
                mm(psRK[:, 2 * E:3 * E], ones, mask[:, 0, :], True, False)
                mm(psRK[:, 2 * E:3 * E], ones, mask[:, 1, :], False, True).then_inc(rk_ps, 1)

            pe.wait_ge(c_x1, 1)
            x1_T(0, 0)

            def routing_step(g, par):
                peeled = isinstance(g, int)
                mlp_use = 8 * g - 4 if not peeled or g else 0

                def router_use(g):
                    return 8 * g if not isinstance(g, int) or g <= B else 8 * g - 4
                if not peeled or g <= B:
                    pe.wait_ge(x1T_sb, g + 1)
                    hidden(mlp_use, w1T, x1T[par], B if peeled and g == B else IMG)
                if not peeled or g >= 2:
                    router_out(g - 2, par, router_use(g - 1))
                if not peeled or 1 <= g <= B + 1:
                    xm_T(g - 1, 1 - par)
                    pe.wait_ge(xmT_sb, g)
                    hidden(router_use(g), rw1, xmT[1 - par], B if peeled and g - 1 == B else IMG)
                if not peeled or g + 1 <= B:
                    x1_T(g + 1, 1 - par)
                if not peeled or g >= 2:
                    ranks(g - 2)
                if not peeled or g <= B:
                    for j in range(1 if peeled and g == B else T):
                        mlp_out(g, par, j, mlp_use)
            for g in range(3):
                routing_step(g, g % 2)
            with pe.Fori(0, 2) as it:
                routing_step(2 * it + 3, 1)
                routing_step(2 * it + 4, 0)
            for g in range(7, B + 3):
                routing_step(g, g % 2)

            loaded = [xs_loaded0, xs_loaded1]
            pe.wait_ge(tables_ready, 1)

            def weights(e, c0, n):
                return experts[:, bass.ds(e, 1), c0:c0 + n].rearrange("p o n -> p (o n)")

            def rows_T(i, par, turns):
                pe.wait_ge(loaded[par], 16 * turns)
                after(pe, xsT_sb, i)
                for k in range(KD):
                    ins = pe.transpose(psT[:, k * P:(k + 1) * P], xs[par][:, k * P:k * P + P], ident)
                ins.then_inc(xsT_ps, 1)

            def up(i, par):
                pe.wait_ge(w1_ready, i + 1)
                pe.wait_ge(xsT_sb, i + 1)
                after(pe, hT_sb, KH * (i - 1))
                for c in range(2):
                    for m in range(4):
                        c0 = P * (4 * c + m)
                        for k in range(KD):
                            ins = mm(psUP[par][c][:, P * m:P * m + P], w1now[par][:, k, c0:c0 + P],
                                     xsT[par][:, k * P:k * P + P], k == 0, k == KD - 1)
                    ins.then_inc(h_ps, 1)

            def down(i, par):
                e = pe.value_load(owner_i[0:1, bass.ds(i, 1)], min_val=0, max_val=E - 1)
                pe.wait_ge(hT_sb, KH * (i + 1))
                after(pe, y_ready, i - 1)
                for k in range(KH):
                    ins = mm(psAT[par][:, 0:D], hT[par][:, k, :], weights(e, KD * HID + k * D, D), k == 0, k == KH - 1)
                ins.then_inc(y_ps, 1)

            rows_T(0, 0, 1)
            rows_T(1, 1, 1)
            pe.wait_ge(low_loaded, 16 * 2 * (E - 2))
            pe.wait_ge(high_loaded, 16 * 2 * 2)
            up(0, 0)

            def expert_step(i, par, turns):
                if not isinstance(i, int) or i + 1 < MOE_TILES:
                    up(i + 1, 1 - par)
                if not isinstance(i, int) or i + 2 < MOE_TILES:
                    rows_T(i + 2, par, turns + 1)
                down(i, par)
            expert_step(0, 0, 1)
            expert_step(1, 1, 1)
            with pe.Fori(0, MOE_TILES // 2 - 2) as it:
                expert_step(2 * it + 2, 0, it + 2)
                expert_step(2 * it + 3, 1, it + 2)
            expert_step(MOE_TILES - 2, 0, MOE_TILES // 2)
            expert_step(MOE_TILES - 1, 1, MOE_TILES // 2)


_INS = ["x", "cls_tok", "L0_tok_Wa", "L0_tok_ba", "L0_tok_Wd1", "L0_tok_bd1", "L0_tok_Wd2", "L0_tok_bd2",
        "L0_tok_Wd3", "L0_tok_bd3", "L0_attn_proj", "L0_attn_w_qkv", "L0_attn_w_out", "L0_attn_b_out",
        "L0_attn_gamma", "L0_attn_beta", "L0_attn_w1", "L0_attn_b1", "L0_attn_w2", "L0_attn_b2",
        "L0_ffn_rw1", "L0_ffn_rb1", "L0_ffn_rw2", "L0_ffn_rb2", "L0_ffn_w1", "L0_ffn_b1", "L0_ffn_w2", "L0_ffn_b2"]


def kernel(**inputs):
    import numpy as _np
    import concourse.bacc as _bacc
    from concourse import mybir as _mybir
    from concourse.bass_utils import run_bass_kernel_spmd as _run

    nc = _bacc.Bacc("TRN2", target_bir_lowering=False, num_devices=1)
    arrays, tensors = {}, {}
    for name in _INS:
        a = _np.ascontiguousarray(inputs[name])
        arrays[f"in_{name}"] = a
        tensors[name] = nc.dram_tensor(f"in_{name}", a.shape, _mybir.dt.from_np(a.dtype), kind="ExternalInput").ap()
    tensors["out"] = nc.dram_tensor("out_tokens", (B, SEQ, D), F32, kind="ExternalOutput").ap()
    build(nc, tensors)
    r = _run(nc, [arrays], core_ids=[0])
    return r.results[0]["out_tokens"]
```

```python
from contextlib import ExitStack

import concourse.bass as bass
from concourse import mybir

F32 = mybir.dt.float32
U32 = mybir.dt.uint32
I32 = mybir.dt.int32
ACT = mybir.ActivationFunctionType
ALU = mybir.AluOpType
AX_X = mybir.AxisListType.X

P = 128
B, IMG = 8, 256
D = IMG
SEQ = IMG + 1
HEADS, HD, FEAT = 16, 16, 64
PAIRS = HEADS // 2
HID = 4 * D
E = 8
KD = D // P
KH = HID // P
T = 2
EPS_LN, EPS_ATTN = 1e-5, 1e-8
TOKENS = B * SEQ
STRIPS = P // B
ROWS = IMG // STRIPS
REGION = 18 * P
MOE_TILES = (2 * TOKENS + E * (P - 1)) // P
PAY = D + 1 + E
VA = HD + 1
PW = 2 * VA
EXPERT = KD * HID + KH * D
LOW_LOADED = 16 * 2 * (E - 2)
ALL_LOADED = 16 * 2 * E
TURNED_FIRST = 4
ROUTING_LINKS = 17


class Chain:

    def __init__(self, eng, sem):
        self.eng, self.sem, self.n, self.base = eng, sem, 0, 0

    def link(self, ins):
        self.n += 1
        ins.then_inc(self.sem, 1)
        self.eng.wait_ge(self.sem, self.base + self.n)

    def loop(self, count, links, body):
        n = self.n
        with self.eng.Fori(0, count) as it:
            self.base = it * links
            body(it)
        assert self.n - n == links, (self.n - n, links)
        self.n, self.base = n + count * links, 0


def apart(eng, passed):
    eng.sem_inc(passed, 1)


def after(eng, sem, value):
    if not isinstance(value, int) or value > 0:
        eng.wait_ge(sem, value)


def build(nc, t):
    xs_d = nc.dram_tensor("routed_rows", (E * REGION + P, PAY), F32, kind="Internal").ap()
    pads_d = nc.dram_tensor("pad_rows", (P + B, PAY), F32, kind="Internal").ap()
    sums = t["out"].rearrange("b q n -> (b q) n")

    with ExitStack() as ctx:
        def sb(name, shape, dt=F32):
            return ctx.enter_context(nc.sbuf_tensor(name, shape, dt))

        def sem(name):
            return ctx.enter_context(nc.semaphore(name))

        arena = sb("arena", [P, E * EXPERT])
        dense = sb("dense", [P, 9280])
        h = sb("h", [P, B * T, D])
        x1 = sb("x1", [P, B * T, D])
        small = sb("small", [P, 2124])

        cut_at = [0]

        def cut(tensor, width):
            a = cut_at[0]
            cut_at[0] += width
            assert cut_at[0] <= tensor.shape[1], (cut_at[0], tensor.shape)
            return tensor[:, a:a + width]

        def at(tensor):
            cut_at[0] = tensor

        at(0)
        wqkvT = cut(dense, KD * 3 * D).rearrange("p (k n) -> p k n", k=KD)
        woT = cut(dense, KD * D).rearrange("p (k n) -> p k n", k=KD)
        w1T = cut(dense, KD * HID).rearrange("p (k n) -> p k n", k=KD)
        w2T = cut(dense, KH * D).rearrange("p (k n) -> p k n", k=KH)
        rw1 = cut(dense, KD * HID).rearrange("p (k n) -> p k n", k=KD)
        projbd = cut(dense, KD * 8 * FEAT).rearrange("p (k n) -> p k n", k=KD)
        rw2 = cut(dense, KH * E).rearrange("p (k n) -> p k n", k=KH)

        at(0)
        xs = [cut(dense, PAY) for _ in range(2)]
        xsT = [cut(dense, D) for _ in range(2)]
        w1now = [cut(dense, KD * HID).rearrange("p (k n) -> p k n", k=KD) for _ in range(2)]
        hT = [cut(dense, HID).rearrange("p (k n) -> p k n", k=KH) for _ in range(2)]
        ybias = [cut(dense, D) for _ in range(2)]
        y = [cut(dense, D) for _ in range(2)]

        at(0)
        img = cut(arena, ROWS * IMG)
        lohi = cut(arena, ROWS * IMG)
        det = {1: cut(arena, 3 * 1024)}
        app = {1: cut(arena, 1024)}
        det[2], app[2] = cut(arena, 3 * 256), cut(arena, 256)
        det[3], app[3] = cut(arena, 3 * 64), cut(arena, 64)
        wd = {2: cut(arena, 9 * 256)}
        at(16384)
        wd[1] = cut(arena, 9 * 1024)
        wd[3] = cut(arena, 9 * 64)
        wa = cut(arena, 64)
        raw_qkv = cut(arena, 6 * D).rearrange("p (m n) -> p m n", m=6)
        raw_o = cut(arena, KD * D).rearrange("p (m n) -> p m n", m=KD)
        raw_w1 = cut(arena, KH * D).rearrange("p (m n) -> p m n", m=KH)
        raw_w2 = cut(arena, KD * HID).rearrange("p (m n) -> p m n", m=KD)
        raw_cols = cut(arena, P)

        at(0)
        kf = [cut(arena, T * HEADS * FEAT).rearrange("p (t c n) -> p t c n", t=T, c=KD) for _ in range(2)]
        xn = [cut(arena, T * D).rearrange("p (t n) -> p t n", t=T) for _ in range(2)]
        xnb = [cut(arena, T * D).rearrange("p (t n) -> p t n", t=T) for _ in range(2)]
        xnT = [cut(arena, KD * IMG).rearrange("p (k n) -> p k n", k=KD) for _ in range(2)]
        qT = [cut(arena, KD * IMG).rearrange("p (k n) -> p k n", k=KD) for _ in range(2)]
        kT = [cut(arena, KD * IMG).rearrange("p (k n) -> p k n", k=KD) for _ in range(2)]
        va = [cut(arena, T * HEADS * VA).rearrange("p (t h d) -> p t h d", t=T, h=HEADS) for _ in range(2)]
        qf = [cut(arena, PAIRS * IMG).rearrange("p (m n) -> p m n", m=PAIRS) for _ in range(2)]
        kvbd = cut(arena, B * PAIRS * PW).rearrange("p (b m n) -> p b m n", b=B, m=PAIRS)
        att = [cut(arena, T * D).rearrange("p (t n) -> p t n", t=T) for _ in range(2)]
        attT = [cut(arena, KD * IMG).rearrange("p (k n) -> p k n", k=KD) for _ in range(2)]
        catt = cut(arena, B * D).rearrange("p (b n) -> p b n", b=B)
        c_va = cut(arena, HEADS * VA).rearrange("p (h d) -> p h d", h=HEADS)
        c_kf = cut(arena, HEADS * FEAT)
        c_kl = cut(arena, HEADS * FEAT)
        c_kv = cut(arena, PAIRS * PW).rearrange("p (m n) -> p m n", m=PAIRS)
        c_den = cut(arena, PAIRS * B * 2).rearrange("p (m b h) -> p m b h", m=PAIRS, b=B)
        t_mv = [cut(arena, T * 2).rearrange("p (t n) -> p t n", t=T) for _ in range(2)]
        t_rstd = [cut(arena, T).rearrange("p (t n) -> p t n", t=T) for _ in range(2)]
        lin = [cut(arena, 512) for _ in range(4)]

        at(0)
        xh = [cut(dense, T * D).rearrange("p (t n) -> p t n", t=T) for _ in range(2)]
        x2 = cut(dense, T * D).rearrange("p (t n) -> p t n", t=T)
        at(KD * (3 * D + D + HID + D * KH // KD + HID))
        x1b = [cut(dense, T * D).rearrange("p (t n) -> p t n", t=T) for _ in range(2)]
        at((E - 2) * EXPERT)
        x1T = [cut(arena, KD * IMG).rearrange("p (k n) -> p k n", k=KD) for _ in range(2)]
        gT = cut(arena, KH * IMG).rearrange("p (k n) -> p k n", k=KH)
        pay = [None, cut(arena, T * PAY).rearrange("p (t n) -> p t n", t=T)]
        at((E - 1) * EXPERT)
        rT = cut(arena, KH * IMG).rearrange("p (k n) -> p k n", k=KH)
        pay[0] = cut(arena, T * PAY).rearrange("p (t n) -> p t n", t=T)
        xmT = [cut(arena, KD * IMG).rearrange("p (k n) -> p k n", k=KD) for _ in range(2)]

        experts = arena[:, :].rearrange("p (e n) -> p e n", e=E)
        b2bc = x1[:, 0:E, :]

        at(0)
        ident = cut(small, P)
        same = cut(small, P)
        before = cut(small, P)
        ones = cut(small, P)
        gamma_bc, beta_bc, beta2_bc, bout_bc = (cut(small, D) for _ in range(4))
        cols = cut(small, E * KH + 2 * KH + 2 * KD)
        eb1T = cols[:, 0:E * KH].rearrange("p (e k) -> p e k", e=E)
        b1T, rb1T = cols[:, 64:72], cols[:, 72:80]
        gammaT, betaT = cols[:, 80:82], cols[:, 82:84]
        gate_now = [cut(small, 1) for _ in range(2)]
        b1now = [cut(small, KH) for _ in range(2)]
        dots = cut(small, 10)
        bd = cut(small, 10)
        gate = cut(small, 10)
        gsc = cut(small, 24)
        stats = cut(small, T * 6).rearrange("p (t n) -> p t n", t=T)
        mv = cut(small, T * 2).rearrange("p (t n) -> p t n", t=T)
        rstd = cut(small, T).rearrange("p (t n) -> p t n", t=T)
        neg_half = cut(small, T).rearrange("p (t n) -> p t n", t=T)
        den = cut(small, T * HEADS).rearrange("p (t h) -> p t h", t=T)
        c_xT, c_qT, c_kT = (cut(small, KD) for _ in range(3))
        c_qf, c_ql = cut(small, PAIRS), cut(small, PAIRS)
        rb2_bc = cut(small, E)
        iota8 = cut(small, E)
        lg = cut(small, T * E).rearrange("p (t e) -> p t e", t=T)
        top = cut(small, T * 8).rearrange("p (t e) -> p t e", t=T)
        topf = cut(small, T * 2).rearrange("p (t e) -> p t e", t=T)
        gap = cut(small, T).rearrange("p (t n) -> p t n", t=T)
        half = cut(small, T).rearrange("p (t n) -> p t n", t=T)
        probs = cut(small, 2 * T).rearrange("p (k t n) -> p k t n", k=2, t=T)
        onehot = cut(small, 2 * T * E).rearrange("p (k t e) -> p k t e", k=2, t=T)
        mask = cut(small, T * E).rearrange("p (t e) -> p t e", t=T)
        weighed = cut(small, 2 * T * E).rearrange("p (k t e) -> p k t e", k=2, t=T)
        rank = cut(small, T * E).rearrange("p (t e) -> p t e", t=T)
        placed = cut(small, 2 * T * E).rearrange("p (k t e) -> p k t e", k=2, t=T)
        placef = cut(small, 2 * T).rearrange("p (k t n) -> p k t n", k=2, t=T)
        used = cut(small, E)
        ids = cut(small, T).rearrange("p (t n) -> p t n", t=T)
        topi = sb("topi", [P, T, 8], U32)
        place = [sb(f"place{i}", [P, 2, T], U32) for i in range(2)]
        c_place = sb("c_place", [P, 2], U32)
        slot_ids = [sb(f"slot_ids{i}", [P, 1], U32) for i in range(2)]
        cx = sb("cx", [B, 3, D])
        c_attT = sb("c_attT", [P, KD, B])
        c_pay = cx[:, 1:3, :].rearrange("p a n -> p (a n)")[:, 0:PAY].rearrange("p (o n) -> p o n", o=1)
        limits = cut(small, 18)
        tnum = cut(small, MOE_TILES)
        region0 = cut(small, E + 1)
        first_src = cut(small, (E + 1) * E).rearrange("p (a e) -> p a e", a=E + 1)
        at(2 * (PAY + D + KD * HID + HID + D + D))
        over = cut(dense, E * 18).rearrange("p (e j) -> p e j", e=E)
        count = cut(dense, E)
        tiles_e = cut(dense, E)
        lower = cut(dense, (E + 1) * E).rearrange("p (a e) -> p a e", a=E + 1)
        first = cut(dense, E + 1)
        steps = cut(dense, E * MOE_TILES).rearrange("p (e i) -> p e i", e=E)
        owner = cut(dense, MOE_TILES)
        high = cut(dense, MOE_TILES)
        rowt = cut(dense, MOE_TILES)
        jump = cut(dense, E + 1)
        jumps = cut(dense, E)
        owner_i, row_i, need_i = (cut(dense, MOE_TILES).bitcast(I32) for _ in range(3))
        pad_from = cut(dense, E).bitcast(I32)
        padrow = x1[:, B * T - 2:B * T, :].rearrange("p t n -> p (t n)")[:, 0:PAY]

        bank = [ctx.enter_context(nc.psum_tensor(f"bank{i}", [P, 512], F32)) for i in range(8)]
        psT, psL, psF, psKV, psAT = bank[0], bank[1:3], bank[3:5], bank[5], bank[6:8]
        psO, psLG, psRK = bank[6:8], bank[1], bank[2]
        psCA = [[bank[3], bank[4], bank[2], bank[5]], [bank[6], bank[7], bank[2], bank[5]]]
        psUP = [bank[3:5], bank[1:3]]

        img_loaded = [sem("img_loaded0"), sem("img_loaded1")]
        wd1_loaded = sem("wd1_loaded")
        wd2_loaded = sem("wd2_loaded")
        wd3_loaded = sem("wd3_loaded")
        wa_loaded = sem("wa_loaded")
        smalls_loaded = sem("smalls_loaded")
        first_raws_loaded = sem("first_raws_loaded")
        raw_loaded = sem("raw_loaded")
        router_loaded = sem("router_loaded")
        direct_loaded = sem("direct_loaded")
        dve_passed = sem("dve_passed")
        pool_passed = sem("pool_passed")
        iota_ready = sem("iota_ready")
        consts_ready = sem("consts_ready")
        pool_step = sem("pool_step")
        dve_step = sem("dve_step")
        act_step = sem("act_step")
        dots_ready = sem("dots_ready")
        totals_ready = sem("totals_ready")
        logits_ready = sem("logits_ready")
        exps_ready = sem("exps_ready")
        image_ready = sem("image_ready")
        relaid = [sem(f"relaid{i}") for i in range(4)]
        wT_ps = sem("wT_ps")
        wT_sb = sem("wT_sb")
        c_norm = sem("c_norm")
        c_ps = sem("c_ps")
        c_done = sem("c_done")
        catt_moved = sem("catt_moved")
        cattT_ps = sem("cattT_ps")
        cattT_sb = sem("cattT_sb")
        c_out_ps = sem("c_out_ps")
        c_x1 = sem("c_x1")
        c_attn_ps = sem("c_attn_ps")
        catt_ready = sem("catt_ready")
        c_var = sem("c_var")
        c_root = sem("c_root")
        t_var = sem("t_var")
        t_root = sem("t_root")
        x_var = sem("x_var")
        x_root = sem("x_root")
        m_var = sem("m_var")
        m_root = sem("m_root")
        ln_ready = sem("ln_ready")
        xnb_ready = sem("xnb_ready")
        xT_ps = sem("xT_ps")
        xT_sb = sem("xT_sb")
        q_ps = sem("q_ps")
        q_sb = sem("q_sb")
        k_ps = sem("k_ps")
        k_sb = sem("k_sb")
        v_ps = sem("v_ps")
        v_sb = sem("v_sb")
        f_ps = sem("f_ps")
        f_neg = sem("f_neg")
        f_read = sem("f_read")
        f_exp = sem("f_exp")
        f_sum = sem("f_sum")
        kv_ps = sem("kv_ps")
        kvbd_ready = sem("kvbd_ready")
        attn_ps = sem("attn_ps")
        att_ready = sem("att_ready")
        attT_ps = sem("attT_ps")
        attT_sb = sem("attT_sb")
        out_ps = sem("out_ps")
        x1_ready = sem("x1_ready")
        xh_ready = sem("xh_ready")
        x1b_ready = sem("x1b_ready")
        x1T_ps = sem("x1T_ps")
        x1T_sb = sem("x1T_sb")
        m_ps = sem("m_ps")
        m_sb = sem("m_sb")
        mlp_ps = sem("mlp_ps")
        xm_ready = sem("xm_ready")
        h1_ready = sem("h1_ready")
        xmT_ps = sem("xmT_ps")
        xmT_sb = sem("xmT_sb")
        lg_ps = sem("lg_ps")
        lg_gap = sem("lg_gap")
        lg_half = sem("lg_half")
        mask_ready = sem("mask_ready")
        rk_ps = sem("rk_ps")
        place_ready = sem("place_ready")
        scat0 = sem("scat0")
        scat1 = sem("scat1")
        h1_stored0 = sem("h1_stored0")
        h1_stored1 = sem("h1_stored1")
        used_ready = sem("used_ready")
        pad_ready = sem("pad_ready")
        tables_ready = sem("tables_ready")
        pads_made = sem("pads_made")
        pads_stored0 = sem("pads_stored0")
        pads_stored1 = sem("pads_stored1")
        idle_stored = sem("idle_stored")
        experts_loaded = sem("experts_loaded")
        b2_loaded = sem("b2_loaded")
        xs_loaded0 = sem("xs_loaded0")
        xs_loaded1 = sem("xs_loaded1")
        xsT_ps = sem("xsT_ps")
        xsT_sb = sem("xsT_sb")
        h_ps = sem("h_ps")
        w1_ready = sem("w1_ready")
        hT_sb = sem("hT_sb")
        y_ps = sem("y_ps")
        y_ready = sem("y_ready")
        b1_ready = sem("b1_ready")
        slot_ready = sem("slot_ready")
        rows_added = sem("rows_added")

        def vector(name):
            return t[name].rearrange("(o n) -> o n", o=1)

        def each_image(ap):
            return ap.rearrange("s (o n) -> o s n", o=1).to_broadcast([B, STRIPS, ap.shape[1]])

        smalls = [(gamma_bc, vector("L0_attn_gamma").to_broadcast([P, D])),
                  (beta_bc, vector("L0_attn_beta").to_broadcast([P, D])),
                  (beta2_bc, vector("L0_attn_b2").to_broadcast([P, D])),
                  (bout_bc, vector("L0_attn_b_out").to_broadcast([P, D])),
                  (bd[:, 0:1], vector("L0_tok_ba").to_broadcast([P, 1])),
                  (bd[:, 1:4], vector("L0_tok_bd1").to_broadcast([P, 3])),
                  (bd[:, 4:7], vector("L0_tok_bd2").to_broadcast([P, 3])),
                  (bd[:, 7:10], vector("L0_tok_bd3").to_broadcast([P, 3])),
                  (rb2_bc, vector("L0_ffn_rb2").to_broadcast([P, E])),
                  (cx[0:B, 0, :], t["cls_tok"].rearrange("o q n -> (o q) n").to_broadcast([B, D]))]
        raws = [(raw_qkv, t["L0_attn_w_qkv"].rearrange("(m p) n -> p m n", p=P)),
                (raw_o, t["L0_attn_w_out"].rearrange("(m p) n -> p m n", p=P)),
                (raw_w1, t["L0_attn_w1"].rearrange("(m p) n -> p m n", p=P)),
                (raw_w2, t["L0_attn_w2"].rearrange("(m p) n -> p m n", p=P)),
                (raw_cols[0:64, :], t["L0_ffn_b1"].rearrange("e (k p) -> (e k) p", p=P)),
                (raw_cols[64:72, :], t["L0_attn_b1"].rearrange("(k p) -> k p", p=P)),
                (raw_cols[72:80, :], t["L0_ffn_rb1"].rearrange("(k p) -> k p", p=P)),
                (raw_cols[80:82, :], t["L0_attn_gamma"].rearrange("(k p) -> k p", p=P)),
                (raw_cols[82:84, :], t["L0_attn_beta"].rearrange("(k p) -> k p", p=P))]

        def feature_rows(par, i):
            if i < 4:
                return kf[par][:, i // 2, i % 2, :]
            return qf[par][:, 2 * (i - 4):2 * (i - 4) + 2, :].rearrange("p m n -> p (m n)")

        def block_of(raw, m, k):
            return raw[:, m, k * P:(k + 1) * P]

        turned = [(wqkvT[:, k, 0:4 * P], [block_of(raw_qkv, m, k) for m in range(4)]) for k in range(KD)]
        turned += [(wqkvT[:, :, 4 * P:6 * P], [block_of(raw_qkv, m, k) for k in range(KD) for m in (4, 5)])]
        turned += [(woT[:, :, :], [block_of(raw_o, m, k) for k in range(KD) for m in range(KD)])]
        turned += [(w1T[:, k, 4 * P * q:4 * P * (q + 1)], [block_of(raw_w1, m, k) for m in range(4 * q, 4 * q + 4)])
                   for k in range(KD) for q in range(2)]
        turned += [(w2T[:, 2 * i:2 * i + 2, :], [block_of(raw_w2, m, k) for k in (2 * i, 2 * i + 1) for m in range(KD)])
                   for i in range(KH // 2)]

        def normalize(dve, link, src, dst, n, tiles, asked, answered, count):
            apart(dve, dve_passed)
            for j in range(tiles):
                ins = dve.bn_stats(stats[0:n, j, :], src(j))
            link(ins)
            apart(dve, dve_passed)
            for j in range(tiles):
                ins = dve.bn_aggr(mv[0:n, j, :], stats[0:n, j, :])
            ins.then_inc(asked, 1)
            dve.wait_ge(answered, count)
            for j in range(tiles):
                ins = dve.tensor_scalar(dst(j), src(j), mv[0:n, j, 0:1], rstd[0:n, j, :], ALU.subtract, ALU.mult)
            return ins

        def root(pool, link, n, tiles, asked, answered, count, mv=mv, rstd=rstd):
            pool.wait_ge(asked, count)
            apart(pool, pool_passed)
            link(pool.tensor_scalar(rstd[0:n, 0:tiles, :], mv[0:n, 0:tiles, 1:2], EPS_LN, None, ALU.add))
            pool.tensor_tensor(rstd[0:n, 0:tiles, :], rstd[0:n, 0:tiles, :], neg_half[0:n, 0:tiles, :], ALU.pow
                               ).then_inc(answered, 1)

        def wait_for_expert(eng, i):
            need = eng.value_load(need_i[0:1, bass.ds(i, 1)], min_val=LOW_LOADED, max_val=ALL_LOADED)
            eng.wait_ge(experts_loaded, need)

        def store_pads(eng, half_, stored):
            eng.wait_ge(used_ready, 1)
            with eng.Fori(0, E // 2) as i:
                row = eng.value_load(pad_from[0:1, bass.ds(i + half_ * (E // 2), 1)], min_val=0,
                                     max_val=E * REGION - P - B)
                eng.dma_start(xs_d[bass.ds(row, P + B), :], pads_d[:, :]).then_inc(stored, 16)

        block = ctx.enter_context(nc.Block())

        @block.sync
        def _(sp):
            rows = t["x"].rearrange("b (s r) w c -> (b s) (r w c)", s=STRIPS)
            half_img = ROWS * IMG // 2
            for i in range(2):
                sp.dma_start(img[:, half_img * i:half_img * (i + 1)], rows[:, half_img * i:half_img * (i + 1)]
                             ).then_inc(img_loaded[i], 16)
            sp.dma_start(wa, each_image(t["L0_tok_Wa"].rearrange("(s n) k -> s (n k)", s=STRIPS))
                         ).then_inc(wa_loaded, 16)
            for lvl, loaded, w in ((3, wd3_loaded, t["L0_tok_Wd1"]), (2, wd2_loaded, t["L0_tok_Wd2"]),
                                   (1, wd1_loaded, t["L0_tok_Wd3"])):
                m = wd[lvl].shape[1] // 3
                for c in range(3):
                    src = w.rearrange("(c s n) k -> c s (n k)", c=3, s=STRIPS)[c]
                    sp.dma_start(wd[lvl][:, m * c:m * (c + 1)], each_image(src)).then_inc(loaded, 16)
            for i, (dst, src) in enumerate(raws):
                sp.dma_start(dst, src).then_inc(first_raws_loaded if i < 2 else raw_loaded, 16)
            sp.dma_start(rw1, t["L0_ffn_rw1"].rearrange("(k p) n -> p k n", p=P)).then_inc(router_loaded, 16)
            sp.dma_start(rw2, t["L0_ffn_rw2"].rearrange("(k p) n -> p k n", p=P)).then_inc(router_loaded, 16)
            sp.wait_ge(image_ready, 1)
            for b in range(B):
                for j in range(T):
                    p0 = STRIPS * b + STRIPS // T * j
                    sp.dma_start(h[:, T * b + j, :],
                                 img[p0:p0 + STRIPS // T, :].rearrange("p (r n) -> p r n", r=ROWS)
                                 ).then_inc(relaid[min(b, 3)], 16)
            sp.wait_ge(catt_ready, PAIRS)
            sp.dma_start(cx[0:B, 2, :], catt[0:1, :, :]).then_inc(catt_moved, 16)
            sp.wait_ge(c_x1, 1)
            sp.wait_ge(x1_ready, B)
            sp.wait_ge(catt_moved, 16)

            def load_first(e):
                sp.dma_start(experts[:, e, 0:KD * HID].rearrange("p (k n) -> p k n", k=KD),
                             t["L0_ffn_w1"][e].rearrange("(k p) n -> p k n", p=P)).then_inc(experts_loaded, 16)

            def load_second(e):
                sp.dma_start(experts[:, e, KD * HID:EXPERT].rearrange("p (k n) -> p k n", k=KH),
                             t["L0_ffn_w2"][e].rearrange("(k p) n -> p k n", p=P)).then_inc(experts_loaded, 16)

            for e in range(E - 2):
                load_first(e)
                load_second(e)
            stored = [h1_stored0, h1_stored1]

            def store_h1(g, par):
                sp.wait_ge(h1_ready, g + 1)
                sp.dma_start(sums[bass.ds(g * SEQ + 1, IMG), :].rearrange("(t p) n -> p t n", p=P),
                             h[:, bass.ds(T * g, T), :]).then_inc(stored[par], 16)
            with sp.Fori(0, B // 2) as it:
                store_h1(2 * it, 0)
                store_h1(2 * it + 1, 1)
            sp.wait_ge(h1_ready, B + 1)
            sp.dma_start(sums.rearrange("(b q) n -> b q n", b=B)[:, 0, :],
                         cx[0:B, 0, :]).then_inc(h1_stored0, 16)
            sp.wait_ge(xh_ready, B)
            sp.dma_start(b2bc, t["L0_ffn_b2"].rearrange("(o e) n -> o e n", o=1).to_broadcast([P, E, D])
                         ).then_inc(b2_loaded, 16)
            sp.wait_ge(mlp_ps, T * B + 1)
            sp.wait_ge(experts_loaded, LOW_LOADED)
            load_first(E - 2)
            sp.wait_ge(pads_made, 16 * 2)
            store_pads(sp, 0, pads_stored0)
            sp.wait_ge(scat1, 16 * 2 * (T * B // 2))
            sp.wait_ge(scat0, 16 * 2 * (T * B // 2 + 1))
            sp.wait_ge(idle_stored, 16)
            sp.wait_ge(tables_ready, 1)
            loaded = [xs_loaded0, xs_loaded1]

            def load_rows(i, par, ahead):
                if ahead:
                    sp.wait_ge(xsT_ps, i - 1)
                    sp.wait_ge(slot_ready, i - 1)
                row = sp.value_load(row_i[0:1, bass.ds(i, 1)], min_val=0, max_val=E * REGION)
                sp.dma_start(xs[par], xs_d[bass.ds(row, P), :]).then_inc(loaded[par], 16)
            load_rows(0, 0, False)
            load_rows(1, 1, False)
            sp.wait_ge(lg_ps, B + 1)
            load_second(E - 2)
            load_first(E - 1)
            load_second(E - 1)
            with sp.Fori(0, MOE_TILES // 2 - 1) as it:
                load_rows(2 * it + 2, 0, True)
                load_rows(2 * it + 3, 1, True)
            sp.wait_ge(rows_added, 16 * MOE_TILES)

        @block.gpsimd
        def _(pool):
            chain = Chain(pool, pool_step)
            link = chain.link

            def triangle(out, op, base, fill, mult, pattern):
                return pool.affine_select(out=out, in_=out, compare_op=op, fill=fill, base=base,
                                          pattern=pattern, channel_multiplier=mult)

            pool.memset(ident, 0.0)
            pool.memset(same, 1.0)
            pool.memset(before, 1.0)
            pool.memset(ones, 1.0)
            pool.memset(neg_half, -0.5)
            pool.memset(first_src[:, :, :], 1.0)
            pool.memset(projbd[:, :, :], 0.0).then_inc(iota_ready, 1)
            link(pool.memset(cols, 0.0))
            triangle(ident, ALU.not_equal, 0, 1.0, 1, [[-1, P]])
            link(triangle(same.rearrange("p (b s) -> p b s", b=B), ALU.is_ge, 0, 0.0, 1, [[-STRIPS, B], [0, STRIPS]]))
            triangle(same.rearrange("p (b s) -> p b s", b=B), ALU.is_ge, STRIPS - 1, 0.0, -1,
                     [[STRIPS, B], [0, STRIPS]])
            triangle(before, ALU.is_ge, -1, 0.0, -1, [[1, P]])
            triangle(first_src, ALU.is_ge, -1, 0.0, 0, [[1, E + 1], [-1, E]])
            pool.iota(iota8, [[1, E]], base=0, channel_multiplier=0, allow_small_or_imprecise_dtypes=True)
            pool.iota(used, [[REGION, E]], base=0, channel_multiplier=0, allow_small_or_imprecise_dtypes=True)
            pool.iota(region0, [[REGION, E + 1]], base=0, channel_multiplier=0, allow_small_or_imprecise_dtypes=True)
            pool.iota(limits, [[P, 18]], base=0, channel_multiplier=0, allow_small_or_imprecise_dtypes=True)
            pool.iota(tnum, [[1, MOE_TILES]], base=0, channel_multiplier=0, allow_small_or_imprecise_dtypes=True)
            pool.iota(ids[:, :, 0], [[P, T]], base=1, channel_multiplier=1,
                      allow_small_or_imprecise_dtypes=True).then_inc(consts_ready, 1)
            link(pool.memset(padrow, 0.0))
            pool.iota(padrow[:, D:D + 1], [[0, 1]], base=TOKENS, channel_multiplier=1,
                      allow_small_or_imprecise_dtypes=True).then_inc(pad_ready, 1)
            pool.wait_ge(smalls_loaded, 16 * len(smalls))
            link(pool.tensor_tensor(beta2_bc, beta2_bc, beta_bc, ALU.add))

            def residual(g, par):
                pool.wait_ge(ln_ready, g + 1)
                after(pool, x1_ready, g - 1)
                for j in range(T):
                    ins = pool.tensor_tensor(xnb[par][:, j, :], xn[par][:, j, :], bout_bc, ALU.add)
                ins.then_inc(xnb_ready, 1)
            root(pool, link, B, 1, c_var, c_root, 1)
            for g in range(3):
                root(pool, link, P, T, t_var, t_root, g + 1, t_mv[g % 2], t_rstd[g % 2])
            residual(0, 0)

            def attention_step(g, par):
                for i in range(8):
                    u = 8 * g + i
                    pool.wait_ge(f_exp, u + 1)
                    dst = feature_rows(par, i)
                    pool.tensor_tensor(dst, dst, lin[i % 4], ALU.add).then_inc(f_sum, 1)
                    if i == 4 and (not isinstance(g, int) or g + 3 < B):
                        root(pool, link, P, T, t_var, t_root, g + 4, t_mv[1 - par], t_rstd[1 - par])
                if not isinstance(g, int) or g + 1 < B:
                    residual(g + 1, 1 - par)

            attention_step(0, 0)

            def turn(it):
                attention_step(2 * it + 1, 1)
                attention_step(2 * it + 2, 0)
            chain.loop((B - 4) // 2, 2, turn)
            for g in range(B - 3, B):
                attention_step(g, g % 2)

            def affine(g, par):
                pool.wait_ge(xh_ready, g + 1)
                tiles, n, hx = (T, P, None) if not (isinstance(g, int) and g == B) else (1, B, cx)
                after(pool, xm_ready, g - 1)
                for j in range(tiles):
                    ins = pool.tensor_tensor(x1b[par][0:n, j, :], xh[par][0:n, j, :], gamma_bc[0:n, :], ALU.mult)
                for j in range(tiles):
                    hj = h[:, bass.ds(T * g + j, 1), :].rearrange("p o n -> p (o n)") if hx is None else cx[0:B, 0, :]
                    ins = pool.tensor_tensor(hj, hj, beta_bc[0:n, :], ALU.add)
                link(ins)
                for j in range(tiles):
                    ins = pool.tensor_tensor(x1b[par][0:n, j, :], x1b[par][0:n, j, :], beta2_bc[0:n, :], ALU.add)
                ins.then_inc(x1b_ready, 1)

            def scatter(g, par):
                pool.wait_ge(place_ready, g + 1)
                apart(pool, pool_passed)
                tail = isinstance(g, int) and g == B
                if tail:
                    pool.wait_ge(pads_stored0, 16 * (E // 2))
                    pool.wait_ge(pads_stored1, 16 * (E // 2))
                done = scat0 if par == 0 else scat1
                for j in range(1 if tail else T):
                    for k in range(2):
                        n = B if tail else P
                        idx = c_place[0:B, k:k + 1] if tail else place[par][:, k, j:j + 1]
                        pool.indirect_dma_start(
                            out=xs_d[:, :], out_offset=bass.IndirectOffsetOnAxis(ap=idx, axis=0),
                            in_=(c_pay if tail else pay[par])[0:n, j, :], in_offset=None).then_inc(done, 16)

            root(pool, link, P, T, x_var, x_root, 1)
            affine(0, 0)

            def routing_step(g, par):
                peeled = isinstance(g, int)
                if not peeled or 1 <= g <= B + 1:
                    n, tiles = (B, 1) if peeled and g - 1 == B else (P, T)
                    root(pool, link, n, tiles, m_var, m_root, 2 * g - 1)
                    root(pool, link, n, tiles, m_var, m_root, 2 * g)
                if not peeled or g + 1 <= B:
                    n, tiles = (B, 1) if peeled and g + 1 == B else (P, T)
                    root(pool, link, n, tiles, x_var, x_root, g + 2)
                    affine(g + 1, 1 - par)
                if not peeled or g >= 2:
                    scatter(g - 2, par)
            for g in range(3):
                routing_step(g, g % 2)

            def turn(it):
                routing_step(2 * it + 3, 1)
                routing_step(2 * it + 4, 0)
            chain.loop(2, 8, turn)
            routing_step(B - 1, 1)
            for g in (B - 1, B):
                n, tiles = (P, T) if g < B else (B, 1)
                root(pool, link, n, tiles, m_var, m_root, 2 * g + 1)
                root(pool, link, n, tiles, m_var, m_root, 2 * g + 2)
            for g in (B - 2, B - 1, B):
                scatter(g, g % 2)

            pool.wait_ge(h1_stored0, 16 * (B // 2 + 1))
            pool.wait_ge(h1_stored1, 16 * (B // 2))

            def add_rows(i, par, later):
                if later:
                    pool.wait_ge(rows_added, i * 16)
                pool.wait_ge(y_ready, i + 1)
                apart(pool, pool_passed)
                pool.indirect_dma_start(
                    out=sums[:, :], out_offset=bass.IndirectOffsetOnAxis(ap=slot_ids[par][:, 0:1], axis=0),
                    in_=y[par], in_offset=None, bounds_check=TOKENS - 1, oob_is_err=False, compute_op=ALU.add).then_inc(rows_added, 16)
            add_rows(0, 0, False)
            add_rows(1, 1, True)
            with pool.Fori(0, MOE_TILES // 2 - 1) as it:
                add_rows(2 * it + 2, 0, True)
                add_rows(2 * it + 3, 1, True)

        @block.vector
        def _(dve):
            chain = Chain(dve, dve_step)
            link = chain.link

            cur, side, rows = img, IMG, ROWS
            for lvl in (1, 2, 3):
                c2 = cur[:, 0:rows * side].rearrange("p (m two) -> p m two", two=2)
                n = rows * side // 2
                lo, hi = lohi[:, 0:n], lohi[:, n:2 * n]
                parts = 2 if lvl == 1 else 1
                for i in range(parts):
                    a, b = n // parts * i, n // parts * (i + 1)
                    if lvl == 1:
                        dve.wait_ge(img_loaded[i], 16)
                    dve.tensor_tensor(lo[:, a:b], c2[:, a:b, 0], c2[:, a:b, 1], ALU.add)
                    ins = dve.tensor_tensor(hi[:, a:b], c2[:, a:b, 0], c2[:, a:b, 1], ALU.subtract)
                link(ins)
                q = n // 2
                lo4 = lo.rearrange("p (r two c) -> p r two c", two=2, c=side // 2)
                hi4 = hi.rearrange("p (r two c) -> p r two c", two=2, c=side // 2)

                def band(ap):
                    return ap.rearrange("p (r c) -> p r c", c=side // 2)
                dd = det[lvl]
                dve.tensor_tensor(band(app[lvl][:, 0:q]), lo4[:, :, 0, :], lo4[:, :, 1, :], ALU.add)
                dve.tensor_tensor(band(dd[:, 0:q]), lo4[:, :, 0, :], lo4[:, :, 1, :], ALU.subtract)
                dve.tensor_tensor(band(dd[:, q:2 * q]), hi4[:, :, 0, :], hi4[:, :, 1, :], ALU.add)
                link(dve.tensor_tensor(band(dd[:, 2 * q:3 * q]), hi4[:, :, 0, :], hi4[:, :, 1, :], ALU.subtract))
                cur, side, rows = app[lvl], side // 2, rows // 2

            dve.wait_ge(smalls_loaded, 16 * len(smalls))
            normalize(dve, link, lambda j: cx[0:B, 0, :], lambda j: cx[0:B, 1, :], B, 1, c_var, c_root, 1
                      ).then_inc(c_norm, 1)
            dve.wait_ge(c_norm, 1)
            dve.wait_ge(c_ps, 1)
            dve.tensor_copy(c_xT, psT[:, 0:KD]).then_inc(c_done, 1)

            junk = img
            dve.wait_ge(wa_loaded, 16)
            link(dve.tensor_tensor_reduce(junk[:, 0:64], app[3], wa, 1.0, 0.0, ALU.mult, ALU.add, dots[:, 0:1]))
            for lvl, loaded, c0 in ((3, wd3_loaded, 1), (2, wd2_loaded, 4), (1, wd1_loaded, 7)):
                dve.wait_ge(loaded, 16 * 3)
                n = det[lvl].shape[1]
                w3 = wd[lvl].rearrange("p (n k) -> p n k", k=3)
                for k in range(3):
                    ins = dve.tensor_tensor_reduce(junk[:, 0:n], det[lvl][:, :], w3[:, :, k], 1.0, 0.0, ALU.mult,
                                                   ALU.add, dots[:, c0 + k:c0 + k + 1])
                    if lvl == 1 and k == 2:
                        ins.then_inc(dots_ready, 1)
                    else:
                        link(ins)
            dve.wait_ge(totals_ready, 1)
            for c0, c1, scale in ((0, 4, 0.125), (4, 7, 0.25), (7, 10, 0.5)):
                ins = dve.scalar_tensor_tensor(out=gate[:, c0:c1], in0=psKV[:, c0:c1], scalar=scale,
                                               in1=bd[:, c0:c1], op0=ALU.mult, op1=ALU.add)
            link(ins)
            g3 = gate[:, 1:10].rearrange("p (l k) -> p l k", k=3)
            m3 = gsc[:, 0:3].rearrange("p (l o) -> p l o", o=1)
            link(dve.tensor_reduce(gsc[:, 0:3], g3, AX_X, ALU.max))
            dve.tensor_tensor(g3, g3, m3.to_broadcast([P, 3, 3]), ALU.subtract).then_inc(logits_ready, 1)
            dve.wait_ge(exps_ready, 1)
            dve.tensor_scalar(gsc[:, 3:4], gate[:, 0:1], 1.0, None, ALU.add)
            link(dve.tensor_reduce(gsc[:, 4:7], g3, AX_X, ALU.add))
            link(dve.reciprocal(gsc[:, 7:11], gsc[:, 3:7]))
            dve.tensor_scalar(gate[:, 0:1], gsc[:, 7:8], 1.0 / 64, None, ALU.mult)
            for l, f in ((0, 1.0 / 64), (1, 1.0 / 16), (2, 1.0 / 4)):
                ins = dve.tensor_scalar(gate[:, 1 + 3 * l:4 + 3 * l], gate[:, 1 + 3 * l:4 + 3 * l],
                                        gsc[:, 8 + l:9 + l], f, ALU.mult, ALU.mult)
            link(ins)
            link(dve.tensor_scalar(gsc[:, 12:21], gate[:, 1:10], -1.0, None, ALU.mult))

            link(dve.tensor_scalar(app[3][:, :], app[3][:, :], gate[:, 0:1], None, ALU.mult))
            for l, lvl in ((0, 3), (1, 2), (2, 1)):
                if lvl == 1:
                    dve.wait_ge(c_ps, 2)
                    dve.tensor_copy(c_qT, psT[:, 4:4 + KD])
                    dve.memset(c_va[0:1, :, HD:VA], 1.0)
                    dve.tensor_copy(c_va[0:1, :, 0:HD], psL[0][0:1, 0:D].rearrange("p (h d) -> p h d", h=HEADS))
                    dve.tensor_copy(c_kT, psT[:, 6:6 + KD]).then_inc(c_done, 1)
                q = app[lvl].shape[1]
                side = IMG >> lvl
                dd = det[lvl]
                lo4 = lohi[:, 0:2 * q].rearrange("p (r two c) -> p r two c", two=2, c=side)
                hi4 = lohi[:, 2 * q:4 * q].rearrange("p (r two c) -> p r two c", two=2, c=side)

                def band(ap):
                    return ap.rearrange("p (r c) -> p r c", c=side)
                gh, gv, gd = (gate[:, 1 + 3 * l + k:2 + 3 * l + k] for k in range(3))
                ngh = gsc[:, 12 + 3 * l:13 + 3 * l]
                link(dve.tensor_scalar(dd[:, 2 * q:3 * q], dd[:, 2 * q:3 * q], gd, None, ALU.mult))
                for r, g, op in ((0, gh, ALU.add), (1, ngh, ALU.add)):
                    dve.scalar_tensor_tensor(out=lo4[:, :, r, :], in0=band(dd[:, 0:q]), scalar=g,
                                             in1=band(app[lvl]), op0=ALU.mult, op1=op)
                for r, op in ((0, ALU.add), (1, ALU.subtract)):
                    ins = dve.scalar_tensor_tensor(out=hi4[:, :, r, :], in0=band(dd[:, q:2 * q]), scalar=gv,
                                                   in1=band(dd[:, 2 * q:3 * q]), op0=ALU.mult, op1=op)
                link(ins)
                to = img if lvl == 1 else app[lvl - 1]
                o2 = to[:, 0:4 * q].rearrange("p (m two) -> p m two", two=2)
                dve.tensor_tensor(o2[:, :, 0], lohi[:, 0:2 * q], lohi[:, 2 * q:4 * q], ALU.add)
                ins = dve.tensor_tensor(o2[:, :, 1], lohi[:, 0:2 * q], lohi[:, 2 * q:4 * q], ALU.subtract)
                if lvl == 1:
                    ins.then_inc(image_ready, 1)
                else:
                    link(ins)

            dve.wait_ge(c_ps, 3)
            for i in range(2):
                dve.tensor_scalar(c_kl[0:1, 512 * i:512 * i + 512], psAT[i][0:1, :], 0.0, None, ALU.max)
                dve.tensor_scalar(c_kf[0:1, 512 * i:512 * i + 512], psAT[i][0:1, :], 0.0, None, ALU.min)
            dve.tensor_scalar(c_ql, psL[1][:, 0:PAIRS], 0.0, None, ALU.max)
            dve.tensor_scalar(c_qf, psL[1][:, 0:PAIRS], 0.0, None, ALU.min).then_inc(c_done, 1)
            dve.tensor_tensor(cx[0:B, 1, :], cx[0:B, 1, :], bout_bc[0:B, :], ALU.add)
            dve.wait_ge(image_ready, 1)
            for i in range(2):
                dve.memset(va[i][:, :, :, HD:VA], 1.0)
            dve.memset(kvbd[:, :, :, :], 0.0)
            dve.wait_ge(c_done, 3)
            dve.wait_ge(act_step, 1)
            dve.tensor_tensor(c_qf, c_qf, c_ql, ALU.add)
            dve.tensor_tensor(c_kf[0:1, :], c_kf[0:1, :], c_kl[0:1, :], ALU.add).then_inc(c_done, 1)
            dve.wait_ge(c_done, 4)

            dve.wait_ge(relaid[0], 16 * T)
            dve.wait_ge(pads_made, 16 * 2)
            dve.wait_ge(idle_stored, 16)

            def token(g, j):
                return h[:, bass.ds(T * g + j, 1), :].rearrange("p o n -> p (o n)")

            def token_stats(g, par):
                after(dve, t_var, g)
                apart(dve, dve_passed)
                for j in range(T):
                    ins = dve.bn_stats(stats[:, j, :], token(g, j))
                link(ins)
                apart(dve, dve_passed)
                for j in range(T):
                    ins = dve.bn_aggr(t_mv[par][:, j, :], stats[:, j, :])
                ins.then_inc(t_var, 1)

            def norm_tokens(g, par):
                dve.wait_ge(t_root, g + 1)
                after(dve, xT_ps, g - 1)
                after(dve, xnb_ready, g - 1)
                for j in range(T):
                    ins = dve.tensor_scalar(xn[par][:, j, :], token(g, j), t_mv[par][:, j, 0:1], t_rstd[par][:, j, :],
                                            ALU.subtract, ALU.mult)
                ins.then_inc(ln_ready, 1)

            def v_rows(g, par):
                dve.wait_ge(v_ps, g + 1)
                after(dve, kv_ps, g - 1)
                dve.tensor_copy(va[par][:, :, :, 0:HD],
                                psL[1][:, :].rearrange("p (t h d) -> p t h d", t=T, h=HEADS)).then_inc(v_sb, 1)

            def x1_rows(g, par):
                dve.wait_ge(out_ps, g + 1)
                dve.wait_ge(xnb_ready, g + 1)
                dve.tensor_tensor(x1[:, bass.ds(T * g, T), :], psL[0][:, :].rearrange("p (t n) -> p t n", t=T),
                                  xnb[par][:, :, :], ALU.add).then_inc(x1_ready, 1)

            token_stats(0, 0)
            def attention_rows(g, par, j):
                dve.wait_ge(attn_ps, T * g + j + 1)
                src = psAT[j][:, 0:PAIRS * PW].rearrange("p (h d) -> p h d", h=HEADS)
                d3 = den[:, j, :].rearrange("p (h o) -> p h o", o=1)
                link(dve.tensor_scalar(d3, src[:, :, HD:VA], EPS_ATTN, None, ALU.add))
                link(dve.reciprocal(den[:, j, :], den[:, j, :]))
                dve.tensor_tensor(att[par][:, j, :].rearrange("p (h d) -> p h d", h=HEADS), src[:, :, 0:HD],
                                  d3.to_broadcast([P, HEADS, HD]), ALU.mult).then_inc(att_ready, 1)

            norm_tokens(0, 0)
            dve.wait_ge(relaid[1], 16 * T)
            token_stats(1, 1)
            dve.wait_ge(ln_ready, 1)
            dve.wait_ge(relaid[2], 16 * T)
            token_stats(2, 0)
            norm_tokens(1, 1)
            dve.wait_ge(c_ps, 4)
            dve.tensor_copy(c_kv[:, :, :], psKV[:, 0:PAIRS * PW].rearrange("p (m n) -> p m n", m=PAIRS)
                            ).then_inc(c_done, 1)
            dve.wait_ge(c_done, 5)
            v_rows(0, 0)

            def attention_step(g, par):
                peeled = isinstance(g, int)
                def negatives(i):
                    dve.wait_ge(f_ps, 8 * g + i + 1)
                    dve.tensor_scalar(feature_rows(par, i), psF[i % 2][:, :], 0.0, None, ALU.min
                                      ).then_inc(f_neg, 1)
                if peeled and g == 0:
                    dve.wait_ge(relaid[3], 16 * T * (B - 3))
                negatives(0)
                negatives(1)
                if not peeled or g >= 1:
                    attention_rows(g - 1, 1 - par, 1)
                if not peeled or g + 2 < B:
                    norm_tokens(g + 2, par)
                negatives(2)
                negatives(3)
                if not peeled or g + 3 < B:
                    token_stats(g + 3, 1 - par)
                for i in range(4, 8):
                    negatives(i)
                if not peeled or g >= 1:
                    x1_rows(g - 1, 1 - par)
                dve.wait_ge(kv_ps, g + 1)
                kvv = psKV[:, 0:PAIRS * PW].rearrange("p (m n) -> p m n", m=PAIRS)
                for p0, p1, c0, c1 in ((0, FEAT, 0, VA), (FEAT, P, VA, PW)):
                    ins = dve.tensor_tensor(kvbd[p0:p1, bass.ds(g, 1), :, c0:c1].rearrange("p o m n -> p (o m) n"),
                                            kvv[p0:p1, :, c0:c1], c_kv[p0:p1, :, c0:c1], ALU.add)
                ins.then_inc(kvbd_ready, 1)
                if not peeled or g + 1 < B:
                    v_rows(g + 1, 1 - par)
                attention_rows(g, par, 0)

            attention_step(0, 0)

            def turn(it):
                attention_step(2 * it + 1, 1)
                attention_step(2 * it + 2, 0)
            chain.loop((B - 4) // 2, 10, turn)
            for g in range(B - 3, B):
                attention_step(g, g % 2)

            def class_rows(part):
                dve.wait_ge(c_attn_ps, 4 * part + 4)
                pairs = [(4 * part + i, psCA[part][i][0:1, 0:B * PW].rearrange("p (b h d) -> p b h d", b=B, h=2))
                         for i in range(4)]
                for m, src in pairs:
                    ins = dve.tensor_scalar(c_den[0:1, m, :, :], src[:, :, :, HD], EPS_ATTN, None, ALU.add)
                link(ins)
                part_den = c_den[0:1, 4 * part:4 * part + 4, :, :]
                link(dve.reciprocal(part_den, part_den))
                for m, src in pairs:
                    dst = catt[0:1, :, 2 * HD * m:2 * HD * (m + 1)].rearrange("p b (h d) -> p b h d", h=2)
                    den4 = c_den[0:1, m, :, :].rearrange("p b (h o) -> p b h o", o=1)
                    dve.tensor_tensor(dst, src[:, :, :, 0:HD], den4.to_broadcast([1, B, 2, HD]), ALU.mult
                                      ).then_inc(catt_ready, 1)
            attention_rows(B - 1, 1, 1)
            class_rows(0)
            x1_rows(B - 1, 1)
            dve.wait_ge(x1_ready, B)

            def norm_x1(g, par):
                tail = isinstance(g, int) and g == B
                after(dve, x1T_ps, g - 1)
                after(dve, x1b_ready, g - 1)
                src = ((lambda j: cx[0:B, 1, :]) if tail else
                       (lambda j: x1[:, bass.ds(T * g + j, 1), :].rearrange("p o n -> p (o n)")))
                n, tiles = (B, 1) if tail else (P, T)
                normalize(dve, link, src, lambda j: xh[par][0:n, j, :], n, tiles, x_var, x_root, g + 1
                          ).then_inc(xh_ready, 1)

            def choose(g, par):
                tail = isinstance(g, int) and g == B
                n, tiles = (B, 1) if tail else (P, T)
                dve.wait_ge(lg_ps, g + 1)
                link(dve.tensor_tensor(lg[0:n, 0:tiles, :], psLG[0:n, 0:tiles * E].rearrange("p (t e) -> p t e", e=E),
                                       rb2_bc[0:n, :].rearrange("p (o e) -> p o e", o=1).to_broadcast([n, tiles, E]),
                                       ALU.add))
                apart(dve, dve_passed)
                for j in range(tiles):
                    ins = dve.max(top[0:n, j, :], lg[0:n, j, :])
                link(ins)
                dve.tensor_tensor(gap[0:n, 0:tiles, :], top[0:n, 0:tiles, 0:1], top[0:n, 0:tiles, 1:2],
                                  ALU.subtract).then_inc(lg_gap, 1)
                for j in range(tiles):
                    ins = dve.max_index(topi[0:n, j, :], top[0:n, j, :], lg[0:n, j, :])
                link(ins)
                link(dve.tensor_copy(topf[0:n, 0:tiles, :], topi[0:n, 0:tiles, 0:2]))
                if tail:
                    dve.memset(mask[:, :, :], 0.0)
                for k in range(2):
                    for j in range(tiles):
                        ins = dve.tensor_scalar(onehot[0:n, k, j, :], iota8[0:n, :], topf[0:n, j, k:k + 1], None,
                                                ALU.is_equal)
                link(ins)
                dve.tensor_tensor(mask[0:n, 0:tiles, :], onehot[0:n, 0, 0:tiles, :], onehot[0:n, 1, 0:tiles, :],
                                  ALU.add).then_inc(mask_ready, 1)

            def gates(g, par):
                tail = isinstance(g, int) and g == B
                rows = c_pay if tail else pay[par]
                n, tiles = (B, 1) if tail else (P, T)
                dve.wait_ge(lg_half, g + 1)
                dve.tensor_scalar(probs[0:n, 0, 0:tiles, :], half[0:n, 0:tiles, :], 0.5, 0.5, ALU.mult, ALU.add)
                link(dve.tensor_scalar(probs[0:n, 1, 0:tiles, :], half[0:n, 0:tiles, :], -0.5, 0.5, ALU.mult, ALU.add))
                for k in range(2):
                    ins = dve.tensor_tensor(weighed[0:n, k, 0:tiles, :], onehot[0:n, k, 0:tiles, :],
                                            probs[0:n, k, 0:tiles, :].to_broadcast([n, tiles, E]), ALU.mult)
                link(ins)
                dve.tensor_tensor(rows[0:n, 0:tiles, D + 1:PAY], weighed[0:n, 0, 0:tiles, :],
                                  weighed[0:n, 1, 0:tiles, :], ALU.add)
                if tail:
                    dve.tensor_scalar(rows[0:n, 0, D:D + 1], ids[0:n, 0, :], float(-B * SEQ - 1), float(SEQ),
                                      ALU.add, ALU.mult)
                else:
                    dve.tensor_copy(pay[par][:, :, D:D + 1], ids[:, :, :])
                    link(dve.tensor_scalar(ids[:, :, :], ids[:, :, :], float(SEQ), None, ALU.add))

            def settle(g, par):
                tail = isinstance(g, int) and g == B
                n, tiles = (B, 1) if tail else (P, T)
                dve.wait_ge(rk_ps, g + 1)
                rk = psRK[:, 0:(T + 1) * E].rearrange("p (t e) -> p t e", e=E)
                link(dve.tensor_tensor(rank[0:n, 0:tiles, :], rk[0:n, 0:tiles, :],
                                       used[0:n, :].rearrange("p (o e) -> p o e", o=1).to_broadcast([n, tiles, E]),
                                       ALU.add))
                dve.tensor_tensor(used, used, rk[:, T, :], ALU.add)
                for k in range(2):
                    ins = dve.tensor_tensor(placed[0:n, k, 0:tiles, :], onehot[0:n, k, 0:tiles, :],
                                            rank[0:n, 0:tiles, :], ALU.mult)
                link(ins)
                for k in range(2):
                    ins = dve.tensor_reduce(placef[0:n, k, 0:tiles, :], placed[0:n, k, 0:tiles, :], AX_X, ALU.add)
                link(ins)
                gates(g, par)
                dst = c_place[0:n, :].rearrange("p (k o) -> p k o", o=1) if tail else place[par][:, :, :]
                dve.tensor_copy(dst, placef[0:n, :, 0:tiles, 0]).then_inc(place_ready, 1)

            def finish_rows(g, par):
                tail = isinstance(g, int) and g == B
                n, tiles = (B, 1) if tail else (P, T)

                def hrow(j):
                    return cx[0:B, 0, :] if tail else h[:, bass.ds(T * g + j, 1), :].rearrange("p o n -> p (o n)")
                dve.wait_ge(x1b_ready, g + 1)
                for j in range(tiles):
                    dve.wait_ge(mlp_ps, T * g + j + 1)
                    ins = dve.tensor_tensor(x2[0:n, j, :], psO[j][0:n, 0:D], x1b[par][0:n, j, :], ALU.add)
                link(ins)
                link(normalize(dve, link, lambda j: x2[0:n, j, :], lambda j: x2[0:n, j, :], n, tiles,
                               m_var, m_root, 2 * g + 1))
                for j in range(tiles):
                    ins = dve.tensor_tensor(x2[0:n, j, :], x2[0:n, j, :], gamma_bc[0:n, :], ALU.mult)
                link(ins)
                for j in range(tiles):
                    ins = dve.tensor_tensor(hrow(j), hrow(j), x2[0:n, j, :], ALU.add)
                ins.then_inc(h1_ready, 1)
                dve.wait_ge(h1_ready, g + 1)
                done = scat0 if par == 0 else scat1
                rows = c_pay if tail else pay[par]
                if isinstance(g, int):
                    if not tail:
                        after(dve, done, 32 * T * (g // 2))
                else:
                    dve.wait_ge(done, (g - par) * (16 * T))
                after(dve, xmT_ps, g - 1)
                normalize(dve, link, hrow, lambda j: rows[0:n, j, 0:D], n, tiles, m_var, m_root, 2 * g + 2
                          ).then_inc(xm_ready, 1)

            norm_x1(0, 0)
            class_rows(1)

            def routing_step(g, par):
                peeled = isinstance(g, int)
                if not peeled or 1 <= g <= B + 1:
                    finish_rows(g - 1, 1 - par)
                if not peeled or g >= 2:
                    choose(g - 2, par)
                if not peeled or g + 1 <= B:
                    norm_x1(g + 1, 1 - par)
                if peeled and g == 0:
                    dve.wait_ge(c_out_ps, 1)
                    dve.tensor_tensor(cx[0:B, 1, :], psL[1][0:B, 0:D], cx[0:B, 1, :], ALU.add).then_inc(c_x1, 1)
                    dve.wait_ge(c_x1, 1)
                if not peeled or g >= 2:
                    settle(g - 2, par)
            for g in range(3):
                routing_step(g, g % 2)

            def turn(it):
                routing_step(2 * it + 3, 1)
                routing_step(2 * it + 4, 0)
            chain.loop(2, 2 * ROUTING_LINKS, turn)
            routing_step(B - 1, 1)
            finish_rows(B - 1, 1)
            finish_rows(B, 0)
            for g in (B - 2, B - 1):
                choose(g, g % 2)
                settle(g, g % 2)
            dve.wait_ge(place_ready, B)
            dve.tensor_copy(pad_from[:, :], used).then_inc(used_ready, 1)
            choose(B, 0)
            settle(B, 0)

            dve.wait_ge(place_ready, B + 1)
            link(dve.tensor_tensor(count, used, region0[:, 0:E], ALU.subtract))
            link(dve.tensor_tensor(over[:, :, :], count.rearrange("p (e o) -> p e o", o=1).to_broadcast([P, E, 18]),
                                   limits.rearrange("p (o j) -> p o j", o=1).to_broadcast([P, E, 18]), ALU.is_gt))
            link(dve.tensor_reduce(tiles_e, over[:, :, :], AX_X, ALU.add))
            link(dve.tensor_tensor(lower[:, :, :], first_src[:, :, :],
                                   tiles_e.rearrange("p (o e) -> p o e", o=1).to_broadcast([P, E + 1, E]), ALU.mult))
            link(dve.tensor_reduce(first, lower[:, :, :], AX_X, ALU.add))
            link(dve.scalar_tensor_tensor(out=jump, in0=first, scalar=float(-P), in1=region0, op0=ALU.mult,
                                          op1=ALU.add))
            dve.tensor_scalar(rowt, tnum, float(P), None, ALU.mult)
            link(dve.tensor_tensor(steps[:, :, :], tnum.rearrange("p (o i) -> p o i", o=1).to_broadcast([P, E, MOE_TILES]),
                                   first[:, 1:E + 1].rearrange("p (e o) -> p e o", o=1).to_broadcast([P, E, MOE_TILES]),
                                   ALU.is_ge))
            dve.tensor_reduce(owner, steps[:, 0:E - 1, :].rearrange("p e i -> p i e"), AX_X, ALU.add)
            link(dve.tensor_tensor(jumps, jump[:, 1:E + 1], jump[:, 0:E], ALU.subtract))
            link(dve.tensor_tensor(steps[:, :, :], steps[:, :, :],
                                   jumps.rearrange("p (e o) -> p e o", o=1).to_broadcast([P, E, MOE_TILES]), ALU.mult))
            link(dve.tensor_reduce(high, steps[:, :, :].rearrange("p e i -> p i e"), AX_X, ALU.add))
            link(dve.tensor_tensor(rowt, rowt, high, ALU.add))
            dve.tensor_scalar(rowt, rowt, float(E * REGION), None, ALU.min)
            link(dve.tensor_scalar(high, owner, float(E - 2), float(ALL_LOADED - LOW_LOADED), ALU.is_ge, ALU.mult))
            dve.tensor_scalar(need_i[:, :], high, float(LOW_LOADED), None, ALU.add)
            dve.tensor_copy(owner_i[:, :], owner)
            dve.tensor_copy(row_i[:, :], rowt).then_inc(tables_ready, 1)
            dve.wait_ge(tables_ready, 1)

            dve.wait_ge(b2_loaded, 16)
            loaded = [xs_loaded0, xs_loaded1]

            def weights_in(i, par):
                e = dve.value_load(owner_i[0:1, bass.ds(i, 1)], min_val=0, max_val=E - 1)
                wait_for_expert(dve, i)
                after(dve, h_ps, 2 * (i - 1))
                dve.tensor_copy(w1now[par].rearrange("p k n -> p (k n)").rearrange("p (o n) -> p o n", o=1),
                                experts[:, bass.ds(e, 1), 0:KD * HID]).then_inc(w1_ready, 1)
                after(dve, hT_sb, KH * (i - 1))
                dve.tensor_copy(b1now[par].rearrange("p (o k) -> p o k", o=1),
                                eb1T[:, bass.ds(e, 1), :]).then_inc(b1_ready, 1)

            def rows_in(i, par, turns):
                e = dve.value_load(owner_i[0:1, bass.ds(i, 1)], min_val=0, max_val=E - 1)
                dve.wait_ge(loaded[par], 16 * turns)
                after(dve, rows_added, 16 * (i - 1))
                dve.tensor_copy(gate_now[par], xs[par][:, bass.ds(e + (D + 1), 1)])
                dve.tensor_copy(slot_ids[par][:, :], xs[par][:, D:D + 1]).then_inc(slot_ready, 1)

            def tile_out(i, par):
                e = dve.value_load(owner_i[0:1, bass.ds(i, 1)], min_val=0, max_val=E - 1)
                dve.wait_ge(y_ps, i + 1)
                link(dve.tensor_tensor(ybias[par].rearrange("p (o n) -> p o n", o=1),
                                       psAT[par][:, 0:D].rearrange("p (o n) -> p o n", o=1),
                                       b2bc[:, bass.ds(e, 1), :], ALU.add))
                dve.tensor_scalar(y[par], ybias[par], gate_now[par], None, ALU.mult).then_inc(y_ready, 1)

            weights_in(0, 0)
            weights_in(1, 1)
            rows_in(0, 0, 1)

            def expert_step(i, par, turns):
                if not isinstance(i, int) or i + 2 < MOE_TILES:
                    weights_in(i + 2, par)
                if not isinstance(i, int) or i + 1 < MOE_TILES:
                    rows_in(i + 1, 1 - par, turns + par)
                tile_out(i, par)
            expert_step(0, 0, 1)
            expert_step(1, 1, 1)

            def turn(it):
                expert_step(2 * it + 2, 0, it + 2)
                expert_step(2 * it + 3, 1, it + 2)
            chain.loop(MOE_TILES // 2 - 2, 2, turn)
            expert_step(MOE_TILES - 2, 0, MOE_TILES // 2)
            expert_step(MOE_TILES - 1, 1, MOE_TILES // 2)

        @block.scalar
        def _(act):
            for dst, src in smalls:
                act.dma_start(dst, src).then_inc(smalls_loaded, 16)
            act.wait_ge(pad_ready, 1)
            act.dma_start(pads_d[0:P, :], padrow).then_inc(pads_made, 16)
            act.dma_start(pads_d[P:P + B, :], padrow[0:B, :]).then_inc(pads_made, 16)
            act.dma_start(xs_d[E * REGION:E * REGION + P, :], padrow).then_inc(idle_stored, 16)
            act.wait_ge(iota_ready, 1)
            for hh in range(HEADS):
                p0, c0 = HD * (hh % 8), FEAT * (hh % 8)
                act.dma_start(projbd[p0:p0 + HD, hh // 8, c0:c0 + FEAT],
                              t["L0_attn_proj"][hh]).then_inc(direct_loaded, 16)

            def turned_out(u):
                dst, blocks = turned[u]
                act.wait_ge(wT_ps, u + 1)
                src = psF[u % 2][:, :]
                if len(dst.shape) == 3:
                    src = src.rearrange("p (a n) -> p a n", a=dst.shape[1])
                act.copy(dst, src).then_inc(wT_sb, 1)
            for u in range(TURNED_FIRST):
                turned_out(u)
            act.wait_ge(logits_ready, 1)
            act.activation(gate[:, 0:1], gate[:, 0:1], ACT.Exp, scale=-1.0)
            act.activation(gate[:, 1:10], gate[:, 1:10], ACT.Exp).then_inc(exps_ready, 1)
            for u in range(TURNED_FIRST, len(turned)):
                turned_out(u)
            act.wait_ge(wT_ps, len(turned) + 1)
            act.copy(cols, psF[len(turned) % 2][:, 0:84]).then_inc(wT_sb, 1)

            act.wait_ge(c_done, 3)
            act.activation(c_kf[0:1, :], c_kf[0:1, :], ACT.Exp)
            act.activation(c_qf, c_qf, ACT.Exp).then_inc(act_step, 1)

            def tokens_T(g, par):
                act.wait_ge(xT_ps, g + 1)
                after(act, v_ps, g - 1)
                act.copy(xnT[par][:, :, :], psT[:, :].rearrange("p (k n) -> p k n", k=KD)).then_inc(xT_sb, 1)

            def q_T(g, par):
                act.wait_ge(q_ps, g + 1)
                after(act, f_ps, 8 * (g - 1))
                act.copy(qT[par][:, :, :], psL[1][:, :].rearrange("p (k n) -> p k n", k=KD)).then_inc(q_sb, 1)

            def k_T(g, par):
                act.wait_ge(k_ps, g + 1)
                act.copy(kT[par][:, :, :], psL[0][:, :].rearrange("p (k n) -> p k n", k=KD)).then_inc(k_sb, 1)

            def att_T(g, par):
                act.wait_ge(attT_ps, g + 1)
                act.copy(attT[par][:, :, :], psT[:, :].rearrange("p (k n) -> p k n", k=KD)).then_inc(attT_sb, 1)

            tokens_T(0, 0)
            q_T(0, 0)
            k_T(0, 0)
            tokens_T(1, 1)

            def attention_step(g, par):
                peeled = isinstance(g, int)

                def bank_out(i):
                    u = 8 * g + i
                    act.wait_ge(f_neg, u + 1)
                    after(act, f_sum, u - 3)
                    act.activation(lin[i % 4], psF[i % 2][:, :], ACT.Relu).then_inc(f_read, 1)
                    act.activation(feature_rows(par, i), feature_rows(par, i), ACT.Exp).then_inc(f_exp, 1)
                bank_out(0)
                bank_out(1)
                if not peeled or g + 1 < B:
                    q_T(g + 1, 1 - par)
                bank_out(2)
                bank_out(3)
                if not peeled or g >= 1:
                    att_T(g - 1, 1 - par)
                if not peeled or g + 1 < B:
                    k_T(g + 1, 1 - par)
                bank_out(4)
                bank_out(5)
                if not peeled or g + 2 < B:
                    tokens_T(g + 2, par)
                bank_out(6)
                bank_out(7)

            attention_step(0, 0)
            with act.Fori(0, (B - 4) // 2) as it:
                attention_step(2 * it + 1, 1)
                attention_step(2 * it + 2, 0)
            for g in range(B - 3, B):
                attention_step(g, g % 2)
            att_T(B - 1, 1)
            act.wait_ge(x1_ready, B)

            def x1_T(g, par):
                tail = isinstance(g, int) and g == B
                n = B if tail else IMG
                act.wait_ge(x1T_ps, g + 1)
                for k in range(KD):
                    ins = act.activation(x1T[par][:, k, 0:n], psT[:, k * IMG:k * IMG + n], ACT.Identity,
                                         bias=betaT[:, k:k + 1], scale=gammaT[:, k:k + 1])
                ins.then_inc(x1T_sb, 1)

            def xm_T(g, par):
                tail = isinstance(g, int) and g == B
                n = B if tail else IMG
                act.wait_ge(xmT_ps, g + 1)
                act.copy(xmT[par][:, :, 0:n], psT[:, :].rearrange("p (k n) -> p k n", k=KD)[:, :, 0:n]
                         ).then_inc(xmT_sb, 1)

            def hidden(g, first_use, func, bias, dst, n):
                for i in range(4):
                    act.wait_ge(m_ps, first_use + i + 1)
                    for m in range(2):
                        ins = act.activation(dst[:, 2 * i + m, 0:n], psF[i % 2][:, m * IMG:m * IMG + n], func,
                                             bias=bias[:, 2 * i + m:2 * i + m + 1])
                    ins.then_inc(m_sb, 1)

            x1_T(0, 0)

            def gate_halves(g, tiles, rows):
                act.wait_ge(lg_gap, g + 1)
                act.activation(half[0:rows, 0:tiles, :], gap[0:rows, 0:tiles, :], ACT.Tanh, scale=0.5
                               ).then_inc(lg_half, 1)

            def routing_step(g, par):
                peeled = isinstance(g, int)
                if not peeled or g <= B:
                    n = B if peeled and g == B else IMG
                    hidden(g, 8 * g - 4 if not peeled or g else 0, ACT.Gelu, b1T, gT, n)
                if not peeled or 1 <= g <= B + 1:
                    n = B if peeled and g - 1 == B else IMG
                    xm_T(g - 1, 1 - par)
                    hidden(g - 1, 8 * g if not peeled or g <= B else 8 * g - 4, ACT.Silu, rb1T, rT, n)
                if not peeled or g + 1 <= B:
                    x1_T(g + 1, 1 - par)
                if peeled and g == 0:
                    act.wait_ge(cattT_ps, 1)
                    act.copy(c_attT[:, :, :], psT[:, 0:KD * B].rearrange("p (k n) -> p k n", k=KD)
                             ).then_inc(cattT_sb, 1)
                if not peeled or g >= 2:
                    gate_halves(g - 2, T, P)
            for g in range(3):
                routing_step(g, g % 2)
            with act.Fori(0, 2) as it:
                routing_step(2 * it + 3, 1)
                routing_step(2 * it + 4, 0)
            routing_step(B - 1, 1)
            hidden(B, 8 * B - 4, ACT.Gelu, b1T, gT, B)
            xm_T(B - 1, 1)
            hidden(B - 1, 8 * B, ACT.Silu, rb1T, rT, IMG)
            gate_halves(B - 2, T, P)
            xm_T(B, 0)
            hidden(B, 8 * B + 4, ACT.Silu, rb1T, rT, B)
            gate_halves(B - 1, T, P)
            gate_halves(B, 1, B)

            act.wait_ge(pads_made, 16 * 2)
            store_pads(act, 1, pads_stored1)

            def rows_T(i, par):
                act.wait_ge(xsT_ps, i + 1)
                act.copy(xsT[par], psT[:, 0:D]).then_inc(xsT_sb, 1)

            def hidden_rows(i, par):
                act.wait_ge(b1_ready, i + 1)
                for c in range(2):
                    act.wait_ge(h_ps, 2 * i + c + 1)
                    for m in range(4):
                        k = 4 * c + m
                        act.activation(hT[par][:, k, :], psUP[par][c][:, P * m:P * m + P], ACT.Silu,
                                       bias=b1now[par][:, k:k + 1]).then_inc(hT_sb, 1)

            rows_T(0, 0)
            rows_T(1, 1)
            hidden_rows(0, 0)

            def expert_step(i, par):
                if not isinstance(i, int) or i + 1 < MOE_TILES:
                    hidden_rows(i + 1, 1 - par)
                if not isinstance(i, int) or i + 2 < MOE_TILES:
                    rows_T(i + 2, par)
            expert_step(0, 0)
            expert_step(1, 1)
            with act.Fori(0, MOE_TILES // 2 - 2) as it:
                expert_step(2 * it + 2, 0)
                expert_step(2 * it + 3, 1)
            expert_step(MOE_TILES - 2, 0)
            expert_step(MOE_TILES - 1, 1)

        @block.tensor
        def _(pe):
            def mm(out, lhsT, rhs, start=True, stop=True, **kw):
                return pe.matmul(out, lhsT, rhs, start=start, stop=stop, **kw)

            pe.wait_ge(consts_ready, 1)

            def turn_block(u):
                after(pe, wT_sb, u - 1)
                for i, src in enumerate(turned[u][1]):
                    ins = pe.transpose(psF[u % 2][:, P * i:P * i + P], src, ident)
                ins.then_inc(wT_ps, 1)

            pe.wait_ge(c_norm, 1)
            for k in range(KD):
                ins = pe.transpose(psT[:, k:k + 1], cx[0:1, 1, k * P:k * P + P], ident[0:1, 0:1])
            ins.then_inc(c_ps, 1)
            pe.wait_ge(first_raws_loaded, 16 * 2)
            for u in range(TURNED_FIRST):
                turn_block(u)
            pe.wait_ge(dots_ready, 1)
            mm(psKV[:, 0:10], same, dots).then_inc(totals_ready, 1)
            pe.wait_ge(c_done, 1)
            pe.wait_ge(wT_sb, TURNED_FIRST)
            for i in range(4):
                for k in range(KD):
                    mm(psT[:, 4 + i:5 + i], wqkvT[:, k, P * i:P * i + P], c_xT[:, k:k + 1], k == 0, k == KD - 1)
            for k in range(KD):
                ins = mm(psL[0][0:1, 0:D], c_xT[:, k:k + 1], wqkvT[:, k, 2 * D:3 * D], k == 0, k == KD - 1)
            ins.then_inc(c_ps, 1)
            pe.wait_ge(raw_loaded, 16 * (len(raws) - 2))
            for u in range(TURNED_FIRST, len(turned)):
                turn_block(u)
            pe.wait_ge(wT_sb, len(turned) - 1)
            pe.transpose(psF[len(turned) % 2][:, 0:84], raw_cols[0:84, :], ident[0:84, 0:84]).then_inc(wT_ps, 1)
            pe.wait_ge(c_done, 2)
            pe.wait_ge(direct_loaded, 16 * HEADS)
            pe.wait_ge(router_loaded, 16 * 2)
            for c in range(2):
                mm(psAT[c][0:1, :], c_kT[:, c:c + 1], projbd[:, c, :])
            for m in range(PAIRS):
                ins = mm(psL[1][:, m:m + 1], projbd[:, m // 4, P * (m % 4):P * (m % 4) + P], c_qT[:, m // 4:m // 4 + 1])
            ins.then_inc(c_ps, 1)

            def tokens_T(g, par):
                pe.wait_ge(ln_ready, g + 1)
                after(pe, xT_sb, g)
                after(pe, attT_sb, g - 2)
                for j in range(T):
                    for k in range(KD):
                        ins = pe.transpose(psT[:, k * IMG + j * P:k * IMG + j * P + P],
                                           xn[par][:, j, k * P:k * P + P], ident)
                ins.then_inc(xT_ps, 1)

            def qk(g, par, half_):
                if half_:
                    dst, done = psL[0], k_ps
                else:
                    dst, done = psL[1], q_ps
                    pe.wait_ge(xT_sb, g + 1)
                    after(pe, v_sb, g)
                for m in range(KD):
                    c0 = D * half_ + P * m
                    for k in range(KD):
                        ins = mm(dst[:, m * IMG:(m + 1) * IMG], wqkvT[:, k, c0:c0 + P], xnT[par][:, k, :],
                                 k == 0, k == KD - 1)
                ins.then_inc(done, 1)

            def values(g, par):
                pe.wait_ge(q_sb, g + 1)
                for j in range(T):
                    for k in range(KD):
                        ins = mm(psL[1][:, j * D:(j + 1) * D], xnT[par][:, k, j * P:j * P + P],
                                 wqkvT[:, k, 2 * D:3 * D], k == 0, k == KD - 1)
                ins.then_inc(v_ps, 1)

            def features(g, par, i):
                u = 8 * g + i
                after(pe, f_read, u - 1)
                if i < 4:
                    ins = mm(psF[i % 2][:, :], kT[par][:, i % 2, (i // 2) * P:(i // 2) * P + P], projbd[:, i % 2, :])
                else:
                    for m in range(2):
                        pair = 2 * (i - 4) + m
                        c0 = P * (pair % 4)
                        ins = mm(psF[i % 2][:, m * IMG:(m + 1) * IMG], projbd[:, pair // 4, c0:c0 + P],
                                 qT[par][:, pair // 4, :])
                ins.then_inc(f_ps, 1)

            def att_T(g, par):
                pe.wait_ge(att_ready, T * g + T)
                pe.wait_ge(xT_sb, g + 3 if not isinstance(g, int) or g + 3 <= B else B)
                for j in range(T):
                    for k in range(KD):
                        ins = pe.transpose(psT[:, k * IMG + j * P:k * IMG + j * P + P],
                                           att[par][:, j, k * P:k * P + P], ident)
                ins.then_inc(attT_ps, 1)

            def out_rows(g, par):
                pe.wait_ge(attT_sb, g + 1)
                pe.wait_ge(k_sb, g + 3 if not isinstance(g, int) or g + 3 <= B else B)
                for j in range(T):
                    for k in range(KD):
                        ins = mm(psL[0][:, j * D:(j + 1) * D], attT[par][:, k, j * P:j * P + P], woT[:, k, :],
                                 k == 0, k == KD - 1)
                ins.then_inc(out_ps, 1)

            def key_values(g, par):
                pe.wait_ge(f_sum, 8 * g + 4)
                pe.wait_ge(v_sb, g + 1)
                for m in range(PAIRS):
                    c0 = P * (m % 4)
                    for j in range(T):
                        ins = mm(psKV[:, m * PW:(m + 1) * PW], kf[par][:, j, m // 4, c0:c0 + P],
                                 va[par][:, j, 2 * m:2 * m + 2, :].rearrange("p h d -> p (h d)"), j == 0, j == T - 1)
                ins.then_inc(kv_ps, 1)

            def attend(g, par, j):
                if j == 0:
                    pe.wait_ge(f_sum, 8 * g + 8)
                    pe.wait_ge(kvbd_ready, g + 1)
                for m in range(PAIRS):
                    ins = mm(psAT[j][:, m * PW:(m + 1) * PW], qf[par][:, m, j * P:j * P + P],
                             kvbd[:, bass.ds(g, 1), m, :].rearrange("p o n -> p (o n)"))
                ins.then_inc(attn_ps, 1)

            def class_attend(part):
                for i in range(4):
                    m = 4 * part + i
                    mm(psCA[part][i][0:1, 0:B * PW].rearrange("p (b n) -> p b n", b=B), c_qf[:, m:m + 1],
                       kvbd[:, :, m, :]).then_inc(c_attn_ps, 1)

            tokens_T(0, 0)
            pe.wait_ge(c_done, 4)
            for m in range(PAIRS):
                ins = mm(psKV[:, m * PW:(m + 1) * PW], c_kf[0:1, m * P:m * P + P],
                         c_va[0:1, 2 * m:2 * m + 2, :].rearrange("p h d -> p (h d)"))
            ins.then_inc(c_ps, 1)
            pe.wait_ge(wT_sb, len(turned) + 1)
            qk(0, 0, 0)
            qk(0, 0, 1)
            tokens_T(1, 1)
            values(0, 0)
            pe.wait_ge(c_done, 5)

            def attention_step(g, par):
                peeled = isinstance(g, int)
                pe.wait_ge(k_sb, g + 1)
                features(g, par, 0)
                features(g, par, 1)
                if not peeled or g >= 1:
                    attend(g - 1, 1 - par, 1)
                if not peeled or g + 1 < B:
                    qk(g + 1, 1 - par, 0)
                features(g, par, 2)
                features(g, par, 3)
                if not peeled or g >= 1:
                    att_T(g - 1, 1 - par)
                if not peeled or g + 1 < B:
                    qk(g + 1, 1 - par, 1)
                features(g, par, 4)
                features(g, par, 5)
                if not peeled or g + 2 < B:
                    tokens_T(g + 2, par)
                if not peeled or g >= 1:
                    out_rows(g - 1, 1 - par)
                features(g, par, 6)
                features(g, par, 7)
                key_values(g, par)
                if not peeled or g + 1 < B:
                    values(g + 1, 1 - par)
                attend(g, par, 0)

            attention_step(0, 0)
            with pe.Fori(0, (B - 4) // 2) as it:
                attention_step(2 * it + 1, 1)
                attention_step(2 * it + 2, 0)
            for g in range(B - 3, B):
                attention_step(g, g % 2)
            pe.wait_ge(v_sb, B)
            attend(B - 1, 1, 1)
            class_attend(0)
            att_T(B - 1, 1)
            out_rows(B - 1, 1)
            pe.wait_ge(catt_ready, 4)
            class_attend(1)

            def class_out():
                pe.wait_ge(catt_moved, 16)
                pe.wait_ge(x1T_sb, 2)
                for k in range(KD):
                    ins = pe.transpose(psT[:, k * B:(k + 1) * B], cx[0:B, 2, k * P:k * P + P], ident[0:B, 0:B])
                ins.then_inc(cattT_ps, 1)
                pe.wait_ge(cattT_sb, 1)
                for k in range(KD):
                    ins = mm(psL[1][0:B, 0:D], c_attT[:, k, :], woT[:, k, :], k == 0, k == KD - 1)
                ins.then_inc(c_out_ps, 1)

            def x1_T(g, par):
                tail = isinstance(g, int) and g == B
                n, tiles = (B, 1) if tail else (P, T)
                pe.wait_ge(xh_ready, g + 1)
                after(pe, xmT_sb, g - 1)
                after(pe, x1T_sb, g)
                for j in range(tiles):
                    for k in range(KD):
                        ins = pe.transpose(psT[:, k * IMG + j * P:k * IMG + j * P + n],
                                           xh[par][0:n, j, k * P:k * P + P], ident[0:n, 0:n])
                ins.then_inc(x1T_ps, 1)

            def xm_T(g, par):
                tail = isinstance(g, int) and g == B
                n, tiles = (B, 1) if tail else (P, T)
                pe.wait_ge(xm_ready, g + 1)
                after(pe, x1T_sb, g + 2 if not isinstance(g, int) or g + 2 <= B else B + 1)
                for j in range(tiles):
                    for k in range(KD):
                        ins = pe.transpose(psT[:, k * IMG + j * P:k * IMG + j * P + n],
                                           (c_pay if tail else pay[par])[0:n, j, k * P:k * P + P], ident[0:n, 0:n])
                ins.then_inc(xmT_ps, 1)

            def hidden(first_use, w, src, n, between=None):
                for i in range(4):
                    if i == 2 and between:
                        between()
                    after(pe, m_sb, first_use + i - 1)
                    for m in range(2):
                        c0 = P * (2 * i + m)
                        for k in range(KD):
                            ins = mm(psF[i % 2][:, m * IMG:m * IMG + n], w[:, k, c0:c0 + P], src[:, k, 0:n],
                                     k == 0, k == KD - 1)
                    ins.then_inc(m_ps, 1)

            def mlp_out(g, par, j, first_use):
                tail = isinstance(g, int) and g == B
                n = B if tail else P
                if j == 0:
                    pe.wait_ge(m_sb, first_use + 4)
                    after(pe, h1_ready, g)
                for k in range(KH):
                    ins = mm(psO[j][0:n, 0:D], gT[:, k, j * P:j * P + n], w2T[:, k, :], k == 0, k == KH - 1)
                ins.then_inc(mlp_ps, 1)

            def router_out(g, par, first_use, j):
                tail = isinstance(g, int) and g == B
                n, tiles = (B, 1) if tail else (P, T)
                if j >= tiles:
                    return
                if j == 0:
                    pe.wait_ge(m_sb, first_use + 4)
                for k in range(KH):
                    ins = mm(psLG[0:n, j * E:(j + 1) * E], rT[:, k, j * P:j * P + n], rw2[:, k, :],
                             k == 0, k == KH - 1)
                if j == tiles - 1:
                    ins.then_inc(lg_ps, 1)

            def ranks(g):
                pe.wait_ge(mask_ready, g + 1)
                mm(psRK[:, 0:E], before, mask[:, 0, :])
                mm(psRK[:, E:2 * E], before, mask[:, 1, :], True, False)
                mm(psRK[:, E:2 * E], ones, mask[:, 0, :], False, True)
                mm(psRK[:, 2 * E:3 * E], ones, mask[:, 0, :], True, False)
                mm(psRK[:, 2 * E:3 * E], ones, mask[:, 1, :], False, True).then_inc(rk_ps, 1)

            x1_T(0, 0)

            def routing_step(g, par):
                peeled = isinstance(g, int)
                mlp_use = 8 * g - 4 if not peeled or g else 0

                def router_use(g):
                    return 8 * g if not isinstance(g, int) or g <= B else 8 * g - 4

                def logits(j):
                    if not peeled or g >= 2:
                        router_out(g - 2, par, router_use(g - 1), j)
                if not peeled or g <= B:
                    pe.wait_ge(x1T_sb, g + 1)
                    hidden(mlp_use, w1T, x1T[par], B if peeled and g == B else IMG, lambda: logits(0))
                else:
                    logits(0)
                if not peeled or 1 <= g <= B + 1:
                    xm_T(g - 1, 1 - par)
                logits(1)
                if not peeled or 1 <= g <= B + 1:
                    pe.wait_ge(xmT_sb, g)
                    hidden(router_use(g), rw1, xmT[1 - par], B if peeled and g - 1 == B else IMG)
                if not peeled or g + 1 <= B:
                    x1_T(g + 1, 1 - par)
                if peeled and g == 0:
                    class_out()
                if not peeled or g >= 2:
                    ranks(g - 2)
                if not peeled or g <= B:
                    for j in range(1 if peeled and g == B else T):
                        mlp_out(g, par, j, mlp_use)
            for g in range(3):
                routing_step(g, g % 2)
            with pe.Fori(0, 2) as it:
                routing_step(2 * it + 3, 1)
                routing_step(2 * it + 4, 0)
            routing_step(B - 1, 1)
            mlp_use, use, last_use = 8 * B - 4, 8 * B, 8 * B + 4
            pe.wait_ge(x1T_sb, B + 1)
            hidden(mlp_use, w1T, x1T[0], B)
            for j in range(T):
                router_out(B - 2, 0, 8 * (B - 1), j)
            mlp_out(B, 0, 0, mlp_use)
            xm_T(B - 1, 1)
            pe.wait_ge(xmT_sb, B)
            hidden(use, rw1, xmT[1], IMG)
            ranks(B - 2)
            xm_T(B, 0)
            for j in range(T):
                router_out(B - 1, 1, use, j)
            pe.wait_ge(xmT_sb, B + 1)
            hidden(last_use, rw1, xmT[0], B)
            ranks(B - 1)
            router_out(B, 0, last_use, 0)
            ranks(B)

            loaded = [xs_loaded0, xs_loaded1]
            pe.wait_ge(tables_ready, 1)

            def weights(e, c0, n):
                return experts[:, bass.ds(e, 1), c0:c0 + n].rearrange("p o n -> p (o n)")

            def rows_T(i, par, turns):
                pe.wait_ge(loaded[par], 16 * turns)
                after(pe, xsT_sb, i)
                for k in range(KD):
                    ins = pe.transpose(psT[:, k * P:(k + 1) * P], xs[par][:, k * P:k * P + P], ident)
                ins.then_inc(xsT_ps, 1)

            def up(i, par):
                pe.wait_ge(w1_ready, i + 1)
                pe.wait_ge(xsT_sb, i + 1)
                after(pe, hT_sb, KH * (i - 1))
                for c in range(2):
                    for m in range(4):
                        c0 = P * (4 * c + m)
                        for k in range(KD):
                            ins = mm(psUP[par][c][:, P * m:P * m + P], w1now[par][:, k, c0:c0 + P],
                                     xsT[par][:, k * P:k * P + P], k == 0, k == KD - 1)
                    ins.then_inc(h_ps, 1)

            def down(i, par):
                e = pe.value_load(owner_i[0:1, bass.ds(i, 1)], min_val=0, max_val=E - 1)
                wait_for_expert(pe, i)
                pe.wait_ge(hT_sb, KH * (i + 1))
                after(pe, y_ready, i - 1)
                for k in range(KH):
                    ins = mm(psAT[par][:, 0:D], hT[par][:, k, :], weights(e, KD * HID + k * D, D), k == 0, k == KH - 1)
                ins.then_inc(y_ps, 1)

            rows_T(0, 0, 1)
            rows_T(1, 1, 1)
            up(0, 0)

            def expert_step(i, par, turns):
                if not isinstance(i, int) or i + 1 < MOE_TILES:
                    up(i + 1, 1 - par)
                if not isinstance(i, int) or i + 2 < MOE_TILES:
                    rows_T(i + 2, par, turns + 1)
                down(i, par)
            expert_step(0, 0, 1)
            expert_step(1, 1, 1)
            with pe.Fori(0, MOE_TILES // 2 - 2) as it:
                expert_step(2 * it + 2, 0, it + 2)
                expert_step(2 * it + 3, 1, it + 2)
            expert_step(MOE_TILES - 2, 0, MOE_TILES // 2)
            expert_step(MOE_TILES - 1, 1, MOE_TILES // 2)


_INS = ["x", "cls_tok", "L0_tok_Wa", "L0_tok_ba", "L0_tok_Wd1", "L0_tok_bd1", "L0_tok_Wd2", "L0_tok_bd2",
        "L0_tok_Wd3", "L0_tok_bd3", "L0_attn_proj", "L0_attn_w_qkv", "L0_attn_w_out", "L0_attn_b_out",
        "L0_attn_gamma", "L0_attn_beta", "L0_attn_w1", "L0_attn_b1", "L0_attn_w2", "L0_attn_b2",
        "L0_ffn_rw1", "L0_ffn_rb1", "L0_ffn_rw2", "L0_ffn_rb2", "L0_ffn_w1", "L0_ffn_b1", "L0_ffn_w2", "L0_ffn_b2"]


def kernel(**inputs):
    import numpy as _np
    import concourse.bacc as _bacc
    from concourse import mybir as _mybir
    from concourse.bass_utils import run_bass_kernel_spmd as _run

    nc = _bacc.Bacc("TRN2", target_bir_lowering=False, num_devices=1)
    arrays, tensors = {}, {}
    for name in _INS:
        a = _np.ascontiguousarray(inputs[name])
        arrays[f"in_{name}"] = a
        tensors[name] = nc.dram_tensor(f"in_{name}", a.shape, _mybir.dt.from_np(a.dtype), kind="ExternalInput").ap()
    tensors["out"] = nc.dram_tensor("out_tokens", (B, SEQ, D), F32, kind="ExternalOutput").ap()
    build(nc, tensors)
    r = _run(nc, [arrays], core_ids=[0])
    return r.results[0]["out_tokens"]
```
